# Optimizing a Trainium2 kernel written in Bass

```python
import numpy as np
import jax
import jax.numpy as jnp

def _softmax(x, axis=-1):
    return jax.nn.softmax(x, axis=axis)

def _gelu(x):
    return jax.nn.gelu(x, approximate=True)

def _silu(x):
    return jax.nn.silu(x)

def _sigmoid(x):
    return jax.nn.sigmoid(x)

def _layernorm(x, axis=-1, eps=1e-05):
    m = jnp.mean(x, axis=axis, keepdims=True)
    v = jnp.var(x, axis=axis, keepdims=True)
    return (x - m) / jnp.sqrt(v + eps)

def _scatter_add(tgt, idx, src, axis=0):
    return tgt.at[idx].add(src)

def _segment_sum(src, seg, n):
    return jax.ops.segment_sum(src, seg, n)
kernel_name = 'mk_sandwich_d1_jaxref_r4_9440bf'

def setup_inputs(seed: int=0):
    np.random.seed(seed)
    _w = jnp.asarray

    def _L0_attn_setup():
        import jax, jax.numpy as jnp
        import numpy as np
        D_MODEL = 256
        NHEAD = 16
        HEAD_DIM = D_MODEL // NHEAD
        ROTARY_DIM = HEAD_DIM
        D_INNER = 2 * D_MODEL
        HEADDIM = 64
        H_SSM = D_INNER // HEADDIM
        D_STATE = 128
        D_CONV = 4
        CHUNK = 64
        CONV_DIM = D_INNER + 2 * D_STATE
        D_IN_PROJ = 2 * D_INNER + 2 * D_STATE + H_SSM
        EPS = 1e-05

        def rmsnorm(x, w):
            var = jnp.mean(x * x, axis=-1, keepdims=True)
            return x * jax.lax.rsqrt(var + EPS) * w

        def apply_rope(q):
            T = q.shape[1]
            half = ROTARY_DIM // 2
            inv_freq = 1.0 / 10000.0 ** (jnp.arange(0, ROTARY_DIM, 2, dtype=jnp.float32) / ROTARY_DIM)
            freqs = jnp.arange(T, dtype=jnp.float32)[:, None] * inv_freq[None, :]
            cos = jnp.cos(freqs)[None, :, None, :]
            sin = jnp.sin(freqs)[None, :, None, :]
            q1 = q[..., :half]
            q2 = q[..., half:ROTARY_DIM]
            rest = q[..., ROTARY_DIM:]
            return jnp.concatenate([q1 * cos - q2 * sin, q2 * cos + q1 * sin, rest], axis=-1)

        def segsum(x):
            T = x.shape[-1]
            xc = jnp.cumsum(x, axis=-1)
            ss = xc[..., :, None] - xc[..., None, :]
            mask = jnp.tril(jnp.ones((T, T), dtype=bool))
            return jnp.where(mask, ss, -jnp.inf)

        def ssd(x, dt, A, Bm, Cm):
            b, l, h, p = x.shape
            n = Bm.shape[-1]
            c = l // CHUNK
            xdt = (x * dt[..., None]).reshape(b, c, CHUNK, h, p)
            Adt = (dt * A).reshape(b, c, CHUNK, h).transpose(0, 3, 1, 2)
            Br = Bm.reshape(b, c, CHUNK, n)
            Cr = Cm.reshape(b, c, CHUNK, n)
            Acs = jnp.cumsum(Adt, axis=-1)
            Lmat = jnp.exp(segsum(Adt))
            Y_diag = jnp.einsum('bcln,bcsn,bhcls,bcshp->bclhp', Cr, Br, Lmat, xdt)
            decay_states = jnp.exp(Acs[..., -1:] - Acs)
            states = jnp.einsum('bcln,bhcl,bclhp->bchpn', Br, decay_states, xdt)
            A_chunk = jnp.pad(Acs[..., -1], ((0, 0), (0, 0), (1, 0)))
            decay_chunk = jnp.exp(segsum(A_chunk))
            states = jnp.concatenate([jnp.zeros_like(states[:, :1]), states], axis=1)
            new_states = jnp.einsum('bhzc,bchpn->bzhpn', decay_chunk, states)
            states_prev = new_states[:, :-1]
            Y_off = jnp.einsum('bcln,bchpn,bhcl->bclhp', Cr, states_prev, jnp.exp(Acs))
            return (Y_diag + Y_off).reshape(b, l, h, p)
        key = jax.random.key(seed)
        ks = jax.random.split(key, 8)
        B, T = (2, 512)
        return {'x': jax.random.normal(ks[0], (B, T, D_MODEL), dtype=jnp.float32), 'W_in': jax.random.normal(ks[1], (3 * D_MODEL, D_MODEL), dtype=jnp.float32) * 0.02, 'W_zxbcdt': jax.random.normal(ks[2], (D_IN_PROJ, D_MODEL), dtype=jnp.float32) * 0.02, 'conv_w': jax.random.normal(ks[3], (CONV_DIM, D_CONV), dtype=jnp.float32) * 0.2, 'conv_b': jnp.zeros((CONV_DIM,), dtype=jnp.float32), 'dt_bias': jax.random.normal(ks[4], (H_SSM,), dtype=jnp.float32) * 0.5, 'A_log': jax.random.normal(ks[5], (H_SSM,), dtype=jnp.float32) * 0.5, 'D_param': jax.random.normal(ks[6], (H_SSM,), dtype=jnp.float32), 'norm_pre_w': jnp.ones((D_MODEL,), dtype=jnp.float32), 'norm_gated_w': jnp.ones((D_INNER,), dtype=jnp.float32), 'W_out': jax.random.normal(ks[7], (D_MODEL, D_INNER), dtype=jnp.float32) * 0.02}
    _L0_attn_in = _L0_attn_setup()

    def _L0_ffn_setup():
        import jax, jax.numpy as jnp
        import numpy as np
        E = 16
        G = 4
        EPG = E // G
        K = 4
        TOPK_GROUP = 2
        PER_GROUP_K = K // TOPK_GROUP

        def _route(xf, router_w, correction_bias):
            S = xf.shape[0]
            logits = xf @ router_w.T
            scores = jax.nn.sigmoid(logits)
            sb = scores + correction_bias
            grp_top = jax.lax.top_k(sb.reshape(S, G, EPG), PER_GROUP_K)[0]
            group_scores = grp_top.sum(axis=-1)
            _, group_idx = jax.lax.top_k(group_scores, TOPK_GROUP)
            group_mask = jnp.zeros((S, G), sb.dtype).at[jnp.arange(S)[:, None], group_idx].set(1.0)
            score_mask = jnp.broadcast_to(group_mask[:, :, None], (S, G, EPG)).reshape(S, E)
            masked = jnp.where(score_mask > 0, sb, -jnp.inf)
            _, topk_idx = jax.lax.top_k(masked, K)
            w = jnp.take_along_axis(scores, topk_idx, axis=1)
            w = w / (w.sum(axis=-1, keepdims=True) + 1e-20)
            return (topk_idx, w, scores)
        key = jax.random.key(seed)
        ks = jax.random.split(key, 9)
        B, T, C, H, HS = (2, 256, 256, 64, 512)
        std = 0.02
        return {'x': jax.random.normal(ks[0], (B, T, C), jnp.float32), 'router_w': jax.random.normal(ks[1], (E, C), jnp.float32) * std, 'correction_bias': jnp.zeros((E,), jnp.float32), 'gate_w': jax.random.normal(ks[2], (E, C, H), jnp.float32) * std, 'up_w': jax.random.normal(ks[3], (E, C, H), jnp.float32) * std, 'down_w': jax.random.normal(ks[4], (E, H, C), jnp.float32) * std, 'shared_gate_w': jax.random.normal(ks[5], (HS, C), jnp.float32) * std, 'shared_up_w': jax.random.normal(ks[6], (HS, C), jnp.float32) * std, 'shared_down_w': jax.random.normal(ks[7], (C, HS), jnp.float32) * std}
    _L0_ffn_in = _L0_ffn_setup()
    _d = {'L0_attn_x': _L0_attn_in['x'], 'L0_attn_W_in': _L0_attn_in['W_in'], 'L0_attn_W_zxbcdt': _L0_attn_in['W_zxbcdt'], 'L0_attn_conv_w': _L0_attn_in['conv_w'], 'L0_attn_conv_b': _L0_attn_in['conv_b'], 'L0_attn_dt_bias': _L0_attn_in['dt_bias'], 'L0_attn_A_log': _L0_attn_in['A_log'], 'L0_attn_D_param': _L0_attn_in['D_param'], 'L0_attn_norm_pre_w': _L0_attn_in['norm_pre_w'], 'L0_attn_norm_gated_w': _L0_attn_in['norm_gated_w'], 'L0_attn_W_out': _L0_attn_in['W_out'], 'L0_ffn_router_w': _L0_ffn_in['router_w'], 'L0_ffn_correction_bias': _L0_ffn_in['correction_bias'], 'L0_ffn_gate_w': _L0_ffn_in['gate_w'], 'L0_ffn_up_w': _L0_ffn_in['up_w'], 'L0_ffn_down_w': _L0_ffn_in['down_w'], 'L0_ffn_shared_gate_w': _L0_ffn_in['shared_gate_w'], 'L0_ffn_shared_up_w': _L0_ffn_in['shared_up_w'], 'L0_ffn_shared_down_w': _L0_ffn_in['shared_down_w']}
    _x0 = _d['L0_attn_x']
    _d['L0_attn_x'] = jax.random.normal(jax.random.fold_in(jax.random.key(seed), 1), (32, 512, 256), dtype=_x0.dtype)
    del _x0
    return _d

def reference(L0_attn_x, L0_attn_W_in, L0_attn_W_zxbcdt, L0_attn_conv_w, L0_attn_conv_b, L0_attn_dt_bias, L0_attn_A_log, L0_attn_D_param, L0_attn_norm_pre_w, L0_attn_norm_gated_w, L0_attn_W_out, L0_ffn_router_w, L0_ffn_correction_bias, L0_ffn_gate_w, L0_ffn_up_w, L0_ffn_down_w, L0_ffn_shared_gate_w, L0_ffn_shared_up_w, L0_ffn_shared_down_w):

    def _L0_attn_ref(x, W_in, W_zxbcdt, conv_w, conv_b, dt_bias, A_log, D_param, norm_pre_w, norm_gated_w, W_out):
        import jax, jax.numpy as jnp
        import numpy as np
        D_MODEL = 256
        NHEAD = 16
        HEAD_DIM = D_MODEL // NHEAD
        ROTARY_DIM = HEAD_DIM
        D_INNER = 2 * D_MODEL
        HEADDIM = 64
        H_SSM = D_INNER // HEADDIM
        D_STATE = 128
        D_CONV = 4
        CHUNK = 64
        CONV_DIM = D_INNER + 2 * D_STATE
        D_IN_PROJ = 2 * D_INNER + 2 * D_STATE + H_SSM
        EPS = 1e-05

        def rmsnorm(x, w):
            var = jnp.mean(x * x, axis=-1, keepdims=True)
            return x * jax.lax.rsqrt(var + EPS) * w

        def apply_rope(q):
            T = q.shape[1]
            half = ROTARY_DIM // 2
            inv_freq = 1.0 / 10000.0 ** (jnp.arange(0, ROTARY_DIM, 2, dtype=jnp.float32) / ROTARY_DIM)
            freqs = jnp.arange(T, dtype=jnp.float32)[:, None] * inv_freq[None, :]
            cos = jnp.cos(freqs)[None, :, None, :]
            sin = jnp.sin(freqs)[None, :, None, :]
            q1 = q[..., :half]
            q2 = q[..., half:ROTARY_DIM]
            rest = q[..., ROTARY_DIM:]
            return jnp.concatenate([q1 * cos - q2 * sin, q2 * cos + q1 * sin, rest], axis=-1)

        def segsum(x):
            T = x.shape[-1]
            xc = jnp.cumsum(x, axis=-1)
            ss = xc[..., :, None] - xc[..., None, :]
            mask = jnp.tril(jnp.ones((T, T), dtype=bool))
            return jnp.where(mask, ss, -jnp.inf)

        def ssd(x, dt, A, Bm, Cm):
            b, l, h, p = x.shape
            n = Bm.shape[-1]
            c = l // CHUNK
            xdt = (x * dt[..., None]).reshape(b, c, CHUNK, h, p)
            Adt = (dt * A).reshape(b, c, CHUNK, h).transpose(0, 3, 1, 2)
            Br = Bm.reshape(b, c, CHUNK, n)
            Cr = Cm.reshape(b, c, CHUNK, n)
            Acs = jnp.cumsum(Adt, axis=-1)
            Lmat = jnp.exp(segsum(Adt))
            Y_diag = jnp.einsum('bcln,bcsn,bhcls,bcshp->bclhp', Cr, Br, Lmat, xdt)
            decay_states = jnp.exp(Acs[..., -1:] - Acs)
            states = jnp.einsum('bcln,bhcl,bclhp->bchpn', Br, decay_states, xdt)
            A_chunk = jnp.pad(Acs[..., -1], ((0, 0), (0, 0), (1, 0)))
            decay_chunk = jnp.exp(segsum(A_chunk))
            states = jnp.concatenate([jnp.zeros_like(states[:, :1]), states], axis=1)
            new_states = jnp.einsum('bhzc,bchpn->bzhpn', decay_chunk, states)
            states_prev = new_states[:, :-1]
            Y_off = jnp.einsum('bcln,bchpn,bhcl->bclhp', Cr, states_prev, jnp.exp(Acs))
            return (Y_diag + Y_off).reshape(b, l, h, p)
        N, T, _ = x.shape
        qkv = (x @ W_in.T).reshape(N, T, 3, NHEAD, HEAD_DIM)
        q = apply_rope(qkv[:, :, 0]).reshape(N, T, D_MODEL)
        residual = q
        h = rmsnorm(q, norm_pre_w)
        zxbcdt = h @ W_zxbcdt.T
        z = zxbcdt[..., :D_INNER]
        xBC = zxbcdt[..., D_INNER:D_INNER + CONV_DIM]
        dt = jax.nn.softplus(zxbcdt[..., -H_SSM:] + dt_bias)
        xp = jnp.pad(xBC, ((0, 0), (D_CONV - 1, 0), (0, 0)))
        conv_out = conv_b
        for k in range(D_CONV):
            conv_out = conv_out + xp[:, k:k + T, :] * conv_w[:, k]
        xBC = jax.nn.silu(conv_out)
        x_ssm = xBC[..., :D_INNER].reshape(N, T, H_SSM, HEADDIM)
        Bm = xBC[..., D_INNER:D_INNER + D_STATE]
        Cm = xBC[..., D_INNER + D_STATE:]
        A = -jnp.exp(A_log)
        y = ssd(x_ssm, dt, A, Bm, Cm) + D_param[None, None, :, None] * x_ssm
        y = y.reshape(N, T, D_INNER)
        y = rmsnorm(y * jax.nn.silu(z), norm_gated_w)
        out = y @ W_out.T
        return out + residual

    def _L0_ffn_ref(x, router_w, correction_bias, gate_w, up_w, down_w, shared_gate_w, shared_up_w, shared_down_w):
        import jax, jax.numpy as jnp
        import numpy as np
        E = 16
        G = 4
        EPG = E // G
        K = 4
        TOPK_GROUP = 2
        PER_GROUP_K = K // TOPK_GROUP

        def _route(xf, router_w, correction_bias):
            S = xf.shape[0]
            logits = xf @ router_w.T
            scores = jax.nn.sigmoid(logits)
            sb = scores + correction_bias
            grp_top = jax.lax.top_k(sb.reshape(S, G, EPG), PER_GROUP_K)[0]
            group_scores = grp_top.sum(axis=-1)
            _, group_idx = jax.lax.top_k(group_scores, TOPK_GROUP)
            group_mask = jnp.zeros((S, G), sb.dtype).at[jnp.arange(S)[:, None], group_idx].set(1.0)
            score_mask = jnp.broadcast_to(group_mask[:, :, None], (S, G, EPG)).reshape(S, E)
            masked = jnp.where(score_mask > 0, sb, -jnp.inf)
            _, topk_idx = jax.lax.top_k(masked, K)
            w = jnp.take_along_axis(scores, topk_idx, axis=1)
            w = w / (w.sum(axis=-1, keepdims=True) + 1e-20)
            return (topk_idx, w, scores)
        B, T, C = x.shape
        S = B * T
        xf = x.reshape(S, C)
        sg = xf @ shared_gate_w.T
        su = xf @ shared_up_w.T
        shared_out = jax.nn.silu(sg) * su @ shared_down_w.T
        topk_idx, w, _scores = _route(xf, router_w, correction_bias)
        combine = jnp.zeros((S, E), xf.dtype).at[jnp.arange(S)[:, None], topk_idx].add(w)
        g = jnp.einsum('sc,ech->esh', xf, gate_w)
        u = jnp.einsum('sc,ech->esh', xf, up_w)
        h = jax.nn.silu(g) * u
        hw = h * combine.T[:, :, None]
        routed = jnp.einsum('esh,ehc->sc', hw, down_w)
        return (shared_out + routed).reshape(B, T, C)
    x = L0_attn_x
    x = x + _layernorm(_L0_attn_ref(_layernorm(x, axis=-1), L0_attn_W_in, L0_attn_W_zxbcdt, L0_attn_conv_w, L0_attn_conv_b, L0_attn_dt_bias, L0_attn_A_log, L0_attn_D_param, L0_attn_norm_pre_w, L0_attn_norm_gated_w, L0_attn_W_out), axis=-1)
    x = x + _layernorm(_L0_ffn_ref(_layernorm(x, axis=-1), L0_ffn_router_w, L0_ffn_correction_bias, L0_ffn_gate_w, L0_ffn_up_w, L0_ffn_down_w, L0_ffn_shared_gate_w, L0_ffn_shared_up_w, L0_ffn_shared_down_w), axis=-1)
    return x

_drawn_inputs = setup_inputs


def setup_inputs(seed=0):
    import zlib

    import numpy as np

    out = dict(_drawn_inputs(seed))
    spreads = {'L0_attn_conv_b': (0.0, 0.1),
     'L0_attn_norm_pre_w': (1.0, 0.2),
     'L0_attn_norm_gated_w': (1.0, 0.2),
     'L0_ffn_correction_bias': (0.0, 0.1)}
    factors = {'L0_attn_A_log': 2.895}
    for name, (base, spread) in spreads.items():
        noise = np.random.default_rng([zlib.crc32(name.encode()), seed]).standard_normal(out[name].shape)
        drawn = base * np.exp(spread * noise) if base else spread * noise
        out[name] = jnp.asarray(drawn.astype(out[name].dtype))
    for name, factor in factors.items():
        out[name] = (out[name] * factor).astype(out[name].dtype)
    return out
```

```python
import concourse.bass as bass
from concourse import mybir
from contextlib import ExitStack

SEQS, T, D = 32, 512, 256
HEADS, HALF = 16, 8
DI, HS, PD, NS = 512, 8, 64, 128
CONV, TAPS = DI + 2 * NS, 4
DT0 = 2 * DI + 2 * NS
E, EH, SH = 16, 64, 512
GROUPS, TOPK, TOPG = 4, 4, 2
P = 128
NT = T // P
KD = D // P
NB = DI // P
CB_ = CONV // P
HB = (SH + E * EH) // P
SB = SH // P
EPS = 1e-5
NEVER = -3e38


def build(nc, x, wq_t, wzx_t, conv_w, conv_b, dt_bias, a_log, d_param, npw, ngw, wo_t,
          router_t, cbias, wg_t, wu_t, wd, swg_t, swu_t, swd_t,
          c_ident, c_upper, c_cos, c_sin, c_reset, c_tri, out):
    fp32, f32r = mybir.dt.float32, mybir.dt.float32r
    ALU, ACT, AX = mybir.AluOpType, mybir.ActivationFunctionType, mybir.AxisListType

    ctx = ExitStack()
    with ctx:
        def sb(name, shape, dt=fp32):
            return ctx.enter_context(nc.sbuf_tensor(name, shape, dt))

        WQ = sb("WQ", [P, KD, D])
        ZH, ZL = sb("ZH", [P, KD, DT0], f32r), sb("ZL", [P, KD, DT0], f32r)
        DTH, DTL = sb("DTH", [P, KD, HS], f32r), sb("DTL", [P, KD, HS], f32r)
        RH, RL = sb("RH", [P, KD, E], f32r), sb("RL", [P, KD, E], f32r)
        WO = sb("WO", [P, NB, D])
        GH, GL = sb("GH", [P, KD, HB * P], f32r), sb("GL", [P, KD, HB * P], f32r)
        UH, UL = sb("UH", [P, KD, HB * P], f32r), sb("UL", [P, KD, HB * P], f32r)
        WD = sb("WD", [P, HB, D])
        ident, upper, ones = sb("ident", [P, P]), sb("upper", [P, P]), sb("ones", [P, P])
        cos_t, sin_t = sb("cos_t", [P, NT, HALF]), sb("sin_t", [P, NT, 2, HALF])
        reset, tri = sb("reset", [P, NT * E]), sb("tri", [P, GROUPS, GROUPS])
        cw, cbv = sb("cw", [P, CB_, TAPS]), sb("cbv", [P, CB_])
        dtb, aneg, dcol = sb("dtb", [P, HS]), sb("aneg", [P, HS]), sb("dcol", [P, NB])
        ebias, npwc, ngwc = sb("ebias", [P, E]), sb("npwc", [P, KD]), sb("ngwc", [P, NB])
        mhalf, one1 = sb("mhalf", [P, NT]), sb("one1", [P, 1])
        xs = sb("xs", [P, NT, D])
        xn = sb("xn", [P, NT, D])
        xT = sb("xT", [P, KD, T])
        qrot, tmp = sb("qrot", [P, NT, D]), sb("tmp", [P, NT, D])
        hTh, hTl = sb("hTh", [P, KD, T], f32r), sb("hTl", [P, KD, T], f32r)
        xc = sb("xc", [P, CB_, T])
        zs = sb("zs", [P, NB, T])
        Btok = sb("Btok", [P, NT, NS])
        xdt = sb("xdt", [P, NT, DI])
        xdec = sb("xdec", [P, 2, DI])
        seg = sb("seg", [P, NT, HS, P])
        S = sb("S", [P, DI])
        CBm = sb("CBm", [P, NT, P])
        acsT = sb("acsT", [NT * HS, P])
        st6 = sb("st6", [P, NT, 6])
        mv = sb("mv", [P, NT, 2])
        ve, rstd = sb("ve", [P, NT]), sb("rstd", [P, NT])
        dr, na, e1, l1 = (sb(n, [P, NT, HS]) for n in ("dr", "na", "e1", "l1"))
        dt, ad = sb("dt", [P, NT, HS]), sb("ad", [P, NT, HS])
        acs = sb("acs", [P, 2, NT * HS])
        ea, ed, el = (sb(n, [P, NT, HS]) for n in ("ea", "ed", "el"))
        x1 = sb("x1", [P, NT, D])
        fTh, fTl = sb("fTh", [P, KD, T], f32r), sb("fTl", [P, KD, T], f32r)
        hid = sb("hid", [P, 3, T])
        cb = sb("cb", [P, 2, T])
        fo = sb("fo", [P, NT, D])
        cT = sb("cT", [E, T])
        fst6, fmv = sb("fst6", [P, NT, 6]), sb("fmv", [P, NT, 2])
        fve, frstd = sb("fve", [P, NT]), sb("frstd", [P, NT])
        th, sc, sbs, msk = (sb(n, [P, NT * E]) for n in ("th", "sc", "sbs", "msk"))
        gt, eq, pre = (sb(n, [P, NT * E]) for n in ("gt", "eq", "pre"))
        hi2, lo2 = sb("hi2", [P, NT * GROUPS, 2]), sb("lo2", [P, NT * GROUPS, 2])
        m1, mn, gs, rk = (sb(n, [P, NT * GROUPS]) for n in ("m1", "mn", "gs", "rk"))
        v8, ws = sb("v8", [P, NT, 8]), sb("ws", [P, NT])

        acs_row = nc.dram_tensor("acs_row", (NT * HS, P), fp32, kind="Internal").ap()
        c_row = nc.dram_tensor("c_row", (E, T), fp32, kind="Internal").ap()

        def rows(ap, dims, offset=0):
            return bass.AP(tensor=ap.tensor, offset=ap.offset + offset, ap=dims)

        apb = [ctx.enter_context(nc.psum_tensor(f"apb{n}", [P, T], fp32)) for n in range(3)]
        fpb = [ctx.enter_context(nc.psum_tensor(f"fpb{n}", [P, T], fp32)) for n in range(3)]
        acc = [ctx.enter_context(nc.psum_tensor(f"acc{n}", [P, T], fp32)) for n in range(2)]

        A_SLOTS = [("xT0", "ACT", "ACT"), ("xT1", "ACT", "ACT"), ("q0", "DVE", "ACT"), ("q1", "DVE", "ACT"),
                   ("hT0", "ACT", "DVE"), ("hT1", "ACT", "DVE"), ("dt", "DVE", "DVE"),
                   ("xc4", "ACT", "ACT"), ("xc5", "ACT", "ACT"), ("xc0", "ACT", "ACT"), ("acs", "DVE", "DVE"),
                   ("xc1", "ACT", "ACT"), ("xc2", "ACT", "ACT"), ("xc3", "ACT", "ACT"),
                   ("z0", "ACT", "ACT"), ("z1", "ACT", "ACT"), ("z2", "ACT", "ACT"), ("z3", "ACT", "ACT"),
                   ("Bt", "ACT", "ACT"), ("CB", "DVE", "DVE")]
        for c in range(NT):
            A_SLOTS += [(f"xt{c}", "DVE", "DVE")]
            A_SLOTS += [(f"yo{c}", "DVE", "DVE")] * (c > 0)
            A_SLOTS += [(f"st{c}", "DVE", "DVE")] * (c < NT - 1)
            A_SLOTS += [(f"yd{c}", "DVE", "DVE")]
        A_SLOTS += [(f"yT{j}", "DVE", "ACT") for j in range(NB)]
        A_SLOTS += [("ssq", "DVE", "DVE"), ("out0", "DVE", "DVE"), ("out1", "DVE", "DVE"),
                    ("fT0", "ACT", "DVE"), ("fT1", "ACT", "DVE")]
        F_SLOTS = [("logits", "ACT", "DVE")]
        for j in range(HB):
            F_SLOTS += [(f"G{j}", "ACT", "with U"), (f"U{j}", "DVE", "DVE" if j < SB else "POOL")]
            F_SLOTS += [("cT", "ACT", "SP")] * (j == SB - 1)
        SLOTS, BANKS = {"a": A_SLOTS, "f": F_SLOTS}, {"a": apb, "f": fpb}
        WHERE = {s[0]: (part, n) for part in SLOTS for n, s in enumerate(SLOTS[part])}

        def count(part, field, engine, upto=None):
            slots = SLOTS[part]
            return sum(s[field] == engine for s in slots[:len(slots) if upto is None else upto + 1])

        def bank(name):
            part, n = WHERE[name]
            return BANKS[part][n % 3]

        NR = HB - SB
        SEM = {
            "x_free": ("SP", "a", 1, True), "acsT_ready": ("SP", "a", 1, False),
            "seg_free": ("SP", "a", 1, True), "acs_stored": ("SP", "a", 16, False),
            "cT_ready": ("SP", "f", 1, False), "c_stored": ("SP", "f", 16, False),
            "cb_free": ("SP", "f", NR, True), "fo_ready": ("SP", "f", 1, False),
            "stored": ("SP", "f", 16, True),
            "x_loaded": ("DVE", "a", 16, False), "rstd_ready": ("DVE", "a", 5, False),
            "ssq_ready": ("DVE", "a", 1, False), "hi_ready": ("DVE", "a", 4, False),
            "conv_first": ("DVE", "a", CB_, False), "ln_ready": ("DVE", "a", 1, False),
            "seg_loaded": ("DVE", "a", 16, False), "exp_ready": ("DVE", "a", NT, False),
            "decay_ready": ("DVE", "a", 1, False), "tmp_free": ("DVE", "a", 1, True),
            "a_for_DVE": ("DVE", "a", count("a", 1, "DVE"), False),
            "f_for_DVE": ("DVE", "f", count("f", 1, "DVE"), False),
            "silu_ready": ("DVE", "f", HB, False), "tanh_ready": ("DVE", "f", 1, False),
            "frstd_ready": ("DVE", "f", 1, False), "acc_ready": ("DVE", "f", 1, False),
            "fo_free": ("DVE", "f", 1, False),
            "a_for_ACT": ("ACT", "a", count("a", 1, "ACT"), False),
            "qrot_ready": ("ACT", "a", 2, False), "na_ready": ("ACT", "a", 1, False),
            "conv_ready": ("ACT", "a", CB_, False), "acs_ready": ("ACT", "a", 1, False),
            "seg_ready": ("ACT", "a", NT, False), "yg_ready": ("ACT", "a", NB, False),
            "f_for_ACT": ("ACT", "f", count("f", 1, "ACT"), False),
            "down_done": ("ACT", "f", HB, True), "x1_ready": ("ACT", "f", 1, False),
            "x1_free": ("ACT", "f", 1, True),
            "var_ready": ("POOL", "a", 5, False), "rope_ready": ("POOL", "a", 2, False),
            "xdt_ready": ("POOL", "a", NT - 1, False), "v_ready": ("POOL", "a", NB, False),
            "fvar_ready": ("POOL", "f", 1, False), "h_half": ("POOL", "f", NR, False),
            "cb_loaded0": ("POOL", "f", 16 * NR // 2, False),
            "cb_loaded1": ("POOL", "f", 16 * NR // 2, False),
            "fo_half": ("POOL", "f", 1, False),
            "a_out_ACT": ("PE", "a", count("a", 2, "ACT"), True),
            "a_out_DVE": ("PE", "a", count("a", 2, "DVE"), True),
            "xn_ready": ("PE", "a", 3, False), "ad_ready": ("PE", "a", 1, False),
            "m_ready": ("PE", "a", NT, False), "xdec_ready": ("PE", "a", NT - 1, False),
            "f_out_SP": ("PE", "f", count("f", 2, "SP"), True),
            "f_out_DVE": ("PE", "f", count("f", 2, "DVE"), True),
            "f_out_POOL": ("PE", "f", count("f", 2, "POOL"), True),
            "c_ready": ("PE", "f", 1, False), "acc_free": ("PE", "f", 1, True),
        }
        sem = {n: ctx.enter_context(nc.semaphore(n)) for n in SEM}
        w_loaded = [ctx.enter_context(nc.semaphore(f"w_loaded{n}")) for n in range(8)]
        s_const = ctx.enter_context(nc.semaphore("consts_loaded"))
        s_scaled = ctx.enter_context(nc.semaphore("w_scaled"))
        s_high = ctx.enter_context(nc.semaphore("w_high"))
        s_low = ctx.enter_context(nc.semaphore("w_low"))
        s_fill = ctx.enter_context(nc.semaphore("consts_filled"))
        s_own = {n: ctx.enter_context(nc.semaphore(f"{n}_own")) for n in ("dve", "act")}
        NCONST = 19 * 16

        def give(eng, who):
            for n, (waiter, _, k, first) in SEM.items():
                if waiter == who and first:
                    eng.sem_inc(sem[n], k)

        def settle(eng, who, part):
            for n, (waiter, p_, k, _) in SEM.items():
                if waiter == who and p_ == part:
                    eng.sem_inc(sem[n], -k)

        def now(name, n=1):
            return SEM[name][2] + n

        def filled(eng, who, name):
            part, n = WHERE[name]
            eng.wait_ge(sem[f"{part}_for_{who}"], count(part, 1, who, n))

        class Own:

            def __init__(self, eng, name):
                self.eng, self.sem, self.n = eng, s_own[name], 0

            def mark(self, ins):
                self.n += 1
                ins.then_inc(self.sem, 1)

            def wait(self):
                if self.n:
                    self.eng.wait_ge(self.sem, self.n)

            def do(self, ins):
                self.mark(ins)
                self.wait()

            def settle(self):
                if self.n:
                    self.wait()
                    self.eng.sem_inc(self.sem, -self.n)
                self.n = 0

        stage = seg[:].rearrange("p a b c -> p (a b c)").rearrange("p (a n) -> p a n", a=2)
        STAGED = []
        for k in range(KD):
            STAGED.append(("z", k, DT0 + HS))
        for k in range(KD):
            STAGED.append(("r", k, E))
        for kind in ("g", "u"):
            for k in range(KD):
                STAGED.append((kind, k, HB * P))

        def split_pieces(n):
            kind, k, w = STAGED[n]
            src = stage[:, n % 2, :]
            if kind == "z":
                return [(src[:, 0:DT0], ZH[:, k, :], ZL[:, k, :]),
                        (src[:, DT0:DT0 + HS], DTH[:, k, :], DTL[:, k, :])]
            hi, lo = {"r": (RH, RL), "g": (GH, GL), "u": (UH, UL)}[kind]
            return [(src[:, 0:w], hi[:, k, :], lo[:, k, :])]

        block = ctx.enter_context(nc.Block())

        @block.sync
        def _(sp):
            for dst, src in ((ident[:], c_ident), (upper[:], c_upper),
                             (cos_t[:], c_cos.rearrange("(t p) f -> p t f", p=P)),
                             (sin_t[:], c_sin.rearrange("(t p) (a f) -> p t a f", p=P, a=2)),
                             (reset[:], rows(c_reset, [[0, P], [1, NT * E]])),
                             (tri[:], rows(c_tri, [[0, P], [GROUPS, GROUPS], [1, GROUPS]])),
                             (cw[:], conv_w.rearrange("(b p) k -> p b k", p=P)),
                             (cbv[:], conv_b.rearrange("(b p) -> p b", p=P)),
                             (dtb[:], rows(dt_bias, [[0, P], [1, HS]])),
                             (aneg[:], rows(a_log, [[0, P], [1, HS]])),
                             (dcol[0:PD, :], rows(d_param, [[0, PD], [2, NB]])),
                             (dcol[PD:P, :], rows(d_param, [[0, PD], [2, NB]], 1)),
                             (ebias[:], rows(cbias, [[0, P], [1, E]])),
                             (npwc[:], npw.rearrange("(k p) -> p k", p=P)),
                             (ngwc[:], ngw.rearrange("(k p) -> p k", p=P)),
                             (WQ[:], wq_t.rearrange("(k p) n -> p k n", p=P)),
                             (WO[:], wo_t.rearrange("(k p) n -> p k n", p=P)),
                             (WD[:, 0:SB, :], swd_t.rearrange("(k p) n -> p k n", p=P)),
                             (WD[:, SB:HB, :], wd.rearrange("(k p) n -> p k n", p=P))):
                with nc.allow_non_contiguous_dma(reason="small columns of weights, once"):
                    sp.dma_start(dst, src).then_inc(s_const, 16)
            for n, (kind, k, w) in enumerate(STAGED):
                if n >= 2:
                    sp.wait_ge(s_low, n - 1)
                dst, sl = stage[:, n % 2, :], slice(k * P, (k + 1) * P)
                if kind in "gu":
                    shared, routed = {"g": (swg_t, wg_t), "u": (swu_t, wu_t)}[kind]
                    sp.dma_start(dst[:, 0:SH], shared[sl, :]).then_inc(w_loaded[n], 16)
                    sp.dma_start(dst[:, SH:w], routed[sl, :]).then_inc(w_loaded[n], 16)
                else:
                    src = {"z": wzx_t, "r": router_t}[kind]
                    sp.dma_start(dst[:, 0:w], src[sl, :]).then_inc(w_loaded[n], 16)
            sp.wait_ge(s_low, len(STAGED))
            give(sp, "SP")

            def load_x(i):
                sp.wait_ge(sem["x_free"], 1)
                sp.dma_start(xs[:], x[i].rearrange("(t p) d -> p t d", p=P)).then_inc(sem["x_loaded"], 16)

            def decay_rows():
                sp.wait_ge(sem["acsT_ready"], 1)
                sp.dma_start(acs_row, acsT[:]).then_inc(sem["acs_stored"], 16)
                sp.wait_ge(sem["acs_stored"], 16)
                sp.wait_ge(sem["seg_free"], 1)
                sp.dma_start(seg[:].rearrange("p a b c -> p (a b c)"),
                             rows(acs_row, [[0, P], [1, NT * HS * P]])).then_inc(sem["seg_loaded"], 16)

            def combine_rows():
                sp.wait_ge(sem["cT_ready"], 1)
                sp.sem_inc(sem["f_out_SP"], 1)
                sp.dma_start(c_row, cT[:]).then_inc(sem["c_stored"], 16)
                sp.wait_ge(sem["c_stored"], 16)

            def combine_block(r):
                sp.wait_ge(sem["cb_free"], now("cb_free", r - 1) if r >= 2 else NR - 1 + r)
                sp.dma_start(cb[:, r % 2, :], rows(c_row, [[T, 2], [0, EH], [1, T]], 2 * r * T)
                             ).then_inc(sem[f"cb_loaded{r % 2}"], 16)

            def store(i):
                sp.wait_ge(sem["fo_ready"], 1)
                sp.sem_inc(sem["x1_free"], 1)
                sp.dma_start(out[i].rearrange("(t p) d -> p t d", p=P), fo[:]).then_inc(sem["stored"], 16)

            def iteration(i, attn, ffn):
                if attn:
                    load_x(i)
                if ffn:
                    sp.wait_ge(sem["stored"], 16)
                    sp.sem_inc(sem["fo_free"], 1)
                    combine_rows()
                    for r in range(4):
                        combine_block(r)
                if attn:
                    decay_rows()
                if ffn:
                    for r in range(4, NR):
                        combine_block(r)
                    store(i - 1)
                for part, on in (("a", attn), ("f", ffn)):
                    if on:
                        settle(sp, "SP", part)

            iteration(0, True, False)
            with sp.Fori(1, SEQS) as i:
                iteration(i, True, True)
            iteration(SEQS, False, True)
            sp.wait_ge(sem["stored"], 16)

        @block.gpsimd
        def _(pool):
            nc.gpsimd.memset(mhalf[:], -0.5).then_inc(s_fill, 1)
            nc.gpsimd.memset(ones[:], 1.0).then_inc(s_fill, 1)
            nc.gpsimd.memset(one1[:], 1.0).then_inc(s_fill, 1)
            give(pool, "POOL")
            pool.wait_ge(s_fill, 3)

            def root(n):
                pool.wait_ge(sem["var_ready"], n)
                nc.gpsimd.tensor_tensor(rstd[:], ve[:], mhalf[:], ALU.pow).then_inc(sem["rstd_ready"], 1)

            def rope_sum(s):
                pool.wait_ge(sem["rope_ready"], s + 1)
                sl = slice(2 * s, 2 * s + 2)
                nc.gpsimd.tensor_tensor(qrot[:, sl, :], qrot[:, sl, :], tmp[:, sl, :], ALU.add
                                        ).then_inc(sem["qrot_ready"], 1)

            def decayed(c):
                pool.wait_ge(sem["xdt_ready"], c + 1)
                v = "p (h d) -> p h d"
                nc.gpsimd.tensor_tensor(
                    xdec[:, c % 2, :].rearrange(v, h=HS), xdt[:, c, :].rearrange(v, h=HS),
                    ed[:, c, :].unsqueeze(2).broadcast_to([P, HS, PD]), ALU.mult
                ).then_inc(sem["xdec_ready"], 1)

            def gated(j):
                pool.wait_ge(sem["v_ready"], j + 1)
                nc.gpsimd.tensor_tensor(zs[:, j, :], zs[:, j, :], xc[:, j, :], ALU.mult
                                        ).then_inc(sem["yg_ready"], 1)

            def combine(j):
                r = j - SB
                pool.wait_ge(sem["h_half"], r + 1)
                pool.wait_ge(sem[f"cb_loaded{r % 2}"], 16 * (r // 2 + 1))
                nc.gpsimd.tensor_tensor(hid[:, j % 3, :], hid[:, j % 3, :], cb[:, r % 2, :], ALU.mult
                                        ).then_inc(sem["f_out_POOL"], 1)

            def final():
                pool.wait_ge(sem["fvar_ready"], 1)
                nc.gpsimd.tensor_tensor(frstd[:], fve[:], mhalf[:], ALU.pow).then_inc(sem["frstd_ready"], 1)
                pool.wait_ge(sem["fo_half"], 1)
                nc.gpsimd.tensor_tensor(fo[:], fo[:], x1[:], ALU.add).then_inc(sem["fo_ready"], 1)

            def iteration(a, f):
                if a: root(1)
                if a: rope_sum(0); rope_sum(1); root(2)
                if f: combine(4); combine(5); combine(6)
                if f: combine(7)
                if a: decayed(0); decayed(1)
                if f: combine(8)
                if a: decayed(2)
                if f: combine(9)
                if a:
                    for j in range(NB):
                        gated(j)
                if a: root(3)
                if f: combine(10)
                if a: root(4)
                if f: combine(11)
                if a: root(5)
                if f: final()
                if a: settle(pool, "POOL", "a")
                if f: settle(pool, "POOL", "f")

            iteration(True, False)
            with pool.Fori(1, SEQS):
                iteration(True, True)
            iteration(False, True)

        @block.scalar
        def _(act):
            own = Own(act, "act")
            act.wait_ge(s_fill, 3)
            act.wait_ge(s_const, NCONST)
            own.do(nc.scalar.activation(aneg[:], aneg[:], ACT.Exp))
            for n, (kind, k, w) in enumerate(STAGED):
                if kind == "z":
                    act.wait_ge(s_scaled, k + 1)
                else:
                    act.wait_ge(w_loaded[n], 32 if kind in "gu" else 16)
                for src, hi, lo in split_pieces(n):
                    ins = nc.scalar.copy(hi, src)
                ins.then_inc(s_high, 1)
            give(act, "ACT")

            def evac_xT(k):
                filled(act, "ACT", f"xT{k}")
                nc.scalar.copy(xT[:, k, :], bank(f"xT{k}")[:]).then_inc(sem["a_out_ACT"], 1)

            def square_q(s):
                act.wait_ge(sem["qrot_ready"], s + 1)
                for t, done in ((2 * s, "a_out_ACT" if s else None), (2 * s + 1, "ssq_ready" if s else "a_out_ACT")):
                    ins = nc.scalar.activation(tmp[:, t, :], qrot[:, t, :], ACT.Square, accum_out=ve[:, t:t + 1])
                    if done:
                        ins.then_inc(sem[done], 1)

            def high(dst, name):
                filled(act, "ACT", name)
                nc.scalar.copy(dst, bank(name)[:]).then_inc(sem["hi_ready"], 1)

            def softplus():
                act.wait_ge(sem["na_ready"], 1)
                own.do(nc.scalar.activation(e1[:], na[:], ACT.Exp))
                nc.scalar.activation(l1[:], e1[:], ACT.Ln, bias=one1[:, 0:1]).then_inc(sem["ln_ready"], 1)

            def conv_first(b):
                filled(act, "ACT", f"xc{b}")
                nc.scalar.activation(xc[:, b, :], bank(f"xc{b}")[:], ACT.Identity, bias=cbv[:, b:b + 1],
                                     scale=cw[:, b, TAPS - 1:TAPS]).then_inc(sem["conv_first"], 1)

            def conv_silu(b, n):
                act.wait_ge(sem["conv_ready"], n)
                nc.scalar.activation(xc[:, b, :], xc[:, b, :], ACT.Silu).then_inc(sem["a_out_ACT"], 1)

            def decays():
                act.wait_ge(sem["acs_ready"], 1)
                nc.scalar.activation(ea[:].rearrange("p t h -> p (t h)"), acs[:, 0, :], ACT.Exp)
                nc.scalar.activation(el[:].rearrange("p t h -> p (t h)"), acs[:, 1, :], ACT.Exp)
                nc.scalar.activation(ed[:], ed[:], ACT.Exp).then_inc(sem["decay_ready"], 1)

            def exp_seg(c):
                act.wait_ge(sem["seg_ready"], c + 1)
                nc.scalar.activation(seg[:, c, :, :], seg[:, c, :, :], ACT.Exp).then_inc(sem["exp_ready"], 1)

            def silu_z(j):
                filled(act, "ACT", f"z{j}")
                nc.scalar.activation(zs[:, j, :], bank(f"z{j}")[:], ACT.Silu).then_inc(sem["a_out_ACT"], 1)

            def evac_B():
                filled(act, "ACT", "Bt")
                nc.scalar.copy(Btok[:].rearrange("p t n -> p (t n)"), bank("Bt")[:]).then_inc(sem["a_out_ACT"], 1)

            def square_y(j):
                act.wait_ge(sem["yg_ready"], j + 1)
                dst = xdec[:, j, :] if j < 2 else xT[:, j - 2, :]
                nc.scalar.activation(dst, zs[:, j, :], ACT.Square).then_inc(sem["a_out_ACT"], 1)

            def save_x1():
                act.wait_ge(sem["x1_ready"], 1)
                act.wait_ge(sem["x1_free"], 1)
                nc.scalar.copy(x1[:], tmp[:]).then_inc(sem["tmp_free"], 1)

            def score_tanh():
                filled(act, "ACT", "logits")
                nc.scalar.activation(th[:], bank("logits")[:, 0:NT * E], ACT.Tanh, scale=0.5
                                     ).then_inc(sem["tanh_ready"], 1)

            def evac_cT():
                filled(act, "ACT", "cT")
                nc.scalar.copy(cT[:], bank("cT")[0:E, :]).then_inc(sem["cT_ready"], 1)

            def gate(j):
                act.wait_ge(sem["down_done"], now("down_done", j - 2) if j >= 3 else HB - 2 + j)
                filled(act, "ACT", f"G{j}")
                nc.scalar.activation(hid[:, j % 3, :], bank(f"G{j}")[:], ACT.Silu).then_inc(sem["silu_ready"], 1)

            def iteration(a, f):
                if f: save_x1(); score_tanh(); gate(0); gate(1)
                if a: evac_xT(0); evac_xT(1)
                if f: gate(2)
                if f: gate(3); evac_cT(); gate(4)
                if a: square_q(0); square_q(1)
                if f: gate(5)
                if a: high(hTh[:, 0, :], "hT0"); high(hTh[:, 1, :], "hT1")
                if f: gate(6)
                if a:
                    nc.scalar.preload_act_table_set("natural_log_exp_and_others")
                    softplus()
                    conv_first(4); conv_first(5)
                    conv_silu(4, 1); conv_first(0); conv_silu(5, 2)
                    conv_silu(0, 3)
                    conv_first(1); conv_first(2); conv_silu(1, 4)
                    conv_first(3); conv_silu(2, 5); conv_silu(3, 6)
                    silu_z(0); silu_z(1)
                if f: gate(7)
                if a:
                    silu_z(2); silu_z(3); evac_B()
                    nc.scalar.preload_act_table_set("natural_log_exp_and_others")
                    decays()
                    for c in range(NT):
                        exp_seg(c)
                if f: gate(8); gate(9)
                if a:
                    for j in range(NB):
                        square_y(j)
                if f: gate(10); gate(11)
                if a: high(fTh[:, 0, :], "fT0"); high(fTh[:, 1, :], "fT1")
                own.settle()
                if a: settle(act, "ACT", "a")
                if f: settle(act, "ACT", "f")

            own.settle()
            iteration(True, False)
            with act.Fori(1, SEQS):
                iteration(True, True)
            iteration(False, True)

        @block.vector
        def _(dve):
            own = Own(dve, "dve")
            V = nc.vector
            dve.wait_ge(s_const, NCONST)
            for k in range(NB):
                V.tensor_scalar(WO[:, k, :], WO[:, k, :], ngwc[:, k:k + 1], None, ALU.mult)
            for n, (kind, k, w) in enumerate(STAGED):
                if kind == "z":
                    dve.wait_ge(w_loaded[n], 16)
                    src = stage[:, n % 2, 0:w]
                    V.tensor_scalar(src, src, npwc[:, k:k + 1], None, ALU.mult).then_inc(s_scaled, 1)
            for n, (kind, k, w) in enumerate(STAGED):
                dve.wait_ge(s_high, n + 1)
                for src, hi, lo in split_pieces(n):
                    ins = V.tensor_tensor(lo, src, hi.bitcast(fp32), ALU.subtract)
                ins.then_inc(s_low, 1)
            own.do(V.tensor_scalar(aneg[:], aneg[:], -1.0, None, ALU.mult))
            own.settle()
            give(dve, "DVE")

            def moments(src, st, m, evac=(), relay=()):
                for t in range(NT):
                    ins = V.bn_stats(st[:, t, :], src(t))
                    if t < len(evac):
                        ins.then_inc(sem[evac[t]], 1)
                own.do(ins)
                for t in range(NT):
                    ins = V.bn_aggr(m[:, t, :], st[:, t, :])
                own.do(ins)

            def normalise(dst, src, nth, done=None):
                V.tensor_scalar(ve[:], mv[:, :, 1], EPS, None, ALU.add).then_inc(sem["var_ready"], 1)
                dve.wait_ge(sem["rstd_ready"], nth)
                for t in range(NT):
                    ins = V.tensor_scalar(dst[:, t, :], src[:, t, :], mv[:, t, 0:1], rstd[:, t:t + 1],
                                          ALU.subtract, ALU.mult)
                if done:
                    ins.then_inc(sem[done], 1)
                else:
                    own.do(ins)

            def norm_x():
                dve.wait_ge(sem["x_loaded"], 16)
                moments(lambda t: xs[:, t, :], st6, mv)
                normalise(xn, xs, 1, "xn_ready")

            def rope(s):
                filled(dve, "DVE", f"q{s}")
                if s == 0:
                    dve.wait_ge(sem["tmp_free"], 1)
                sl = slice(2 * s, 2 * s + 2)
                q = bank(f"q{s}")[:].rearrange("p (t h a f) -> p t h a f", t=2, a=2, f=HALF)
                o = tmp[:, sl, :].rearrange("p t (h a f) -> p t h a f", a=2, f=HALF)
                for a in range(2):
                    V.tensor_tensor(o[:, :, :, a, :], q[:, :, :, 1 - a, :],
                                    sin_t[:, sl, a, :].unsqueeze(2).broadcast_to([P, 2, HEADS, HALF]), ALU.mult)
                V.tensor_tensor(qrot[:, sl, :].rearrange("p t (g f) -> p t g f", f=HALF),
                                bank(f"q{s}")[:].rearrange("p (t g f) -> p t g f", t=2, f=HALF),
                                cos_t[:, sl, :].unsqueeze(2).broadcast_to([P, 2, 2 * HEADS, HALF]), ALU.mult
                                ).then_inc(sem["rope_ready"], 1)

            def norm_q():
                dve.wait_ge(sem["ssq_ready"], 1)
                V.tensor_scalar(ve[:], ve[:], 1.0 / D, EPS, ALU.mult, ALU.add).then_inc(sem["var_ready"], 1)
                dve.wait_ge(sem["rstd_ready"], 2)
                for t in range(NT):
                    ins = V.tensor_scalar(xn[:, t, :], qrot[:, t, :], rstd[:, t:t + 1], None, ALU.mult)
                ins.then_inc(sem["xn_ready"], 1)

            def low(lo, hi, name, n):
                dve.wait_ge(sem["hi_ready"], n)
                V.tensor_tensor(lo, bank(name)[:], hi.bitcast(fp32), ALU.subtract).then_inc(sem["a_out_DVE"], 1)

            def dt_bias_add():
                filled(dve, "DVE", "dt")
                own.do(V.tensor_tensor(dr[:], bank("dt")[:, 0:NT * HS].rearrange("p (t h) -> p t h", t=NT),
                                       dtb[:].unsqueeze(1).broadcast_to([P, NT, HS]), ALU.add))
                dve.sem_inc(sem["a_out_DVE"], 1)
                V.scalar_tensor_tensor(na[:], dr[:], -1.0, dr[:], ALU.mult, ALU.min).then_inc(sem["na_ready"], 1)

            def dt_finish():
                dve.wait_ge(sem["ln_ready"], 1)
                own.do(V.scalar_tensor_tensor(dt[:], dr[:], 0.0, l1[:], ALU.max, ALU.add))
                V.tensor_tensor(ad[:], dt[:], aneg[:].unsqueeze(1).broadcast_to([P, NT, HS]), ALU.mult
                                ).then_inc(sem["ad_ready"], 1)

            def conv(b, n):
                dve.wait_ge(sem["conv_first"], n)
                src = bank(f"xc{b}")
                for s in range(1, TAPS):
                    ins = V.scalar_tensor_tensor(xc[:, b, s:], src[:, 0:T - s], cw[:, b, TAPS - 1 - s:TAPS - s],
                                                 xc[:, b, s:], ALU.mult, ALU.add)
                    if s < TAPS - 1:
                        own.do(ins)
                ins.then_inc(sem["conv_ready"], 1)

            def evac_acs():
                filled(dve, "DVE", "acs")
                V.tensor_copy(acs[:].rearrange("p a n -> p (a n)"), bank("acs")[:, 0:2 * NT * HS])
                own.do(V.tensor_copy(acsT[:], bank("acs")[0:NT * HS, P:2 * P]))
                dve.sem_inc(sem["acsT_ready"], 1)
                dve.sem_inc(sem["a_out_DVE"], 1)
                V.tensor_tensor(ed[:].rearrange("p t h -> p (t h)"), acs[:, 1, :], acs[:, 0, :], ALU.subtract
                                ).then_inc(sem["acs_ready"], 1)

            def decay_exponents(c):
                if c == 0:
                    dve.wait_ge(sem["seg_loaded"], 16)
                for h in range(HS):
                    own_row = acs[:, 0, c * HS + h:c * HS + h + 1]
                    ins = V.tensor_scalar(seg[:, c, h, :], seg[:, c, h, :], own_row, own_row, ALU.min, ALU.subtract)
                ins.then_inc(sem["seg_ready"], 1)

            def mask_CB():
                filled(dve, "DVE", "CB")
                V.tensor_tensor(CBm[:], bank("CB")[:].rearrange("p (t n) -> p t n", t=NT),
                                upper[:].unsqueeze(1).broadcast_to([P, NT, P]), ALU.mult
                                ).then_inc(sem["a_out_DVE"], 1)

            def by_head(ap):
                return ap.rearrange("p (h d) -> p h d", h=HS)

            def along(small):
                return small.unsqueeze(2).broadcast_to([P, HS, PD])

            def times_dt(c):
                if c == 0:
                    dve.wait_ge(sem["decay_ready"], 1)
                filled(dve, "DVE", f"xt{c}")
                own.do(V.tensor_tensor(by_head(xdt[:, c, :]), by_head(bank(f"xt{c}")[:]), along(dt[:, c, :]), ALU.mult))
                dve.sem_inc(sem["a_out_DVE"], 1)
                if c < NT - 1:
                    dve.sem_inc(sem["xdt_ready"], 1)

            def decay_CB(c):
                dve.wait_ge(sem["exp_ready"], c + 1)
                V.tensor_tensor(seg[:, c, :, :], seg[:, c, :, :],
                                CBm[:, c, :].unsqueeze(1).broadcast_to([P, HS, P]), ALU.mult
                                ).then_inc(sem["m_ready"], 1)

            def state_part(c):
                filled(dve, "DVE", f"yo{c}")
                own.do(V.tensor_tensor(by_head(xT[:, c % 2, :]), by_head(bank(f"yo{c}")[:]), along(ea[:, c, :]), ALU.mult))
                dve.sem_inc(sem["a_out_DVE"], 1)

            def new_state(c):
                if c:
                    own.do(V.tensor_tensor(by_head(S[:]), by_head(S[:]), along(el[:, c, :]), ALU.mult))
                filled(dve, "DVE", f"st{c}")
                if c:
                    ins = V.tensor_tensor(S[:], S[:], bank(f"st{c}")[:], ALU.add)
                else:
                    ins = V.tensor_copy(S[:], bank("st0")[:])
                own.do(ins)
                dve.sem_inc(sem["a_out_DVE"], 1)

            def chunk_y(c):
                filled(dve, "DVE", f"yd{c}")
                if c:
                    ins = V.tensor_tensor(xdt[:, c, :], xT[:, c % 2, :], bank(f"yd{c}")[:], ALU.add)
                else:
                    ins = V.tensor_copy(xdt[:, c, :], bank(f"yd{c}")[:])
                ins.then_inc(sem["a_out_DVE"], 1)

            def add_Dx(j):
                filled(dve, "DVE", f"yT{j}")
                V.scalar_tensor_tensor(xc[:, j, :], xc[:, j, :], dcol[:, j:j + 1], bank(f"yT{j}")[:],
                                       ALU.mult, ALU.add).then_inc(sem["v_ready"], 1)

            def norm_gated():
                filled(dve, "DVE", "ssq")
                own.do(V.tensor_scalar(ve[:], bank("ssq")[:, 0:NT], 1.0 / DI, EPS, ALU.mult, ALU.add))
                dve.sem_inc(sem["var_ready"], 1)
                dve.sem_inc(sem["a_out_DVE"], 1)

            def mixed_out():
                dve.wait_ge(sem["rstd_ready"], 3)
                for t in range(NT):
                    filled(dve, "DVE", f"out{t // 2}")
                    ins = V.scalar_tensor_tensor(
                        tmp[:, t, :], bank(f"out{t // 2}")[:, (t % 2) * D:(t % 2 + 1) * D], rstd[:, t:t + 1],
                        qrot[:, t, :], ALU.mult, ALU.add)
                own.do(ins)
                dve.sem_inc(sem["a_out_DVE"], 2)
                moments(lambda t: tmp[:, t, :], st6, mv)

            def form_x1():
                normalise(tmp, tmp, 4)
                own.do(V.tensor_tensor(tmp[:], tmp[:], xs[:], ALU.add))
                moments(lambda t: tmp[:, t, :], st6, mv, evac=("x_free", "x1_ready"))

            def norm_x1():
                normalise(xn, tmp, 5, "xn_ready")

            def up(j):
                dve.wait_ge(sem["silu_ready"], j + 1)
                filled(dve, "DVE", f"U{j}")
                V.tensor_tensor(hid[:, j % 3, :], hid[:, j % 3, :], bank(f"U{j}")[:], ALU.mult
                                ).then_inc(sem["f_out_DVE" if j < SB else "h_half"], 1)

            te = "p (t e) -> p t e"

            def route_scores():
                dve.wait_ge(sem["tanh_ready"], 1)
                own.do(V.tensor_scalar(sc[:], th[:], 0.5, 0.5, ALU.mult, ALU.add))
                dve.sem_inc(sem["f_out_DVE"], 1)
                own.do(V.tensor_tensor(sbs[:].rearrange(te, t=NT), sc[:].rearrange(te, t=NT),
                                       ebias[:].unsqueeze(1).broadcast_to([P, NT, E]), ALU.add))

            def route_groups():
                pairs = sbs[:].rearrange("p (g a b) -> p g a b", a=2, b=2)
                V.tensor_tensor(hi2[:], pairs[:, :, :, 0], pairs[:, :, :, 1], ALU.max)
                own.do(V.tensor_tensor(lo2[:], pairs[:, :, :, 0], pairs[:, :, :, 1], ALU.min))
                V.tensor_tensor(m1[:], hi2[:, :, 0], hi2[:, :, 1], ALU.max)
                V.tensor_tensor(mn[:], hi2[:, :, 0], hi2[:, :, 1], ALU.min)
                own.do(V.tensor_tensor(rk[:], lo2[:, :, 0], lo2[:, :, 1], ALU.max))
                own.do(V.tensor_tensor(mn[:], mn[:], rk[:], ALU.max))
                own.do(V.tensor_tensor(gs[:], m1[:], mn[:], ALU.add))
                g4 = gs[:].rearrange("p (t g) -> p t g", t=NT)
                theirs = g4.unsqueeze(2).broadcast_to([P, NT, GROUPS, GROUPS])
                ours = g4.unsqueeze(3).broadcast_to([P, NT, GROUPS, GROUPS])
                v4 = "p (t g j) -> p t g j"
                GT, EQ = (b[:].rearrange(v4, t=NT, g=GROUPS) for b in (gt, eq))
                V.tensor_tensor(GT, theirs, ours, ALU.is_gt)
                own.do(V.tensor_tensor(EQ, theirs, ours, ALU.is_equal))
                own.do(V.tensor_tensor(EQ, EQ, tri[:].unsqueeze(1).broadcast_to([P, NT, GROUPS, GROUPS]), ALU.mult))
                own.do(V.tensor_tensor(gt[:], gt[:], eq[:], ALU.add))
                own.do(V.reduce_sum(rk[:], gt[:].rearrange("p (g j) -> p g j", j=GROUPS), AX.X))
                own.do(V.tensor_scalar(rk[:], rk[:], float(TOPG), NEVER, ALU.is_ge, ALU.mult))
                own.do(V.tensor_tensor(msk[:].rearrange("p (g j) -> p g j", j=GROUPS),
                                       sbs[:].rearrange("p (g j) -> p g j", j=GROUPS),
                                       rk[:].unsqueeze(2).broadcast_to([P, NT * GROUPS, GROUPS]), ALU.add))

            def route_experts():
                for t in range(NT):
                    ins = V.max(v8[:, t, :], msk[:, t * E:(t + 1) * E])
                own.do(ins)
                m3 = msk[:].rearrange(te, t=NT)
                fourth = v8[:, :, TOPK - 1:TOPK].broadcast_to([P, NT, E])
                V.tensor_tensor(gt[:].rearrange(te, t=NT), m3, fourth, ALU.is_gt)
                own.do(V.tensor_tensor(eq[:].rearrange(te, t=NT), m3, fourth, ALU.is_equal))
                V.reduce_sum(ws[:], gt[:].rearrange(te, t=NT), AX.X)
                own.do(V.tensor_tensor_scan(pre[:], reset[:], eq[:], 0.0, ALU.mult, ALU.add))
                p3 = pre[:].rearrange(te, t=NT)
                own.do(V.tensor_tensor(p3, p3, ws[:].unsqueeze(2).broadcast_to([P, NT, E]), ALU.add))
                own.do(V.scalar_tensor_tensor(eq[:], pre[:], float(TOPK), eq[:], ALU.is_le, ALU.mult))
                own.do(V.tensor_tensor(gt[:], gt[:], eq[:], ALU.add))
                own.do(V.tensor_tensor(gt[:], gt[:], sc[:], ALU.mult))
                own.do(V.reduce_sum(ws[:], gt[:].rearrange(te, t=NT), AX.X))
                own.do(V.tensor_scalar(ws[:], ws[:], 1e-20, None, ALU.add))
                own.do(V.reciprocal(ws[:], ws[:]))
                V.tensor_tensor(gt[:].rearrange(te, t=NT), gt[:].rearrange(te, t=NT),
                                ws[:].unsqueeze(2).broadcast_to([P, NT, E]), ALU.mult).then_inc(sem["c_ready"], 1)

            def final():
                dve.wait_ge(sem["acc_ready"], 1)
                dve.sem_inc(sem["down_done"], 1)
                moments(lambda t: acc[t // 2][:, (t % 2) * D:(t % 2 + 1) * D], fst6, fmv)
                V.tensor_scalar(fve[:], fmv[:, :, 1], EPS, None, ALU.add).then_inc(sem["fvar_ready"], 1)
                dve.wait_ge(sem["fo_free"], 1)
                dve.wait_ge(sem["frstd_ready"], 1)
                for t in range(NT):
                    ins = V.tensor_scalar(fo[:, t, :], acc[t // 2][:, (t % 2) * D:(t % 2 + 1) * D], fmv[:, t, 0:1],
                                          frstd[:, t:t + 1], ALU.subtract, ALU.mult)
                own.do(ins)
                dve.sem_inc(sem["acc_free"], 1)
                dve.sem_inc(sem["fo_half"], 1)

            def iteration(a, f):
                if a: norm_x()
                if f: route_scores(); up(0); route_groups(); up(1); route_experts(); up(2)
                if a: rope(0); rope(1)
                if f: up(3); up(4)
                if a: norm_q()
                if f: up(5)
                if a: low(hTl[:, 0, :], hTh[:, 0, :], "hT0", 1); low(hTl[:, 1, :], hTh[:, 1, :], "hT1", 2)
                if f: up(6)
                if a:
                    dt_bias_add(); conv(4, 1); dt_finish(); conv(5, 2); conv(0, 3)
                    evac_acs(); conv(1, 4); conv(2, 5); conv(3, 6)
                if f: up(7)
                if a:
                    for c in range(NT):
                        decay_exponents(c)
                    mask_CB()
                    times_dt(0); decay_CB(0); new_state(0); chunk_y(0)
                    times_dt(1); decay_CB(1)
                if f: up(8)
                if a:
                    state_part(1); new_state(1); chunk_y(1)
                    times_dt(2); decay_CB(2); state_part(2); new_state(2); chunk_y(2)
                if f: up(9)
                if a:
                    times_dt(3); decay_CB(3); state_part(3); chunk_y(3)
                    for j in range(NB):
                        add_Dx(j)
                    norm_gated()
                if f: up(10)
                if a: mixed_out()
                if f: up(11)
                if a: form_x1(); norm_x1()
                if f: final()
                if a: low(fTl[:, 0, :], fTh[:, 0, :], "fT0", 3); low(fTl[:, 1, :], fTh[:, 1, :], "fT1", 4)
                own.settle()
                if a: settle(dve, "DVE", "a")
                if f: settle(dve, "DVE", "f")

            iteration(True, False)
            with dve.Fori(1, SEQS):
                iteration(True, True)
            iteration(False, True)

        @block.tensor
        def _(pe):
            pe.wait_ge(s_low, len(STAGED))
            pe.wait_ge(s_fill, 3)
            give(pe, "PE")

            def out_of(name):
                part, n = WHERE[name]
                if SLOTS[part][n][2] == "with U":
                    n += 1
                who = SLOTS[part][n][2]
                return f"{part}_out_{who}", count(part, 2, who, n)

            def slot(name):
                part, n = WHERE[name]
                if n >= 3:
                    s, k = out_of(SLOTS[part][n - 3][0])
                    pe.wait_ge(sem[s], now(s, k))
                else:
                    s, k = out_of(SLOTS[part][n - 3][0])
                    pe.wait_ge(sem[s], k)
                return bank(name)

            def read_out(name):
                s, k = out_of(name)
                pe.wait_ge(sem[s], now(s, k))

            def fill(name, ins):
                part, n = WHERE[name]
                ins.then_inc(sem[f"{part}_for_{SLOTS[part][n][1]}"], 1)

            def split_mm(dst, parts, last=True):
                n, total = 0, 3 * len(parts)
                for ah, al, bh, bl in parts:
                    for l, r in ((ah, bh), (ah, bl), (al, bh)):
                        ins = nc.tensor.matmul(dst, l, r, start=n == 0, stop=n == total - 1)
                        n += 1
                return ins

            def transposes(name, src, n=NT):
                b = slot(name)
                for t in range(n):
                    ins = nc.tensor.transpose(b[:, t * P:(t + 1) * P], src(t), ident[:])
                return ins

            def x_transposes(names, nth):
                pe.wait_ge(sem["xn_ready"], nth)
                for k, name in enumerate(names):
                    fill(name, transposes(name, lambda t: xn[:, t, k * P:(k + 1) * P]))

            def project_q(s):
                b = slot(f"q{s}")
                read_out("xT1")
                for t in range(2):
                    for k in range(KD):
                        ins = nc.tensor.matmul(b[:, t * D:(t + 1) * D], xT[:, k, (2 * s + t) * P:(2 * s + t + 1) * P],
                                               WQ[:, k, :], start=k == 0, stop=k == KD - 1)
                fill(f"q{s}", ins)

            def project_dt():
                b = slot("dt")
                read_out("hT1")
                for t in range(NT):
                    tk = slice(t * P, (t + 1) * P)
                    ins = split_mm(b[:, t * HS:(t + 1) * HS],
                                   [(hTh[:, k, tk], hTl[:, k, tk], DTH[:, k, :], DTL[:, k, :]) for k in range(KD)])
                fill("dt", ins)

            def project(name, col):
                b = slot(name)
                cs = slice(col, col + P)
                fill(name, split_mm(b[:], [(ZH[:, k, cs], ZL[:, k, cs], hTh[:, k, :], hTl[:, k, :]) for k in range(KD)]))

            def project_x(b):
                project(f"xc{b}", DI + b * P)

            def cumulate():
                b = slot("acs")
                pe.wait_ge(sem["ad_ready"], 1)
                rhs = ad[:].rearrange("p t h -> p (t h)")
                n = NT * HS
                nc.tensor.matmul(b[:, 0:n], upper[:], rhs, start=True, stop=True)
                nc.tensor.matmul(b[:, n:2 * n], ones[:], rhs, start=True, stop=True)
                fill("acs", nc.tensor.matmul(b[0:n, P:2 * P], rhs, upper[:], start=True, stop=True))

            def B_by_token():
                read_out("xc4")
                fill("Bt", transposes("Bt", lambda t: xc[:, 4, t * P:(t + 1) * P]))

            def CB():
                b = slot("CB")
                read_out("xc5")
                for t in range(NT):
                    tk = slice(t * P, (t + 1) * P)
                    ins = nc.tensor.matmul(b[:, tk], xc[:, 4, tk], xc[:, 5, tk], start=True, stop=True)
                fill("CB", ins)

            def x_by_token(c):
                read_out("xc3")
                fill(f"xt{c}", transposes(f"xt{c}", lambda j: xc[:, j, c * P:(c + 1) * P], NB))

            def from_state(c):
                b = slot(f"yo{c}")
                read_out(f"st{c - 1}")
                fill(f"yo{c}", nc.tensor.matmul(b[:], xc[:, 5, c * P:(c + 1) * P], S[:], start=True, stop=True))

            def state(c):
                b = slot(f"st{c}")
                pe.wait_ge(sem["xdec_ready"], c + 1)
                fill(f"st{c}", nc.tensor.matmul(b[:], Btok[:, c, :], xdec[:, c % 2, :], start=True, stop=True))

            def diagonal(c):
                b = slot(f"yd{c}")
                pe.wait_ge(sem["m_ready"], c + 1)
                for h in range(HS):
                    hs = slice(h * PD, (h + 1) * PD)
                    ins = nc.tensor.matmul(b[:, hs], seg[:, c, h, :], xdt[:, c, hs], start=True, stop=True)
                fill(f"yd{c}", ins)

            def y_by_channel(j):
                b = slot(f"yT{j}")
                read_out(f"yd{NT - 1}")
                for t in range(NT):
                    ins = nc.tensor.transpose(b[:, t * P:(t + 1) * P], xdt[:, t, j * P:(j + 1) * P], ident[:])
                    if j == 0 and t == 0:
                        ins.then_inc(sem["seg_free"], 1)
                fill(f"yT{j}", ins)

            def squares():
                b = slot("ssq")
                for j in range(NB):
                    read_out(f"yT{j}")
                    src = xdec[:, j, :] if j < 2 else xT[:, j - 2, :]
                    for t in range(NT):
                        ins = nc.tensor.matmul(b[:, t:t + 1], src[:, t * P:(t + 1) * P], ones[:, 0:1],
                                               start=j == 0 and t == 0, stop=j == NB - 1, skip_group_check=True)
                fill("ssq", ins)

            def project_out(s):
                b = slot(f"out{s}")
                for t in range(2):
                    for j in range(NB):
                        ins = nc.tensor.matmul(b[:, t * D:(t + 1) * D], zs[:, j, (2 * s + t) * P:(2 * s + t + 1) * P],
                                               WO[:, j, :], start=j == 0, stop=j == NB - 1)
                fill(f"out{s}", ins)

            def logits():
                b = slot("logits")
                pe.wait_ge(sem["a_out_DVE"], SEM["a_out_DVE"][2])
                for t in range(NT):
                    tk = slice(t * P, (t + 1) * P)
                    ins = split_mm(b[:, t * E:(t + 1) * E],
                                   [(fTh[:, k, tk], fTl[:, k, tk], RH[:, k, :], RL[:, k, :]) for k in range(KD)])
                fill("logits", ins)

            def combine_by_expert():
                b = slot("cT")
                pe.wait_ge(sem["c_ready"], 1)
                for t in range(NT):
                    ins = nc.tensor.transpose(b[0:E, t * P:(t + 1) * P], gt[:, t * E:(t + 1) * E], ident[:])
                fill("cT", ins)

            def hidden(name, hi, lo, j):
                b = slot(name)
                cs = slice(j * P, (j + 1) * P)
                fill(name, split_mm(b[:], [(hi[:, k, cs], lo[:, k, cs], fTh[:, k, :], fTl[:, k, :]) for k in range(KD)]))

            def down(j):
                read_out(f"U{j}")
                if j == 0:
                    pe.wait_ge(sem["acc_free"], 1)
                for t in range(NT):
                    ins = nc.tensor.matmul(acc[t // 2][:, (t % 2) * D:(t % 2 + 1) * D],
                                           hid[:, j % 3, t * P:(t + 1) * P], WD[:, j, :],
                                           start=j == 0 and t % 2 == 0, stop=j == HB - 1, skip_group_check=True)
                    if t == 0 and j >= SB:
                        ins.then_inc(sem["cb_free"], 1)
                ins.then_inc(sem["acc_ready" if j == HB - 1 else "down_done"], 1)

            def block_of(j):
                hidden(f"G{j}", GH, GL, j)
                if j >= 2:
                    down(j - 2)
                hidden(f"U{j}", UH, UL, j)

            def iteration(a, f):
                if f: logits(); block_of(0); block_of(1)
                if a: x_transposes(("xT0", "xT1"), 1)
                if f: block_of(2)
                if a: project_q(0); project_q(1)
                if f: block_of(3); combine_by_expert(); block_of(4); block_of(5)
                if a: x_transposes(("hT0", "hT1"), 2)
                if f: block_of(6)
                if a:
                    project_dt(); project_x(4); project_x(5); project_x(0)
                    cumulate()
                    project_x(1); project_x(2); project_x(3)
                    project("z0", 0); project("z1", P)
                if f: block_of(7)
                if a:
                    project("z2", 2 * P); project("z3", 3 * P)
                    B_by_token(); CB()
                    x_by_token(0); state(0); diagonal(0); x_by_token(1)
                if f: block_of(8)
                if a:
                    from_state(1); state(1); diagonal(1)
                    x_by_token(2); from_state(2); state(2); diagonal(2)
                if f: block_of(9)
                if a:
                    x_by_token(3); from_state(3); diagonal(3)
                    for j in range(NB):
                        y_by_channel(j)
                    squares()
                if f: block_of(10)
                if a: project_out(0); project_out(1)
                if f: block_of(11); down(10); down(11)
                if a: x_transposes(("fT0", "fT1"), 3)
                if a: settle(pe, "PE", "a")
                if f: settle(pe, "PE", "f")

            iteration(True, False)
            with pe.Fori(1, SEQS):
                iteration(True, True)
            iteration(False, True)


def kernel(**inputs):
    import numpy as np
    import concourse.bacc as bacc
    from concourse.bass_utils import run_bass_kernel_spmd as run

    g = {k: np.asarray(v) for k, v in inputs.items()}

    def t(a):
        return np.ascontiguousarray(a.T)

    def by_expert(w):
        return np.ascontiguousarray(w.transpose(1, 0, 2).reshape(D, E * EH))

    angle = np.arange(T, dtype=np.float32)[:, None] * (
        np.float32(1.0) / np.float32(10000.0) ** (np.arange(0, 2 * HALF, 2, dtype=np.float32) / np.float32(2 * HALF))
    )[None, :]
    angle = angle.astype(np.float32)
    sin = np.sin(angle).astype(np.float32)
    arrays = {
        "x": g["L0_attn_x"],
        "wq_t": t(g["L0_attn_W_in"][:D]),
        "wzx_t": t(g["L0_attn_W_zxbcdt"]),
        "conv_w": g["L0_attn_conv_w"], "conv_b": g["L0_attn_conv_b"], "dt_bias": g["L0_attn_dt_bias"],
        "a_log": g["L0_attn_A_log"], "d_param": g["L0_attn_D_param"],
        "npw": g["L0_attn_norm_pre_w"], "ngw": g["L0_attn_norm_gated_w"],
        "wo_t": t(g["L0_attn_W_out"]),
        "router_t": t(g["L0_ffn_router_w"]), "cbias": g["L0_ffn_correction_bias"],
        "wg_t": by_expert(g["L0_ffn_gate_w"]), "wu_t": by_expert(g["L0_ffn_up_w"]),
        "wd": g["L0_ffn_down_w"].reshape(E * EH, D),
        "swg_t": t(g["L0_ffn_shared_gate_w"]), "swu_t": t(g["L0_ffn_shared_up_w"]),
        "swd_t": t(g["L0_ffn_shared_down_w"]),
        "c_ident": np.eye(P, dtype=np.float32),
        "c_upper": np.triu(np.ones((P, P), np.float32)),
        "c_cos": np.cos(angle).astype(np.float32),
        "c_sin": np.concatenate([-sin, sin], axis=1),
        "c_reset": (np.arange(NT * E) % E != 0).astype(np.float32),
        "c_tri": np.tril(np.ones((GROUPS, GROUPS), np.float32), -1),
    }
    nc = bacc.Bacc("TRN2", target_bir_lowering=False, num_devices=1)
    in_map, args = {}, []
    for name, a in arrays.items():
        a = np.ascontiguousarray(a)
        in_map[f"in_{name}"] = a
        args.append(nc.dram_tensor(f"in_{name}", a.shape, mybir.dt.from_np(a.dtype), kind="ExternalInput").ap())
    args.append(nc.dram_tensor("out", (SEQS, T, D), mybir.dt.float32, kind="ExternalOutput").ap())
    build(nc, *args)
    return run(nc, [in_map], core_ids=[0]).results[0]["out"]
```

```python
import concourse.bass as bass
from concourse import mybir
from contextlib import ExitStack

SEQS, T, D = 32, 512, 256
HEADS, HALF = 16, 8
DI, HS, PD, NS = 512, 8, 64, 128
CONV, TAPS = DI + 2 * NS, 4
DT0 = 2 * DI + 2 * NS
E, EH, SH = 16, 64, 512
GROUPS, TOPK, TOPG = 4, 4, 2
P = 128
NT = T // P
KD = D // P
NB = DI // P
CB_ = CONV // P
HB = (SH + E * EH) // P
SB = SH // P
EPS = 1e-5
NEVER = -3e38


def build(nc, x, wq_t, wzx_t, conv_w, conv_b, dt_bias, a_log, d_param, npw, ngw, wo_t,
          router_t, cbias, wg_t, wu_t, wd, swg_t, swu_t, swd_t,
          c_ident, c_upper, c_cos, c_sin, c_reset, c_tri, out):
    fp32, f32r = mybir.dt.float32, mybir.dt.float32r
    ALU, ACT, AX = mybir.AluOpType, mybir.ActivationFunctionType, mybir.AxisListType

    ctx = ExitStack()
    with ctx:
        def sb(name, shape, dt=fp32):
            return ctx.enter_context(nc.sbuf_tensor(name, shape, dt))

        WQ = sb("WQ", [P, KD, D])
        ZH, ZL = sb("ZH", [P, KD, DT0], f32r), sb("ZL", [P, KD, DT0], f32r)
        DT = sb("DT", [P, KD, 2 * HS], f32r)
        R = sb("R", [P, KD, 2 * E], f32r)
        WO = sb("WO", [P, NB, D])
        GH, GL = sb("GH", [P, KD, HB * P], f32r), sb("GL", [P, KD, HB * P], f32r)
        UH, UL = sb("UH", [P, KD, HB * P], f32r), sb("UL", [P, KD, HB * P], f32r)
        WD = sb("WD", [P, HB, D])
        ident, upper, ones = sb("ident", [P, P]), sb("upper", [P, P]), sb("ones", [P, P])
        cos_t, sin_t = sb("cos_t", [P, NT, HALF]), sb("sin_t", [P, NT, 2, HALF])
        reset, tri = sb("reset", [P, NT * E]), sb("tri", [P, GROUPS, GROUPS])
        cw, cbv = sb("cw", [P, CB_, TAPS]), sb("cbv", [P, CB_])
        dtb, aneg, dbc = sb("dtb", [P, HS]), sb("aneg", [P, HS]), sb("dbc", [P, HS])
        ebias, npwc, ngwc = sb("ebias", [P, E]), sb("npwc", [P, KD]), sb("ngwc", [P, NB])
        mhalf, one1 = sb("mhalf", [P, NT]), sb("one1", [P, 1])
        xs = sb("xs", [P, NT, D])
        xn = sb("xn", [P, NT, D])
        xT = sb("xT", [P, KD, T])
        qrot, tmp = sb("qrot", [P, NT, D]), sb("tmp", [P, NT, D])
        hTh, hTl = sb("hTh", [P, KD, T], f32r), sb("hTl", [P, KD, T], f32r)
        xc = sb("xc", [P, CB_, T])
        zs = sb("zs", [P, NT, DI])
        yT = sb("yT", [P, 2, NB, P])
        Btok = sb("Btok", [P, NT, NS])
        xdt = sb("xdt", [P, NT, DI])
        xdec = sb("xdec", [P, 2, DI])
        seg = sb("seg", [P, NT, HS, P])
        S = sb("S", [P, DI])
        CBs = sb("CBs", [P, NT, P])
        acsT = sb("acsT", [NT * HS, P])
        st6 = sb("st6", [P, NT, 6])
        mv = sb("mv", [P, NT, 2])
        ve, rstd = sb("ve", [P, NT]), sb("rstd", [P, NT])
        ssq, rq = sb("ssq", [P, NT]), sb("rq", [P, NT])
        ssy, ry = sb("ssy", [P, NT]), sb("ry", [P, NT])
        dr, na, e1, l1 = (sb(n, [P, NT, HS]) for n in ("dr", "na", "e1", "l1"))
        dt, ad = sb("dt", [P, NT, HS]), sb("ad", [P, NT, HS])
        acs = sb("acs", [P, 2, NT * HS])
        ea, ed, el = (sb(n, [P, NT, HS]) for n in ("ea", "ed", "el"))
        x1 = sb("x1", [P, NT, D])
        fTh, fTl = sb("fTh", [P, KD, T], f32r), sb("fTl", [P, KD, T], f32r)
        hid = sb("hid", [P, 3, T])
        cb = sb("cb", [P, 2, T])
        fo = sb("fo", [P, NT, D])
        cT = cb[0:E, 0, :]
        fst6, fmv = sb("fst6", [P, NT, 6]), sb("fmv", [P, NT, 2])
        fve, frstd = sb("fve", [P, NT]), sb("frstd", [P, NT])
        th, sc, sbs, msk = (sb(n, [P, NT * E]) for n in ("th", "sc", "sbs", "msk"))
        gt, eq, pre = (sb(n, [P, NT * E]) for n in ("gt", "eq", "pre"))
        hi2, lo2 = sb("hi2", [P, NT * GROUPS, 2]), sb("lo2", [P, NT * GROUPS, 2])
        m1, mn, gs, rk = (sb(n, [P, NT * GROUPS]) for n in ("m1", "mn", "gs", "rk"))
        v8, ws = sb("v8", [P, NT, 8]), sb("ws", [P, NT])

        xD = xn[:].rearrange("p (a b) d -> p a (b d)", a=2)
        junk = (xc[:, 4, :], xdec[:, 1, :])

        acs_row = nc.dram_tensor("acs_row", (NT * HS, P), fp32, kind="Internal").ap()
        c_row = nc.dram_tensor("c_row", (E, T), fp32, kind="Internal").ap()

        def rows(ap, dims, offset=0):
            return bass.AP(tensor=ap.tensor, offset=ap.offset + offset, ap=dims)

        apb = [ctx.enter_context(nc.psum_tensor(f"apb{n}", [P, T], fp32)) for n in range(3)]
        fpb = [ctx.enter_context(nc.psum_tensor(f"fpb{n}", [P, T], fp32)) for n in range(3)]
        acc = [ctx.enter_context(nc.psum_tensor(f"acc{n}", [P, T], fp32)) for n in range(2)]

        A_SLOTS = [("xT0", "ACT", "ACT"), ("xT1", "ACT", "ACT"), ("q0", "DVE", "ACT"), ("q1", "DVE", "ACT"),
                   ("hT0", "ACT", "DVE"), ("hT1", "ACT", "DVE"), ("dt", "DVE", "DVE"),
                   ("xc4", "ACT", "ACT"), ("xc5", "ACT", "ACT"), ("xc0", "ACT", "ACT"), ("acs", "DVE", "DVE"),
                   ("xc1", "ACT", "ACT"), ("xc2", "ACT", "ACT"), ("xc3", "ACT", "ACT"),
                   ("Bt", "ACT", "ACT"), ("CB", "ACT", "ACT"), ("xt0", "DVE", "DVE"),
                   ("st0", "DVE", "DVE"), ("z0", "ACT", "ACT"), ("yd0", "DVE", "DVE"), ("xt1", "DVE", "DVE"),
                   ("yo1", "DVE", "DVE"), ("st1", "DVE", "DVE"), ("z1", "ACT", "ACT"), ("yd1", "DVE", "DVE"),
                   ("yT0", "ACT", "ACT"), ("xt2", "DVE", "DVE"),
                   ("yo2", "DVE", "DVE"), ("st2", "DVE", "DVE"), ("z2", "ACT", "ACT"), ("yd2", "DVE", "DVE"),
                   ("yT1", "ACT", "ACT"), ("xt3", "DVE", "DVE"), ("out0", "DVE", "DVE"),
                   ("yo3", "DVE", "DVE"), ("z3", "ACT", "ACT"), ("yd3", "DVE", "DVE"),
                   ("yT2", "ACT", "ACT"), ("yT3", "ACT", "ACT"), ("out1", "DVE", "DVE"),
                   ("fT0", "ACT", "DVE"), ("fT1", "ACT", "DVE")]
        F_SLOTS = [("logits", "DVE", "DVE")]
        for j in range(HB):
            F_SLOTS += [(f"G{j}", "ACT", "with U"), (f"U{j}", "DVE", "DVE" if j < SB else "POOL")]
            F_SLOTS += [("cT", "ACT", "SP")] * (j == SB - 1)
        SLOTS, BANKS = {"a": A_SLOTS, "f": F_SLOTS}, {"a": apb, "f": fpb}
        WHERE = {s[0]: (part, n) for part in SLOTS for n, s in enumerate(SLOTS[part])}

        def count(part, field, engine, upto=None):
            slots = SLOTS[part]
            return sum(s[field] == engine for s in slots[:len(slots) if upto is None else upto + 1])

        def bank(name):
            part, n = WHERE[name]
            return BANKS[part][n % 3]

        NR = HB - SB
        EARLY = 2
        SEM = {
            "x_free": ("SP", "a", 1, True), "acsT_ready": ("SP", "a", 1, False),
            "seg_free": ("SP", "a", 1, True), "acs_stored": ("SP", "a", 16, False),
            "cT_ready": ("SP", "f", 1, False), "c_stored": ("SP", "f", 16, False),
            "cb_free": ("SP", "f", NR, True), "fo_ready": ("SP", "f", 1, False),
            "stored": ("SP", "f", 16, True),
            "x_loaded": ("DVE", "a", 16, False), "rstd_ready": ("DVE", "a", 8, False), "hi_ready": ("DVE", "a", 4, False),
            "conv_first": ("DVE", "a", CB_, False), "ln_ready": ("DVE", "a", 1, False),
            "seg_loaded": ("DVE", "a", 16, False), "exp_ready": ("DVE", "a", NT, False),
            "decay_ready": ("DVE", "a", 1, False), "tmp_free": ("DVE", "a", 1, True),
            "a_for_DVE": ("DVE", "a", count("a", 1, "DVE"), False),
            "f_for_DVE": ("DVE", "f", count("f", 1, "DVE"), False),
            "silu_ready": ("DVE", "f", HB, False), "tanh_ready": ("DVE", "f", 1, False),
            "frstd_ready": ("DVE", "f", 1, False), "acc_ready": ("DVE", "f", 1, False),
            "fo_free": ("DVE", "f", 1, False),
            "a_for_ACT": ("ACT", "a", count("a", 1, "ACT"), False),
            "qrot_ready": ("ACT", "a", 2, False), "na_ready": ("ACT", "a", 1, False),
            "conv_ready": ("ACT", "a", CB_, False), "acs_ready": ("ACT", "a", 1, False),
            "masked": ("ACT", "a", NT, False), 
            "f_for_ACT": ("ACT", "f", count("f", 1, "ACT"), False),
            "down_done": ("ACT", "f", HB, True), "x1_ready": ("ACT", "f", 1, False),
            "x1_free": ("ACT", "f", 1, True), "logits_ready": ("ACT", "f", 1, False),
            "var_ready": ("POOL", "a", 5, False), "rope_ready": ("POOL", "a", 2, False),
            "ssq_ready": ("POOL", "a", 1, False), "ssy_ready": ("POOL", "a", 2, False),
            "seg_ready": ("POOL", "a", NT, False),
            "xdt_ready": ("POOL", "a", NT - 1, False), "y_ready": ("POOL", "a", NT, False),
            "z_ready": ("POOL", "a", NT, False),
            "fvar_ready": ("POOL", "f", 1, False), "h_half": ("POOL", "f", NR, False),
            "cb_loaded0": ("POOL", "f", 16 * NR // 2, False),
            "cb_loaded1": ("POOL", "f", 16 * NR // 2, False),
            "fo_half": ("POOL", "f", 1, False),
            "a_out_ACT": ("PE", "a", count("a", 2, "ACT"), True),
            "a_out_DVE": ("PE", "a", count("a", 2, "DVE"), True),
            "xn_ready": ("PE", "a", 4, False), "ad_ready": ("PE", "a", 1, False),
            "m_ready": ("PE", "a", NT, False), "yg_ready": ("PE", "a", NT, False), "xdec_ready": ("PE", "a", NT - 1, False),
            "f_out_SP": ("PE", "f", count("f", 2, "SP"), True),
            "f_out_DVE": ("PE", "f", count("f", 2, "DVE"), True),
            "f_out_POOL": ("PE", "f", count("f", 2, "POOL"), True),
            "c_ready": ("PE", "f", 1, False), "acc_free": ("PE", "f", 1, True),
        }
        sem = {n: ctx.enter_context(nc.semaphore(n)) for n in SEM}
        w_loaded = [ctx.enter_context(nc.semaphore(f"w_loaded{n}")) for n in range(8)]
        s_const = ctx.enter_context(nc.semaphore("consts_loaded"))
        s_scaled = ctx.enter_context(nc.semaphore("w_scaled"))
        s_high = ctx.enter_context(nc.semaphore("w_high"))
        s_low = ctx.enter_context(nc.semaphore("w_low"))
        s_fill = ctx.enter_context(nc.semaphore("consts_filled"))
        s_own = {n: ctx.enter_context(nc.semaphore(f"{n}_own")) for n in ("dve", "act", "pool")}
        NCONST = 18 * 16

        def give(eng, who):
            for n, (waiter, _, k, first) in SEM.items():
                if waiter == who and first:
                    eng.sem_inc(sem[n], k)

        def settle(eng, who, part):
            for n, (waiter, p_, k, _) in SEM.items():
                if waiter == who and p_ == part:
                    eng.sem_inc(sem[n], -k)

        def now(name, n=1):
            return SEM[name][2] + n

        def filled(eng, who, name):
            part, n = WHERE[name]
            eng.wait_ge(sem[f"{part}_for_{who}"], count(part, 1, who, n))

        class Own:

            def __init__(self, eng, name):
                self.eng, self.sem, self.n = eng, s_own[name], 0

            def mark(self, ins):
                self.n += 1
                ins.then_inc(self.sem, 1)

            def wait(self):
                if self.n:
                    self.eng.wait_ge(self.sem, self.n)

            def do(self, ins):
                self.mark(ins)
                self.wait()

            def settle(self):
                if self.n:
                    self.wait()
                    self.eng.sem_inc(self.sem, -self.n)
                self.n = 0

        stage = seg[:].rearrange("p a b c -> p (a b c)").rearrange("p (a n) -> p a n", a=2)
        STAGED = []
        for k in range(KD):
            STAGED.append(("z", k, DT0 + HS))
        for k in range(KD):
            STAGED.append(("r", k, E))
        for kind in ("g", "u"):
            for k in range(KD):
                STAGED.append((kind, k, HB * P))

        def split_pieces(n):
            kind, k, w = STAGED[n]
            src = stage[:, n % 2, :]
            if kind == "z":
                return [(src[:, 0:DT0], ZH[:, k, :], ZL[:, k, :]),
                        (src[:, DT0:DT0 + HS], DT[:, k, 0:HS], DT[:, k, HS:2 * HS])]
            if kind == "r":
                return [(src[:, 0:w], R[:, k, 0:E], R[:, k, E:2 * E])]
            hi, lo = {"g": (GH, GL), "u": (UH, UL)}[kind]
            return [(src[:, 0:w], hi[:, k, :], lo[:, k, :])]

        block = ctx.enter_context(nc.Block())

        @block.sync
        def _(sp):
            for dst, src in ((ident[:], c_ident), (upper[:], c_upper),
                             (cos_t[:], c_cos.rearrange("(t p) f -> p t f", p=P)),
                             (sin_t[:], c_sin.rearrange("(t p) (a f) -> p t a f", p=P, a=2)),
                             (reset[:], rows(c_reset, [[0, P], [1, NT * E]])),
                             (tri[:], rows(c_tri, [[0, P], [GROUPS, GROUPS], [1, GROUPS]])),
                             (cw[:], conv_w.rearrange("(b p) k -> p b k", p=P)),
                             (cbv[:], conv_b.rearrange("(b p) -> p b", p=P)),
                             (dtb[:], rows(dt_bias, [[0, P], [1, HS]])),
                             (aneg[:], rows(a_log, [[0, P], [1, HS]])),
                             (dbc[:], rows(d_param, [[0, P], [1, HS]])),
                             (ebias[:], rows(cbias, [[0, P], [1, E]])),
                             (npwc[:], npw.rearrange("(k p) -> p k", p=P)),
                             (ngwc[:], ngw.rearrange("(k p) -> p k", p=P)),
                             (WQ[:], wq_t.rearrange("(k p) n -> p k n", p=P)),
                             (WO[:], wo_t.rearrange("(k p) n -> p k n", p=P)),
                             (WD[:, 0:SB, :], swd_t.rearrange("(k p) n -> p k n", p=P)),
                             (WD[:, SB:HB, :], wd.rearrange("(k p) n -> p k n", p=P))):
                with nc.allow_non_contiguous_dma(reason="small columns of weights, once"):
                    sp.dma_start(dst, src).then_inc(s_const, 16)
            for n, (kind, k, w) in enumerate(STAGED):
                if n >= 2:
                    sp.wait_ge(s_low, n - 1)
                dst, sl = stage[:, n % 2, :], slice(k * P, (k + 1) * P)
                if kind in "gu":
                    shared, routed = {"g": (swg_t, wg_t), "u": (swu_t, wu_t)}[kind]
                    sp.dma_start(dst[:, 0:SH], shared[sl, :]).then_inc(w_loaded[n], 16)
                    sp.dma_start(dst[:, SH:w], routed[sl, :]).then_inc(w_loaded[n], 16)
                else:
                    src = {"z": wzx_t, "r": router_t}[kind]
                    sp.dma_start(dst[:, 0:w], src[sl, :]).then_inc(w_loaded[n], 16)
            sp.wait_ge(s_low, len(STAGED))
            give(sp, "SP")

            def load_x(i):
                sp.wait_ge(sem["x_free"], 1)
                sp.dma_start(xs[:], x[i].rearrange("(t p) d -> p t d", p=P)).then_inc(sem["x_loaded"], 16)

            def decay_rows():
                sp.wait_ge(sem["acsT_ready"], 1)
                sp.dma_start(acs_row, acsT[:]).then_inc(sem["acs_stored"], 16)
                sp.wait_ge(sem["acs_stored"], 16)
                sp.wait_ge(sem["seg_free"], 1)
                sp.dma_start(seg[:].rearrange("p a b c -> p (a b c)"),
                             rows(acs_row, [[0, P], [1, NT * HS * P]])).then_inc(sem["seg_loaded"], 16)

            def combine_rows():
                sp.wait_ge(sem["cT_ready"], 1)
                sp.sem_inc(sem["f_out_SP"], 1)
                sp.dma_start(c_row, cT).then_inc(sem["c_stored"], 16)
                sp.wait_ge(sem["c_stored"], 16)

            def combine_block(r):
                sp.wait_ge(sem["cb_free"], now("cb_free", r - 1) if r >= 2 else NR - 1 + r)
                sp.dma_start(cb[:, r % 2, :], rows(c_row, [[T, 2], [0, EH], [1, T]], 2 * r * T)
                             ).then_inc(sem[f"cb_loaded{r % 2}"], 16)

            def store(i):
                sp.wait_ge(sem["fo_ready"], 1)
                sp.sem_inc(sem["x1_free"], 1)
                sp.dma_start(out[i].rearrange("(t p) d -> p t d", p=P), fo[:]).then_inc(sem["stored"], 16)

            def iteration(i, attn, ffn):
                if attn:
                    load_x(i)
                if ffn:
                    sp.wait_ge(sem["stored"], 16)
                    sp.sem_inc(sem["fo_free"], 1)
                    combine_rows()
                    for r in range(EARLY):
                        combine_block(r)
                if attn:
                    decay_rows()
                if ffn:
                    for r in range(EARLY, NR):
                        combine_block(r)
                    store(i - 1)
                for part, on in (("a", attn), ("f", ffn)):
                    if on:
                        settle(sp, "SP", part)

            iteration(0, True, False)
            with sp.Fori(1, SEQS) as i:
                iteration(i, True, True)
            iteration(SEQS, False, True)
            sp.wait_ge(sem["stored"], 16)

        @block.gpsimd
        def _(pool):
            nc.gpsimd.memset(mhalf[:], -0.5).then_inc(s_fill, 1)
            nc.gpsimd.memset(ones[:], 1.0).then_inc(s_fill, 1)
            nc.gpsimd.memset(one1[:], 1.0).then_inc(s_fill, 1)
            give(pool, "POOL")
            pool.wait_ge(s_fill, 3)

            own = Own(pool, "pool")

            def root(n, ts=slice(0, NT)):
                pool.wait_ge(sem["var_ready"], n)
                nc.gpsimd.tensor_tensor(rstd[:, ts], ve[:, ts], mhalf[:, ts], ALU.pow).then_inc(sem["rstd_ready"], 1)

            def root_of_mean(dst, sums, width, ts):
                own.do(nc.gpsimd.tensor_scalar(sums[:, ts], sums[:, ts], 1.0 / width, EPS, ALU.mult, ALU.add))
                nc.gpsimd.tensor_tensor(dst[:, ts], sums[:, ts], mhalf[:, ts], ALU.pow).then_inc(sem["rstd_ready"], 1)

            def root_q():
                pool.wait_ge(sem["ssq_ready"], 1)
                root_of_mean(rq, ssq, D, slice(0, NT))

            def root_y(s):
                pool.wait_ge(sem["ssy_ready"], s + 1)
                root_of_mean(ry, ssy, DI, slice(2 * s, 2 * s + 2))

            def mask(c):
                pool.wait_ge(sem["seg_ready"], c + 1)
                nc.gpsimd.affine_select(out=seg[:, c, :, :], in_=seg[:, c, :, :], compare_op=ALU.is_ge, fill=NEVER,
                                        base=0, pattern=[[0, HS], [1, P]], channel_multiplier=-1
                                        ).then_inc(sem["masked"], 1)

            def rope_sum(s):
                pool.wait_ge(sem["rope_ready"], s + 1)
                sl = slice(2 * s, 2 * s + 2)
                nc.gpsimd.tensor_tensor(qrot[:, sl, :], qrot[:, sl, :], tmp[:, sl, :], ALU.add
                                        ).then_inc(sem["qrot_ready"], 1)

            def decayed(c):
                pool.wait_ge(sem["xdt_ready"], c + 1)
                v = "p (h d) -> p h d"
                nc.gpsimd.tensor_tensor(
                    xdec[:, c % 2, :].rearrange(v, h=HS), xdt[:, c, :].rearrange(v, h=HS),
                    ed[:, c, :].unsqueeze(2).broadcast_to([P, HS, PD]), ALU.mult
                ).then_inc(sem["xdec_ready"], 1)

            def gated(c):
                pool.wait_ge(sem["z_ready"], c + 1)
                pool.wait_ge(sem["y_ready"], c + 1)
                own.do(nc.gpsimd.tensor_tensor(xD[:, c % 2, :], xD[:, c % 2, :], xdt[:, c, :], ALU.add))
                nc.gpsimd.tensor_tensor(zs[:, c, :], zs[:, c, :], xD[:, c % 2, :], ALU.mult
                                        ).then_inc(sem["yg_ready"], 1)

            def combine(j):
                r = j - SB
                pool.wait_ge(sem["h_half"], r + 1)
                pool.wait_ge(sem[f"cb_loaded{r % 2}"], 16 * (r // 2 + 1))
                nc.gpsimd.tensor_tensor(hid[:, j % 3, :], hid[:, j % 3, :], cb[:, r % 2, :], ALU.mult
                                        ).then_inc(sem["f_out_POOL"], 1)

            def final():
                pool.wait_ge(sem["fvar_ready"], 1)
                nc.gpsimd.tensor_tensor(frstd[:], fve[:], mhalf[:], ALU.pow).then_inc(sem["frstd_ready"], 1)
                pool.wait_ge(sem["fo_half"], 1)
                nc.gpsimd.tensor_tensor(fo[:], fo[:], x1[:], ALU.add).then_inc(sem["fo_ready"], 1)

            def iteration(a, f):
                h0, h1 = slice(0, 2), slice(2, 4)
                if a: root(1); rope_sum(0); rope_sum(1); root_q()
                if f: combine(4); combine(5)
                if a:
                    for c in range(NT):
                        mask(c)
                if f: combine(6)
                if a: decayed(0); decayed(1)
                if f: combine(7)
                if a: gated(0); decayed(2); gated(1); root_y(0)
                if f: combine(8)
                if a: root(2, h0); gated(2); gated(3); root_y(1)
                if f: combine(9)
                if a: root(3, h1); root(4, h0)
                if f: combine(10)
                if a: root(5, h1)
                if f: combine(11)
                if f: final()
                own.settle()
                if a: settle(pool, "POOL", "a")
                if f: settle(pool, "POOL", "f")

            iteration(True, False)
            with pool.Fori(1, SEQS):
                iteration(True, True)
            iteration(False, True)

        @block.scalar
        def _(act):
            own = Own(act, "act")
            act.wait_ge(s_fill, 3)
            act.wait_ge(s_const, NCONST)
            own.do(nc.scalar.activation(aneg[:], aneg[:], ACT.Exp))
            for n, (kind, k, w) in enumerate(STAGED):
                if kind == "z":
                    act.wait_ge(s_scaled, k + 1)
                else:
                    act.wait_ge(w_loaded[n], 32 if kind in "gu" else 16)
                for src, hi, lo in split_pieces(n):
                    ins = nc.scalar.copy(hi, src)
                ins.then_inc(s_high, 1)
            give(act, "ACT")

            def evac_xT(k):
                filled(act, "ACT", f"xT{k}")
                nc.scalar.copy(xT[:, k, :], bank(f"xT{k}")[:]).then_inc(sem["a_out_ACT"], 1)

            def square_q(s):
                act.wait_ge(sem["qrot_ready"], s + 1)
                for t, done in ((2 * s, "a_out_ACT" if s else None), (2 * s + 1, "ssq_ready" if s else "a_out_ACT")):
                    ins = nc.scalar.activation(zs[:, t, 0:D], qrot[:, t, :], ACT.Square, accum_out=ssq[:, t:t + 1])
                    if done:
                        ins.then_inc(sem[done], 1)

            def high(dst, name):
                filled(act, "ACT", name)
                nc.scalar.copy(dst, bank(name)[:]).then_inc(sem["hi_ready"], 1)

            def softplus():
                act.wait_ge(sem["na_ready"], 1)
                own.do(nc.scalar.activation(e1[:], na[:], ACT.Exp))
                nc.scalar.activation(l1[:], e1[:], ACT.Ln, bias=one1[:, 0:1]).then_inc(sem["ln_ready"], 1)

            def conv_first(b):
                filled(act, "ACT", f"xc{b}")
                nc.scalar.activation(xc[:, b, :], bank(f"xc{b}")[:], ACT.Identity, bias=cbv[:, b:b + 1],
                                     scale=cw[:, b, TAPS - 1:TAPS]).then_inc(sem["conv_first"], 1)

            def conv_silu(b, n):
                act.wait_ge(sem["conv_ready"], n)
                nc.scalar.activation(xc[:, b, :], xc[:, b, :], ACT.Silu).then_inc(sem["a_out_ACT"], 1)

            def decays():
                act.wait_ge(sem["acs_ready"], 1)
                nc.scalar.activation(ea[:].rearrange("p t h -> p (t h)"), acs[:, 0, :], ACT.Exp)
                nc.scalar.activation(el[:].rearrange("p t h -> p (t h)"), acs[:, 1, :], ACT.Exp)
                nc.scalar.activation(ed[:], ed[:], ACT.Exp).then_inc(sem["decay_ready"], 1)

            def exp_seg(c):
                act.wait_ge(sem["masked"], c + 1)
                nc.scalar.activation(seg[:, c, :, :], seg[:, c, :, :], ACT.Exp).then_inc(sem["exp_ready"], 1)

            def silu_z(j):
                filled(act, "ACT", f"z{j}")
                own.do(nc.scalar.activation(zs[:, j, :], bank(f"z{j}")[:], ACT.Silu))
                act.sem_inc(sem["a_out_ACT"], 1)
                act.sem_inc(sem["z_ready"], 1)

            def evac_B():
                filled(act, "ACT", "Bt")
                nc.scalar.copy(Btok[:].rearrange("p t n -> p (t n)"), bank("Bt")[:]).then_inc(sem["a_out_ACT"], 1)

            def evac_CB():
                filled(act, "ACT", "CB")
                nc.scalar.copy(CBs[:].rearrange("p t n -> p (t n)"), bank("CB")[:]).then_inc(sem["a_out_ACT"], 1)

            def evac_y(c):
                filled(act, "ACT", f"yT{c}")
                nc.scalar.copy(yT[:, c % 2, :, :].rearrange("p j n -> p (j n)"), bank(f"yT{c}")[:]
                               ).then_inc(sem["a_out_ACT"], 1)
                if c >= 2:
                    own.wait()
                ins = nc.scalar.activation(junk[c % 2], zs[:, c, :], ACT.Square, accum_out=ssy[:, c:c + 1])
                if c % 2:
                    ins.then_inc(sem["ssy_ready"], 1)
                else:
                    own.mark(ins)

            def save_x1():
                act.wait_ge(sem["x1_ready"], 1)
                act.wait_ge(sem["x1_free"], 1)
                nc.scalar.copy(x1[:], tmp[:]).then_inc(sem["tmp_free"], 1)

            def score_tanh():
                act.wait_ge(sem["logits_ready"], 1)
                nc.scalar.activation(th[:], msk[:], ACT.Tanh, scale=0.5).then_inc(sem["tanh_ready"], 1)

            def evac_cT():
                filled(act, "ACT", "cT")
                nc.scalar.copy(cT, bank("cT")[0:E, :]).then_inc(sem["cT_ready"], 1)

            def gate(j):
                act.wait_ge(sem["down_done"], now("down_done", j - 2) if j >= 3 else HB - 2 + j)
                filled(act, "ACT", f"G{j}")
                nc.scalar.activation(hid[:, j % 3, :], bank(f"G{j}")[:], ACT.Silu).then_inc(sem["silu_ready"], 1)

            def iteration(a, f):
                if f: save_x1(); score_tanh(); gate(0); gate(1)
                if a: evac_xT(0); evac_xT(1)
                if f: gate(2); gate(3); evac_cT()
                if a: square_q(0); square_q(1)
                if f: gate(4)
                if a: high(hTh[:, 0, :], "hT0"); high(hTh[:, 1, :], "hT1")
                if f: gate(5)
                if a:
                    nc.scalar.preload_act_table_set("natural_log_exp_and_others")
                    softplus()
                    conv_first(4); conv_first(5); conv_silu(4, 1)
                    conv_first(0); conv_silu(5, 2); conv_silu(0, 3)
                if f: gate(6)
                if a:
                    conv_first(1); conv_first(2); conv_silu(1, 4)
                    conv_first(3); conv_silu(2, 5); conv_silu(3, 6)
                    evac_B(); evac_CB()
                    nc.scalar.preload_act_table_set("natural_log_exp_and_others")
                    decays()
                    for c in range(NT):
                        exp_seg(c)
                    silu_z(0)
                if f: gate(7)
                if a: silu_z(1)
                if f: gate(8)
                if a: evac_y(0); silu_z(2); evac_y(1); silu_z(3)
                if f: gate(9)
                if a: evac_y(2); evac_y(3)
                if f: gate(10); gate(11)
                if a: high(fTh[:, 0, :], "fT0"); high(fTh[:, 1, :], "fT1")
                own.settle()
                if a: settle(act, "ACT", "a")
                if f: settle(act, "ACT", "f")

            own.settle()
            iteration(True, False)
            with act.Fori(1, SEQS):
                iteration(True, True)
            iteration(False, True)

        @block.vector
        def _(dve):
            own = Own(dve, "dve")
            V = nc.vector
            dve.wait_ge(s_const, NCONST)
            for k in range(NB):
                V.tensor_scalar(WO[:, k, :], WO[:, k, :], ngwc[:, k:k + 1], None, ALU.mult)
            for n, (kind, k, w) in enumerate(STAGED):
                if kind == "z":
                    dve.wait_ge(w_loaded[n], 16)
                    src = stage[:, n % 2, 0:w]
                    V.tensor_scalar(src, src, npwc[:, k:k + 1], None, ALU.mult).then_inc(s_scaled, 1)
            for n, (kind, k, w) in enumerate(STAGED):
                dve.wait_ge(s_high, n + 1)
                for src, hi, lo in split_pieces(n):
                    ins = V.tensor_tensor(lo, src, hi.bitcast(fp32), ALU.subtract)
                ins.then_inc(s_low, 1)
            own.do(V.tensor_scalar(aneg[:], aneg[:], -1.0, None, ALU.mult))
            own.settle()
            give(dve, "DVE")

            def moments(src, st, m, ts=range(NT)):
                for t in ts:
                    ins = V.bn_stats(st[:, t, :], src(t))
                own.do(ins)
                for t in ts:
                    ins = V.bn_aggr(m[:, t, :], st[:, t, :])
                own.do(ins)

            def send_variance(ts):
                sl = slice(ts[0], ts[-1] + 1)
                V.tensor_scalar(ve[:, sl], mv[:, sl, 1], EPS, None, ALU.add).then_inc(sem["var_ready"], 1)

            def normalise(dst, src, nth, ts=range(NT), done=None):
                dve.wait_ge(sem["rstd_ready"], nth)
                for t in ts:
                    ins = V.tensor_scalar(dst[:, t, :], src[:, t, :], mv[:, t, 0:1], rstd[:, t:t + 1],
                                          ALU.subtract, ALU.mult)
                if done:
                    ins.then_inc(sem[done], 1)
                else:
                    own.do(ins)

            def norm_x():
                dve.wait_ge(sem["x_loaded"], 16)
                moments(lambda t: xs[:, t, :], st6, mv)
                send_variance(range(NT))
                normalise(xn, xs, 1, done="xn_ready")

            def rope(s):
                filled(dve, "DVE", f"q{s}")
                if s == 0:
                    dve.wait_ge(sem["tmp_free"], 1)
                sl = slice(2 * s, 2 * s + 2)
                q = bank(f"q{s}")[:].rearrange("p (t h a f) -> p t h a f", t=2, a=2, f=HALF)
                o = tmp[:, sl, :].rearrange("p t (h a f) -> p t h a f", a=2, f=HALF)
                for a in range(2):
                    V.tensor_tensor(o[:, :, :, a, :], q[:, :, :, 1 - a, :],
                                    sin_t[:, sl, a, :].unsqueeze(2).broadcast_to([P, 2, HEADS, HALF]), ALU.mult)
                V.tensor_tensor(qrot[:, sl, :].rearrange("p t (g f) -> p t g f", f=HALF),
                                bank(f"q{s}")[:].rearrange("p (t g f) -> p t g f", t=2, f=HALF),
                                cos_t[:, sl, :].unsqueeze(2).broadcast_to([P, 2, 2 * HEADS, HALF]), ALU.mult
                                ).then_inc(sem["rope_ready"], 1)

            def norm_q():
                dve.wait_ge(sem["rstd_ready"], 2)
                for t in range(NT):
                    ins = V.tensor_scalar(xn[:, t, :], qrot[:, t, :], rq[:, t:t + 1], None, ALU.mult)
                ins.then_inc(sem["xn_ready"], 1)

            def low(lo, hi, name, n):
                dve.wait_ge(sem["hi_ready"], n)
                V.tensor_tensor(lo, bank(name)[:], hi.bitcast(fp32), ALU.subtract).then_inc(sem["a_out_DVE"], 1)

            def dt_bias_add():
                filled(dve, "DVE", "dt")
                parts = bank("dt")[:, 0:2 * NT * HS].rearrange("p (t a h) -> p t a h", t=NT, a=2)
                own.do(V.tensor_tensor(dr[:], parts[:, :, 0, :], dtb[:].unsqueeze(1).broadcast_to([P, NT, HS]), ALU.add))
                own.do(V.tensor_tensor(dr[:], dr[:], parts[:, :, 1, :], ALU.add))
                dve.sem_inc(sem["a_out_DVE"], 1)
                V.scalar_tensor_tensor(na[:], dr[:], -1.0, dr[:], ALU.mult, ALU.min).then_inc(sem["na_ready"], 1)

            def dt_finish():
                dve.wait_ge(sem["ln_ready"], 1)
                own.do(V.scalar_tensor_tensor(dt[:], dr[:], 0.0, l1[:], ALU.max, ALU.add))
                V.tensor_tensor(ad[:], dt[:], aneg[:].unsqueeze(1).broadcast_to([P, NT, HS]), ALU.mult
                                ).then_inc(sem["ad_ready"], 1)

            def conv(b, n):
                dve.wait_ge(sem["conv_first"], n)
                src = bank(f"xc{b}")
                for s in range(1, TAPS):
                    ins = V.scalar_tensor_tensor(xc[:, b, s:], src[:, 0:T - s], cw[:, b, TAPS - 1 - s:TAPS - s],
                                                 xc[:, b, s:], ALU.mult, ALU.add)
                    if s < TAPS - 1:
                        own.do(ins)
                ins.then_inc(sem["conv_ready"], 1)

            def evac_acs():
                filled(dve, "DVE", "acs")
                V.tensor_copy(acs[:].rearrange("p a n -> p (a n)"), bank("acs")[:, 0:2 * NT * HS])
                own.do(V.tensor_copy(acsT[:], bank("acs")[0:NT * HS, P:2 * P]))
                dve.sem_inc(sem["acsT_ready"], 1)
                dve.sem_inc(sem["a_out_DVE"], 1)
                V.tensor_tensor(ed[:].rearrange("p t h -> p (t h)"), acs[:, 1, :], acs[:, 0, :], ALU.subtract
                                ).then_inc(sem["acs_ready"], 1)

            def decay_exponents(c):
                if c == 0:
                    dve.wait_ge(sem["seg_loaded"], 16)
                V.tensor_tensor(seg[:, c, :, :], seg[:, c, :, :],
                                acs[:, 0, c * HS:(c + 1) * HS].unsqueeze(2).broadcast_to([P, HS, P]), ALU.subtract
                                ).then_inc(sem["seg_ready"], 1)

            def by_head(ap):
                return ap.rearrange("p (h d) -> p h d", h=HS)

            def along(small):
                return small.unsqueeze(2).broadcast_to([P, HS, PD])

            def times_dt(c):
                if c == 0:
                    dve.wait_ge(sem["decay_ready"], 1)
                filled(dve, "DVE", f"xt{c}")
                V.tensor_tensor(by_head(xD[:, c % 2, :]), by_head(bank(f"xt{c}")[:]), along(dbc[:]), ALU.mult)
                own.do(V.tensor_tensor(by_head(xdt[:, c, :]), by_head(bank(f"xt{c}")[:]), along(dt[:, c, :]), ALU.mult))
                dve.sem_inc(sem["a_out_DVE"], 1)
                if c < NT - 1:
                    dve.sem_inc(sem["xdt_ready"], 1)

            def decay_CB(c):
                dve.wait_ge(sem["exp_ready"], c + 1)
                V.tensor_tensor(seg[:, c, :, :], seg[:, c, :, :],
                                CBs[:, c, :].unsqueeze(1).broadcast_to([P, HS, P]), ALU.mult
                                ).then_inc(sem["m_ready"], 1)

            def state_part(c):
                filled(dve, "DVE", f"yo{c}")
                own.do(V.tensor_tensor(by_head(xT[:, c % 2, :]), by_head(bank(f"yo{c}")[:]), along(ea[:, c, :]), ALU.mult))
                dve.sem_inc(sem["a_out_DVE"], 1)

            def new_state(c):
                if c:
                    own.do(V.tensor_tensor(by_head(S[:]), by_head(S[:]), along(el[:, c, :]), ALU.mult))
                filled(dve, "DVE", f"st{c}")
                if c:
                    ins = V.tensor_tensor(S[:], S[:], bank(f"st{c}")[:], ALU.add)
                else:
                    ins = V.tensor_copy(S[:], bank("st0")[:])
                own.do(ins)
                dve.sem_inc(sem["a_out_DVE"], 1)

            def chunk_y(c):
                filled(dve, "DVE", f"yd{c}")
                if c:
                    ins = V.tensor_tensor(xdt[:, c, :], xT[:, c % 2, :], bank(f"yd{c}")[:], ALU.add)
                else:
                    ins = V.tensor_copy(xdt[:, c, :], bank(f"yd{c}")[:])
                own.do(ins)
                dve.sem_inc(sem["a_out_DVE"], 1)
                dve.sem_inc(sem["y_ready"], 1)

            def mixed_out(s, nth):
                ts = (2 * s, 2 * s + 1)
                filled(dve, "DVE", f"out{s}")
                dve.wait_ge(sem["rstd_ready"], nth)
                for t in ts:
                    ins = V.scalar_tensor_tensor(
                        tmp[:, t, :], bank(f"out{s}")[:, (t % 2) * D:(t % 2 + 1) * D], ry[:, t:t + 1],
                        qrot[:, t, :], ALU.mult, ALU.add)
                own.do(ins)
                dve.sem_inc(sem["a_out_DVE"], 1)
                moments(lambda t: tmp[:, t, :], st6, mv, ts)
                send_variance(ts)

            def form_x1(s, nth):
                ts = (2 * s, 2 * s + 1)
                normalise(tmp, tmp, nth, ts)
                sl = slice(2 * s, 2 * s + 2)
                own.do(V.tensor_tensor(tmp[:, sl, :], tmp[:, sl, :], xs[:, sl, :], ALU.add))
                if s:
                    dve.sem_inc(sem["x_free"], 1)
                    dve.sem_inc(sem["x1_ready"], 1)
                moments(lambda t: tmp[:, t, :], st6, mv, ts)
                send_variance(ts)

            def norm_x1(s, nth):
                normalise(xn, tmp, nth, (2 * s, 2 * s + 1), "xn_ready")

            def up(j):
                dve.wait_ge(sem["silu_ready"], j + 1)
                filled(dve, "DVE", f"U{j}")
                V.tensor_tensor(hid[:, j % 3, :], hid[:, j % 3, :], bank(f"U{j}")[:], ALU.mult
                                ).then_inc(sem["f_out_DVE" if j < SB else "h_half"], 1)

            te = "p (t e) -> p t e"

            def route_scores():
                filled(dve, "DVE", "logits")
                parts = bank("logits")[:, 0:2 * NT * E].rearrange("p (t a e) -> p t a e", t=NT, a=2)
                own.do(V.tensor_copy(msk[:].rearrange(te, t=NT), parts[:, :, 0, :]))
                own.do(V.tensor_tensor(msk[:].rearrange(te, t=NT), msk[:].rearrange(te, t=NT), parts[:, :, 1, :], ALU.add))
                dve.sem_inc(sem["f_out_DVE"], 1)
                dve.sem_inc(sem["logits_ready"], 1)
                dve.wait_ge(sem["tanh_ready"], 1)
                own.do(V.tensor_scalar(sc[:], th[:], 0.5, 0.5, ALU.mult, ALU.add))
                own.do(V.tensor_tensor(sbs[:].rearrange(te, t=NT), sc[:].rearrange(te, t=NT),
                                       ebias[:].unsqueeze(1).broadcast_to([P, NT, E]), ALU.add))

            def route_groups():
                pairs = sbs[:].rearrange("p (g a b) -> p g a b", a=2, b=2)
                V.tensor_tensor(hi2[:], pairs[:, :, :, 0], pairs[:, :, :, 1], ALU.max)
                own.do(V.tensor_tensor(lo2[:], pairs[:, :, :, 0], pairs[:, :, :, 1], ALU.min))
                V.tensor_tensor(m1[:], hi2[:, :, 0], hi2[:, :, 1], ALU.max)
                V.tensor_tensor(mn[:], hi2[:, :, 0], hi2[:, :, 1], ALU.min)
                own.do(V.tensor_tensor(rk[:], lo2[:, :, 0], lo2[:, :, 1], ALU.max))
                own.do(V.tensor_tensor(mn[:], mn[:], rk[:], ALU.max))
                own.do(V.tensor_tensor(gs[:], m1[:], mn[:], ALU.add))
                g4 = gs[:].rearrange("p (t g) -> p t g", t=NT)
                theirs = g4.unsqueeze(2).broadcast_to([P, NT, GROUPS, GROUPS])
                ours = g4.unsqueeze(3).broadcast_to([P, NT, GROUPS, GROUPS])
                v4 = "p (t g j) -> p t g j"
                GT, EQ = (b[:].rearrange(v4, t=NT, g=GROUPS) for b in (gt, eq))
                V.tensor_tensor(GT, theirs, ours, ALU.is_gt)
                own.do(V.tensor_tensor(EQ, theirs, ours, ALU.is_equal))
                own.do(V.tensor_tensor(EQ, EQ, tri[:].unsqueeze(1).broadcast_to([P, NT, GROUPS, GROUPS]), ALU.mult))
                own.do(V.tensor_tensor(gt[:], gt[:], eq[:], ALU.add))
                own.do(V.reduce_sum(rk[:], gt[:].rearrange("p (g j) -> p g j", j=GROUPS), AX.X))
                own.do(V.tensor_scalar(rk[:], rk[:], float(TOPG), NEVER, ALU.is_ge, ALU.mult))
                own.do(V.tensor_tensor(msk[:].rearrange("p (g j) -> p g j", j=GROUPS),
                                       sbs[:].rearrange("p (g j) -> p g j", j=GROUPS),
                                       rk[:].unsqueeze(2).broadcast_to([P, NT * GROUPS, GROUPS]), ALU.add))

            def route_experts():
                for t in range(NT):
                    ins = V.max(v8[:, t, :], msk[:, t * E:(t + 1) * E])
                own.do(ins)
                m3 = msk[:].rearrange(te, t=NT)
                fourth = v8[:, :, TOPK - 1:TOPK].broadcast_to([P, NT, E])
                V.tensor_tensor(gt[:].rearrange(te, t=NT), m3, fourth, ALU.is_gt)
                own.do(V.tensor_tensor(eq[:].rearrange(te, t=NT), m3, fourth, ALU.is_equal))
                V.reduce_sum(ws[:], gt[:].rearrange(te, t=NT), AX.X)
                own.do(V.tensor_tensor_scan(pre[:], reset[:], eq[:], 0.0, ALU.mult, ALU.add))
                p3 = pre[:].rearrange(te, t=NT)
                own.do(V.tensor_tensor(p3, p3, ws[:].unsqueeze(2).broadcast_to([P, NT, E]), ALU.add))
                own.do(V.scalar_tensor_tensor(eq[:], pre[:], float(TOPK), eq[:], ALU.is_le, ALU.mult))
                own.do(V.tensor_tensor(gt[:], gt[:], eq[:], ALU.add))
                own.do(V.tensor_tensor(gt[:], gt[:], sc[:], ALU.mult))
                own.do(V.reduce_sum(ws[:], gt[:].rearrange(te, t=NT), AX.X))
                own.do(V.tensor_scalar(ws[:], ws[:], 1e-20, None, ALU.add))
                own.do(V.reciprocal(ws[:], ws[:]))
                V.tensor_tensor(gt[:].rearrange(te, t=NT), gt[:].rearrange(te, t=NT),
                                ws[:].unsqueeze(2).broadcast_to([P, NT, E]), ALU.mult).then_inc(sem["c_ready"], 1)

            def final():
                dve.wait_ge(sem["acc_ready"], 1)
                dve.sem_inc(sem["down_done"], 1)
                moments(lambda t: acc[t // 2][:, (t % 2) * D:(t % 2 + 1) * D], fst6, fmv)
                V.tensor_scalar(fve[:], fmv[:, :, 1], EPS, None, ALU.add).then_inc(sem["fvar_ready"], 1)
                dve.wait_ge(sem["fo_free"], 1)
                dve.wait_ge(sem["frstd_ready"], 1)
                for t in range(NT):
                    ins = V.tensor_scalar(fo[:, t, :], acc[t // 2][:, (t % 2) * D:(t % 2 + 1) * D], fmv[:, t, 0:1],
                                          frstd[:, t:t + 1], ALU.subtract, ALU.mult)
                own.do(ins)
                dve.sem_inc(sem["acc_free"], 1)
                dve.sem_inc(sem["fo_half"], 1)

            def iteration(a, f):
                if f: route_scores(); up(0)
                if a: norm_x()
                if f: route_groups(); up(1); route_experts(); up(2)
                if a: rope(0); rope(1)
                if f: up(3); up(4)
                if a: norm_q()
                if a: low(hTl[:, 0, :], hTh[:, 0, :], "hT0", 1); low(hTl[:, 1, :], hTh[:, 1, :], "hT1", 2)
                if f: up(5)
                if a: dt_bias_add(); conv(4, 1); dt_finish(); conv(5, 2); evac_acs(); conv(0, 3)
                if f: up(6)
                if a:
                    conv(1, 4); conv(2, 5)
                    decay_exponents(0); decay_exponents(1)
                    conv(3, 6)
                    decay_exponents(2); decay_exponents(3)
                    times_dt(0); decay_CB(0); new_state(0)
                if f: up(7)
                if a: decay_CB(1); chunk_y(0); times_dt(1); state_part(1); new_state(1); decay_CB(2)
                if f: up(8)
                if a:
                    chunk_y(1); times_dt(2); state_part(2); new_state(2); decay_CB(3); chunk_y(2)
                    times_dt(3)
                    mixed_out(0, 3)
                    state_part(3); chunk_y(3)
                if f: up(9)
                if a: mixed_out(1, 5); form_x1(0, 4)
                if f: up(10)
                if a: form_x1(1, 6); norm_x1(0, 7); norm_x1(1, 8)
                if f: up(11)
                if a: low(fTl[:, 0, :], fTh[:, 0, :], "fT0", 3); low(fTl[:, 1, :], fTh[:, 1, :], "fT1", 4)
                if f: final()
                own.settle()
                if a: settle(dve, "DVE", "a")
                if f: settle(dve, "DVE", "f")

            iteration(True, False)
            with dve.Fori(1, SEQS):
                iteration(True, True)
            iteration(False, True)

        @block.tensor
        def _(pe):
            pe.wait_ge(s_low, len(STAGED))
            pe.wait_ge(s_fill, 3)
            give(pe, "PE")

            def out_of(name):
                part, n = WHERE[name]
                if SLOTS[part][n][2] == "with U":
                    n += 1
                who = SLOTS[part][n][2]
                return f"{part}_out_{who}", count(part, 2, who, n)

            def slot(name):
                part, n = WHERE[name]
                if n >= 3:
                    s, k = out_of(SLOTS[part][n - 3][0])
                    pe.wait_ge(sem[s], now(s, k))
                else:
                    s, k = out_of(SLOTS[part][n - 3][0])
                    pe.wait_ge(sem[s], k)
                return bank(name)

            def read_out(name):
                s, k = out_of(name)
                pe.wait_ge(sem[s], now(s, k))

            def fill(name, ins):
                part, n = WHERE[name]
                ins.then_inc(sem[f"{part}_for_{SLOTS[part][n][1]}"], 1)

            def split_mm(dst, parts, last=True):
                n, total = 0, 3 * len(parts)
                for ah, al, bh, bl in parts:
                    for l, r in ((ah, bh), (ah, bl), (al, bh)):
                        ins = nc.tensor.matmul(dst, l, r, start=n == 0, stop=n == total - 1)
                        n += 1
                return ins

            def transposes(name, src, n=NT):
                b = slot(name)
                for t in range(n):
                    ins = nc.tensor.transpose(b[:, t * P:(t + 1) * P], src(t), ident[:])
                return ins

            def x_transposes(names, nth):
                pe.wait_ge(sem["xn_ready"], nth)
                for k, name in enumerate(names):
                    fill(name, transposes(name, lambda t: xn[:, t, k * P:(k + 1) * P]))

            def project_q(s):
                b = slot(f"q{s}")
                read_out("xT1")
                for t in range(2):
                    for k in range(KD):
                        ins = nc.tensor.matmul(b[:, t * D:(t + 1) * D], xT[:, k, (2 * s + t) * P:(2 * s + t + 1) * P],
                                               WQ[:, k, :], start=k == 0, stop=k == KD - 1)
                fill(f"q{s}", ins)

            def narrow(b, hi, lo, w, n):
                for t in range(NT):
                    tk = slice(t * P, (t + 1) * P)
                    for k in range(KD):
                        nc.tensor.matmul(b[:, 2 * n * t:2 * n * (t + 1)], hi[:, k, tk], w[:, k, :],
                                         start=k == 0, stop=False, skip_group_check=True)
                        ins = nc.tensor.matmul(b[:, 2 * n * t:2 * n * t + n], lo[:, k, tk], w[:, k, 0:n],
                                               start=False, stop=k == KD - 1, skip_group_check=True)
                return ins

            def project_dt():
                b = slot("dt")
                read_out("hT1")
                fill("dt", narrow(b, hTh, hTl, DT, HS))

            def project(name, col):
                b = slot(name)
                cs = slice(col, col + P)
                fill(name, split_mm(b[:], [(ZH[:, k, cs], ZL[:, k, cs], hTh[:, k, :], hTl[:, k, :]) for k in range(KD)]))

            def project_x(b):
                project(f"xc{b}", DI + b * P)

            def cumulate():
                b = slot("acs")
                pe.wait_ge(sem["ad_ready"], 1)
                rhs = ad[:].rearrange("p t h -> p (t h)")
                n = NT * HS
                nc.tensor.matmul(b[:, 0:n], upper[:], rhs, start=True, stop=True)
                nc.tensor.matmul(b[:, n:2 * n], ones[:], rhs, start=True, stop=True)
                fill("acs", nc.tensor.matmul(b[0:n, P:2 * P], rhs, upper[:], start=True, stop=True))

            def project_z(c):
                tk = slice(c * P, (c + 1) * P)
                fill(f"z{c}", split_mm(slot(f"z{c}")[:], [(hTh[:, k, tk], hTl[:, k, tk], ZH[:, k, 0:DI], ZL[:, k, 0:DI])
                                                          for k in range(KD)]))

            def B_by_token():
                read_out("xc4")
                fill("Bt", transposes("Bt", lambda t: xc[:, 4, t * P:(t + 1) * P]))

            def CB():
                b = slot("CB")
                read_out("xc5")
                for t in range(NT):
                    tk = slice(t * P, (t + 1) * P)
                    ins = nc.tensor.matmul(b[:, tk], xc[:, 4, tk], xc[:, 5, tk], start=True, stop=True)
                fill("CB", ins)

            def x_by_token(c):
                read_out("xc3")
                fill(f"xt{c}", transposes(f"xt{c}", lambda j: xc[:, j, c * P:(c + 1) * P], NB))

            def from_state(c):
                b = slot(f"yo{c}")
                read_out(f"st{c - 1}")
                fill(f"yo{c}", nc.tensor.matmul(b[:], xc[:, 5, c * P:(c + 1) * P], S[:], start=True, stop=True))

            def state(c):
                b = slot(f"st{c}")
                pe.wait_ge(sem["xdec_ready"], c + 1)
                fill(f"st{c}", nc.tensor.matmul(b[:], Btok[:, c, :], xdec[:, c % 2, :], start=True, stop=True))

            def diagonal(c):
                b = slot(f"yd{c}")
                pe.wait_ge(sem["m_ready"], c + 1)
                for h in range(HS):
                    hs = slice(h * PD, (h + 1) * PD)
                    ins = nc.tensor.matmul(b[:, hs], seg[:, c, h, :], xdt[:, c, hs], start=True, stop=True)
                fill(f"yd{c}", ins)

            def y_by_channel(c):
                b = slot(f"yT{c}")
                pe.wait_ge(sem["yg_ready"], c + 1)
                for j in range(NB):
                    ins = nc.tensor.transpose(b[:, j * P:(j + 1) * P], zs[:, c, j * P:(j + 1) * P], ident[:])
                    if j == 0 and c == NT - 1:
                        ins.then_inc(sem["seg_free"], 1)
                fill(f"yT{c}", ins)

            def project_out(s):
                b = slot(f"out{s}")
                for t in range(2):
                    read_out(f"yT{2 * s + t}")
                    for j in range(NB):
                        ins = nc.tensor.matmul(b[:, t * D:(t + 1) * D], yT[:, t, j, :], WO[:, j, :],
                                               start=j == 0, stop=j == NB - 1)
                fill(f"out{s}", ins)

            def logits():
                b = slot("logits")
                pe.wait_ge(sem["a_out_DVE"], SEM["a_out_DVE"][2])
                fill("logits", narrow(b, fTh, fTl, R, E))

            def combine_by_expert():
                b = slot("cT")
                pe.wait_ge(sem["c_ready"], 1)
                for t in range(NT):
                    ins = nc.tensor.transpose(b[0:E, t * P:(t + 1) * P], gt[:, t * E:(t + 1) * E], ident[:])
                fill("cT", ins)

            def hidden(name, hi, lo, j):
                b = slot(name)
                cs = slice(j * P, (j + 1) * P)
                fill(name, split_mm(b[:], [(hi[:, k, cs], lo[:, k, cs], fTh[:, k, :], fTl[:, k, :]) for k in range(KD)]))

            def down(j):
                read_out(f"U{j}")
                if j == 0:
                    pe.wait_ge(sem["acc_free"], 1)
                for t in range(NT):
                    ins = nc.tensor.matmul(acc[t // 2][:, (t % 2) * D:(t % 2 + 1) * D],
                                           hid[:, j % 3, t * P:(t + 1) * P], WD[:, j, :],
                                           start=j == 0 and t % 2 == 0, stop=j == HB - 1, skip_group_check=True)
                    if t == 0 and j >= SB:
                        ins.then_inc(sem["cb_free"], 1)
                ins.then_inc(sem["acc_ready" if j == HB - 1 else "down_done"], 1)

            def block_of(j):
                hidden(f"G{j}", GH, GL, j)
                if j >= 2:
                    down(j - 2)
                hidden(f"U{j}", UH, UL, j)

            def iteration(a, f):
                if f: logits(); block_of(0); block_of(1)
                if a: x_transposes(("xT0", "xT1"), 1)
                if f: block_of(2)
                if a: project_q(0); project_q(1)
                if f: block_of(3); combine_by_expert(); block_of(4)
                if a: x_transposes(("hT0", "hT1"), 2)
                if f: block_of(5)
                if a: project_dt(); project_x(4); project_x(5); project_x(0); cumulate()
                if f: block_of(6)
                if a:
                    project_x(1); project_x(2); project_x(3)
                    B_by_token(); CB()
                    x_by_token(0); state(0); project_z(0); diagonal(0)
                if f: block_of(7)
                if a: x_by_token(1); from_state(1); state(1); project_z(1); diagonal(1)
                if f: block_of(8)
                if a:
                    y_by_channel(0); x_by_token(2)
                    from_state(2); state(2); project_z(2); diagonal(2)
                    y_by_channel(1); x_by_token(3); project_out(0)
                    from_state(3); project_z(3); diagonal(3)
                if f: block_of(9)
                if a: y_by_channel(2); y_by_channel(3); project_out(1)
                if f: block_of(10); block_of(11); down(10); down(11)
                if a: x_transposes(("fT0", "fT1"), 4)
                if a: settle(pe, "PE", "a")
                if f: settle(pe, "PE", "f")

            iteration(True, False)
            with pe.Fori(1, SEQS):
                iteration(True, True)
            iteration(False, True)


def kernel(**inputs):
    import numpy as np
    import concourse.bacc as bacc
    from concourse.bass_utils import run_bass_kernel_spmd as run

    g = {k: np.asarray(v) for k, v in inputs.items()}

    def t(a):
        return np.ascontiguousarray(a.T)

    def by_expert(w):
        return np.ascontiguousarray(w.transpose(1, 0, 2).reshape(D, E * EH))

    angle = np.arange(T, dtype=np.float32)[:, None] * (
        np.float32(1.0) / np.float32(10000.0) ** (np.arange(0, 2 * HALF, 2, dtype=np.float32) / np.float32(2 * HALF))
    )[None, :]
    angle = angle.astype(np.float32)
    sin = np.sin(angle).astype(np.float32)
    arrays = {
        "x": g["L0_attn_x"],
        "wq_t": t(g["L0_attn_W_in"][:D]),
        "wzx_t": t(g["L0_attn_W_zxbcdt"]),
        "conv_w": g["L0_attn_conv_w"], "conv_b": g["L0_attn_conv_b"], "dt_bias": g["L0_attn_dt_bias"],
        "a_log": g["L0_attn_A_log"], "d_param": g["L0_attn_D_param"],
        "npw": g["L0_attn_norm_pre_w"], "ngw": g["L0_attn_norm_gated_w"],
        "wo_t": t(g["L0_attn_W_out"]),
        "router_t": t(g["L0_ffn_router_w"]), "cbias": g["L0_ffn_correction_bias"],
        "wg_t": by_expert(g["L0_ffn_gate_w"]), "wu_t": by_expert(g["L0_ffn_up_w"]),
        "wd": g["L0_ffn_down_w"].reshape(E * EH, D),
        "swg_t": t(g["L0_ffn_shared_gate_w"]), "swu_t": t(g["L0_ffn_shared_up_w"]),
        "swd_t": t(g["L0_ffn_shared_down_w"]),
        "c_ident": np.eye(P, dtype=np.float32),
        "c_upper": np.triu(np.ones((P, P), np.float32)),
        "c_cos": np.cos(angle).astype(np.float32),
        "c_sin": np.concatenate([-sin, sin], axis=1),
        "c_reset": (np.arange(NT * E) % E != 0).astype(np.float32),
        "c_tri": np.tril(np.ones((GROUPS, GROUPS), np.float32), -1),
    }
    nc = bacc.Bacc("TRN2", target_bir_lowering=False, num_devices=1)
    in_map, args = {}, []
    for name, a in arrays.items():
        a = np.ascontiguousarray(a)
        in_map[f"in_{name}"] = a
        args.append(nc.dram_tensor(f"in_{name}", a.shape, mybir.dt.from_np(a.dtype), kind="ExternalInput").ap())
    args.append(nc.dram_tensor("out", (SEQS, T, D), mybir.dt.float32, kind="ExternalOutput").ap())
    build(nc, *args)
    return run(nc, [in_map], core_ids=[0]).results[0]["out"]
```

```python
import concourse.bass as bass
from concourse import mybir
from contextlib import ExitStack

SEQS, T, D = 32, 512, 256
HEADS, HALF = 16, 8
DI, HS, PD, NS = 512, 8, 64, 128
CONV, TAPS = DI + 2 * NS, 4
DT0 = 2 * DI + 2 * NS
E, EH, SH = 16, 64, 512
GROUPS, TOPK, TOPG = 4, 4, 2
P = 128
NT = T // P
KD = D // P
NB = DI // P
CB_ = CONV // P
HB = (SH + E * EH) // P
SB = SH // P
EPS = 1e-5
NEVER = -3e38


def build(nc, x, wq_t, wzx_t, conv_w, conv_b, dt_bias, a_log, d_param, npw, ngw, wo_t,
          router_t, cbias, wg_t, wu_t, wd, swg_t, swu_t, swd_t,
          c_ident, c_upper, c_cos, c_sin, c_reset, c_tri, out):
    fp32, f32r = mybir.dt.float32, mybir.dt.float32r
    ALU, ACT, AX = mybir.AluOpType, mybir.ActivationFunctionType, mybir.AxisListType

    ctx = ExitStack()
    with ctx:
        def sb(name, shape, dt=fp32):
            return ctx.enter_context(nc.sbuf_tensor(name, shape, dt))

        def low_part(name, shape):
            offset = nc.sbuf_base
            low = sb(name, shape, f32r)
            return low, nc.alloc_sbuf_tensor_at(name + "_loaded", shape, fp32, offset=offset)

        WQ = sb("WQ", [P, KD, D])
        ZH, (ZL, ZW) = sb("ZH", [P, KD, DT0], f32r), low_part("ZL", [P, KD, DT0])
        DT, DTW = low_part("DT", [P, KD, 2 * HS])
        R, RW = low_part("R", [P, KD, 2 * E])
        WO = sb("WO", [P, NB, D])
        GH, (GL, GW) = sb("GH", [P, KD, HB * P], f32r), low_part("GL", [P, KD, HB * P])
        UH, (UL, UW) = sb("UH", [P, KD, HB * P], f32r), low_part("UL", [P, KD, HB * P])
        WDH, (WDL, WDW) = sb("WDH", [P, HB, D], f32r), low_part("WDL", [P, HB, D])
        ident, upper, ones = sb("ident", [P, P]), sb("upper", [P, P]), sb("ones", [P, P])
        cos_t, sin_t = sb("cos_t", [P, NT, HALF]), sb("sin_t", [P, NT, 2, HALF])
        reset, tri = sb("reset", [P, NT * E]), sb("tri", [P, GROUPS, GROUPS])
        cw, cbv = sb("cw", [P, CB_, TAPS]), sb("cbv", [P, CB_])
        dtb, aneg, dbc = sb("dtb", [P, HS]), sb("aneg", [P, HS]), sb("dbc", [P, HS])
        ebias, npwc, ngwc = sb("ebias", [P, E]), sb("npwc", [P, KD]), sb("ngwc", [P, NB])
        mhalf, one1 = sb("mhalf", [P, NT]), sb("one1", [P, 1])
        xs = sb("xs", [P, NT, D])
        xn = sb("xn", [P, NT, D])
        xT = sb("xT", [P, KD, T])
        qrot, tmp = sb("qrot", [P, NT, D]), sb("tmp", [P, NT, D])
        hTh, hTl = sb("hTh", [P, KD, T], f32r), sb("hTl", [P, KD, T], f32r)
        xc = sb("xc", [P, CB_, T])
        zs = sb("zs", [P, NT, DI])
        yT = sb("yT", [P, 2, NB, P])
        Btok = sb("Btok", [P, NT, NS])
        xdt = sb("xdt", [P, 2, DI])
        xdec = sb("xdec", [P, 2, DI])
        seg = sb("seg", [P, 2, HS, P])
        S = sb("S", [P, DI])
        CBs = sb("CBs", [P, NT, P])
        acsT = sb("acsT", [NT * HS, P])
        st6 = sb("st6", [P, NT, 6])
        mv = sb("mv", [P, NT, 2])
        ve, rstd = sb("ve", [P, NT]), sb("rstd", [P, NT])
        ssq, rq = sb("ssq", [P, NT]), sb("rq", [P, NT])
        ssy, ry = sb("ssy", [P, NT]), sb("ry", [P, NT])
        dr, na, e1, l1 = (sb(n, [P, NT, HS]) for n in ("dr", "na", "e1", "l1"))
        dt, ad = sb("dt", [P, NT, HS]), sb("ad", [P, NT, HS])
        acs = sb("acs", [P, 2, NT * HS])
        ea, ed, el = (sb(n, [P, NT, HS]) for n in ("ea", "ed", "el"))
        x1 = sb("x1", [P, NT, D])
        fTh, fTl = sb("fTh", [P, KD, T], f32r), sb("fTl", [P, KD, T], f32r)
        hid = sb("hid", [P, 2, T])
        hidH, hidL = sb("hidH", [P, 2, T], f32r), sb("hidL", [P, 2, T], f32r)
        cb = sb("cb", [P, 2, T])
        cT = cb[0:E, 0, :]
        fst6, fmv = sb("fst6", [P, NT, 6]), sb("fmv", [P, NT, 2])
        fve, frstd, fnm = sb("fve", [P, NT]), sb("frstd", [P, NT]), sb("fnm", [P, NT])
        th, sc, sbs, msk = (sb(n, [P, NT * E]) for n in ("th", "sc", "sbs", "msk"))
        gt, eq, pre = (sb(n, [P, NT * E]) for n in ("gt", "eq", "pre"))
        hi2, lo2 = sb("hi2", [P, NT * GROUPS, 2]), sb("lo2", [P, NT * GROUPS, 2])
        m1, mn, gs, rk = (sb(n, [P, NT * GROUPS]) for n in ("m1", "mn", "gs", "rk"))
        v8, ws = sb("v8", [P, NT, 8]), sb("ws", [P, NT])

        xD = xn[:].rearrange("p (a b) d -> p a (b d)", a=2)
        junk = (xc[:, 4, :], xdec[:, 1, :])

        acs_row = nc.dram_tensor("acs_row", (NT * HS, P), fp32, kind="Internal").ap()
        c_row = nc.dram_tensor("c_row", (E, T), fp32, kind="Internal").ap()

        def rows(ap, dims, offset=0):
            return bass.AP(tensor=ap.tensor, offset=ap.offset + offset, ap=dims)

        apb = [ctx.enter_context(nc.psum_tensor(f"apb{n}", [P, T], fp32)) for n in range(3)]
        fpb = [ctx.enter_context(nc.psum_tensor(f"fpb{n}", [P, T], fp32)) for n in range(3)]
        acc = [ctx.enter_context(nc.psum_tensor(f"acc{n}", [P, T], fp32)) for n in range(2)]

        A_SLOTS = [("xT0", "ACT", "ACT"), ("xT1", "ACT", "ACT"), ("q0", "DVE", "ACT"), ("q1", "DVE", "ACT"),
                   ("hT0", "ACT", "DVE"), ("hT1", "ACT", "DVE"), ("dt", "DVE", "DVE"), ("xc4", "ACT", "ACT"),
                   ("xc5", "ACT", "ACT"), ("acs", "DVE", "DVE"), ("xc0", "ACT", "ACT"), ("xc1", "ACT", "ACT"),
                   ("xc2", "ACT", "ACT"), ("xc3", "ACT", "ACT"), ("z0", "ACT", "ACT"), ("Bt", "ACT", "ACT"),
                   ("CB", "ACT", "ACT"), ("xt0", "DVE", "DVE"), ("xt1", "DVE", "DVE"), ("st0", "DVE", "DVE"),
                   ("yd0", "DVE", "DVE"), ("z1", "ACT", "ACT"), ("yo1", "DVE", "DVE"), ("st1", "DVE", "DVE"),
                   ("yd1", "DVE", "DVE"), ("yT0", "ACT", "ACT"), ("xt2", "DVE", "DVE"), ("yo2", "DVE", "DVE"),
                   ("z2", "ACT", "ACT"), ("st2", "DVE", "DVE"), ("yd2", "DVE", "DVE"), ("yT1", "ACT", "ACT"),
                   ("xt3", "DVE", "DVE"), ("yo3", "DVE", "DVE"), ("z3", "ACT", "ACT"), ("yd3", "DVE", "DVE"),
                   ("out0", "DVE", "DVE"), ("yT2", "ACT", "ACT"), ("yT3", "ACT", "ACT"),
                   ("out1", "DVE", "DVE"), ("fT0", "ACT", "DVE"), ("fT1", "ACT", "DVE"),
                   ("logits", "DVE", "DVE")]
        F_SLOTS = []
        for j in range(HB):
            F_SLOTS += [(f"G{j}", "ACT", "with U"), (f"U{j}", "DVE", "DVE")]
            F_SLOTS += [("cT", "ACT", "SP")] * (j == SB - 1)
        SLOTS, BANKS = {"a": A_SLOTS, "f": F_SLOTS}, {"a": apb, "f": fpb}
        WHERE = {s[0]: (part, n) for part in SLOTS for n, s in enumerate(SLOTS[part])}

        def count(part, field, engine, upto=None):
            slots = SLOTS[part]
            return sum(s[field] == engine for s in slots[:len(slots) if upto is None else upto + 1])

        def bank(name):
            part, n = WHERE[name]
            return BANKS[part][n % 3]

        NR = HB - SB
        SEM = {
            "x_free": ("SP", "a", 1, False), "acsT_ready": ("SP", "a", 1, False),
            "seg_free": ("SP", "a", NT, True), "acs_stored": ("SP", "a", 16, False),
            "cT_ready": ("SP", "f", 1, False), "c_stored": ("SP", "f", 16, False),
            "cb_free": ("SP", "f", NR, True), "result_ready": ("SP", "f", 1, False),
            "stored": ("SP", "f", 16, True),
            "x_loaded": ("DVE", "a", 16, False), "rstd_ready": ("DVE", "a", 8, False), "hi_ready": ("DVE", "a", 4, False),
            "conv_first": ("DVE", "a", CB_, False), "ln_ready": ("DVE", "a", 1, False),
            "seg_loaded": ("DVE", "a", 16, False), "seg_loaded2": ("DVE", "a", 16, False),
            "seg_loaded3": ("DVE", "a", 16, False), "xdt_free": ("DVE", "a", 2, False),
            "exp_ready": ("DVE", "a", NT, False),
            "decay_ready": ("DVE", "a", 1, False), "tmp_free": ("DVE", "a", 1, True),
            "a_for_DVE": ("DVE", "a", count("a", 1, "DVE"), False),
            "f_for_DVE": ("DVE", "f", count("f", 1, "DVE"), False),
            "silu_ready": ("DVE", "f", HB, False), "tanh_ready": ("DVE", "a", 1, False),
            "acc_ready": ("DVE", "f", 1, False),
            "a_for_ACT": ("ACT", "a", count("a", 1, "ACT"), False),
            "qrot_ready": ("ACT", "a", 2, False), "na_ready": ("ACT", "a", 1, False),
            "conv_ready": ("ACT", "a", CB_, False), "acs_ready": ("ACT", "a", 1, False),
            "masked": ("ACT", "a", NT, False),
            "f_for_ACT": ("ACT", "f", count("f", 1, "ACT"), False),
            "down_done": ("ACT", "f", HB, True), "hid_free": ("ACT", "f", HB, True),
            "shared_ready": ("ACT", "f", SB, False), "routed_ready": ("ACT", "f", NR, False),
            "x1_ready": ("ACT", "f", 1, False), "x1_free": ("ACT", "f", 1, False), "frstd_ready": ("ACT", "f", 1, False),
            "xT_free": ("ACT", "a", 1, True), "logits_ready": ("ACT", "a", 1, False),
            "var_ready": ("POOL", "a", 5, False), "rope_ready": ("POOL", "a", 2, False),
            "ssq_ready": ("POOL", "a", 1, False), "ssy_ready": ("POOL", "a", 2, False),
            "seg_ready": ("POOL", "a", NT, False),
            "xdt_ready": ("POOL", "a", NT - 1, False), "y_ready": ("POOL", "a", NT, False),
            "z_ready": ("POOL", "a", NT, False),
            "fvar_ready": ("POOL", "f", 1, False), "product_ready": ("POOL", "f", NR, False),
            "cb_loaded0": ("POOL", "f", 16 * NR // 2, False),
            "cb_loaded1": ("POOL", "f", 16 * NR // 2, False),
            "hidden_high": ("POOL", "f", HB, False), "normalised": ("POOL", "f", 1, False),
            "a_out_ACT": ("PE", "a", count("a", 2, "ACT"), True),
            "a_out_DVE": ("PE", "a", count("a", 2, "DVE"), True),
            "xn_ready": ("PE", "a", 4, False), "ad_ready": ("PE", "a", 1, False),
            "m_ready": ("PE", "a", NT, False), "yg_ready": ("PE", "a", NT, False),
            "xdec_ready": ("PE", "a", NT - 1, False),
            "f_out_SP": ("PE", "f", count("f", 2, "SP"), True),
            "f_out_DVE": ("PE", "f", count("f", 2, "DVE"), True),
            "hidden_split": ("PE", "f", HB, False),
            "c_ready": ("PE", "f", 1, False), "acc_free": ("PE", "f", 1, True),
        }
        sem = {n: ctx.enter_context(nc.semaphore(n)) for n in SEM}
        w_loaded = [ctx.enter_context(nc.semaphore(f"w_loaded{n}")) for n in range(3 * KD + 1 + 3)]
        s_const = ctx.enter_context(nc.semaphore("consts_loaded"))
        s_late = ctx.enter_context(nc.semaphore("late_weights_loaded"))
        s_scaled = ctx.enter_context(nc.semaphore("w_out_scaled"))
        s_aexp = ctx.enter_context(nc.semaphore("a_exponential"))
        s_high = ctx.enter_context(nc.semaphore("w_high"))
        s_low = ctx.enter_context(nc.semaphore("w_low"))
        s_fill = ctx.enter_context(nc.semaphore("consts_filled"))
        s_own = {n: ctx.enter_context(nc.semaphore(f"{n}_own")) for n in ("dve", "act", "pool")}

        def give(eng, who):
            for n, (waiter, _, k, first) in SEM.items():
                if waiter == who and first:
                    eng.sem_inc(sem[n], k)

        def settle(eng, who, part):
            for n, (waiter, p_, k, _) in SEM.items():
                if waiter == who and p_ == part:
                    eng.sem_inc(sem[n], -k)

        def now(name, n=1):
            return SEM[name][2] + n

        def filled(eng, who, name):
            part, n = WHERE[name]
            eng.wait_ge(sem[f"{part}_for_{who}"], count(part, 1, who, n))

        class Own:

            def __init__(self, eng, name):
                self.eng, self.sem, self.n = eng, s_own[name], 0

            def mark(self, ins):
                self.n += 1
                ins.then_inc(self.sem, 1)

            def wait(self):
                if self.n:
                    self.eng.wait_ge(self.sem, self.n)

            def do(self, ins):
                self.mark(ins)
                self.wait()

            def settle(self):
                if self.n:
                    self.wait()
                    self.eng.sem_inc(self.sem, -self.n)
                self.n = 0

        SPLIT = []
        for k in range(KD):
            ks, w = slice(k * P, (k + 1) * P), slice(DT0, DT0 + HS)
            dtw = DTW[:, k, HS:2 * HS]
            SPLIT.append(([(ZW[:, k, :], wzx_t[ks, 0:DT0]), (dtw, wzx_t[ks, w])],
                           [(ZW[:, k, :], ZH[:, k, :], ZL[:, k, :]), (dtw, DT[:, k, 0:HS], DT[:, k, HS:2 * HS])],
                           npwc[:, k:k + 1]))
        SPLIT.append(([(RW[:, :, E:2 * E], router_t.rearrange("(k p) e -> p k e", p=P))],
                       [(RW[:, :, E:2 * E], R[:, :, 0:E], R[:, :, E:2 * E])], None))
        for raw, hi, lo, shared, routed in ((GW, GH, GL, swg_t, wg_t), (UW, UH, UL, swu_t, wu_t)):
            for k in range(KD):
                ks = slice(k * P, (k + 1) * P)
                SPLIT.append(([(raw[:, k, 0:SH], shared[ks, :]), (raw[:, k, SH:HB * P], routed[ks, :])],
                               [(raw[:, k, :], hi[:, k, :], lo[:, k, :])], None))
        for js, src in ((slice(0, SB), swd_t), (slice(SB, SB + NR // 2), wd[0:NR // 2 * P, :]),
                        (slice(SB + NR // 2, HB), wd[NR // 2 * P:NR * P, :])):
            SPLIT.append(([(WDW[:, js, :], src.rearrange("(k p) n -> p k n", p=P))],
                           [(WDW[:, js, :], WDH[:, js, :], WDL[:, js, :])], None))

        FIRST = ((ident[:], c_ident), (WQ[:], wq_t.rearrange("(k p) n -> p k n", p=P)),
                 (npwc[:], npw.rearrange("(k p) -> p k", p=P)),
                 (cos_t[:], c_cos.rearrange("(t p) f -> p t f", p=P)),
                 (sin_t[:], c_sin.rearrange("(t p) (a f) -> p t a f", p=P, a=2)),
                 (cw[:], conv_w.rearrange("(b p) k -> p b k", p=P)),
                 (cbv[:], conv_b.rearrange("(b p) -> p b", p=P)),
                 (dtb[:], rows(dt_bias, [[0, P], [1, HS]])),
                 (aneg[:], rows(a_log, [[0, P], [1, HS]])),
                 (dbc[:], rows(d_param, [[0, P], [1, HS]])),
                 (upper[:], c_upper),
                 (ngwc[:], ngw.rearrange("(k p) -> p k", p=P)),
                 (reset[:], rows(c_reset, [[0, P], [1, NT * E]])),
                 (tri[:], rows(c_tri, [[0, P], [GROUPS, GROUPS], [1, GROUPS]])),
                 (ebias[:], rows(cbias, [[0, P], [1, E]])))
        LATE = ((WO[:], wo_t.rearrange("(k p) n -> p k n", p=P)),)

        block = ctx.enter_context(nc.Block())

        @block.sync
        def _(sp):
            def load_split(n):
                with nc.allow_non_contiguous_dma(reason="small columns of weights, once"):
                    for dst, src in SPLIT[n][0]:
                        sp.dma_start(dst, src).then_inc(w_loaded[n], 16)

            def load_x(i):
                sp.dma_start(xs[:], x[i].rearrange("(t p) d -> p t d", p=P)).then_inc(sem["x_loaded"], 16)

            load_x(0)
            for n, (dst, src) in enumerate(FIRST):
                with nc.allow_non_contiguous_dma(reason="small columns of weights, once"):
                    sp.dma_start(dst, src).then_inc(s_const, 16)
                if n == 1:
                    load_split(0)
                    load_split(1)
            for dst, src in LATE:
                sp.dma_start(dst, src).then_inc(s_late, 16)
            for n in range(KD, len(SPLIT)):
                load_split(n)
            give(sp, "SP")

            def decay_rows():
                sp.wait_ge(sem["acsT_ready"], 1)
                sp.dma_start(acs_row, acsT[:]).then_inc(sem["acs_stored"], 16)
                sp.wait_ge(sem["acs_stored"], 16)
                sp.wait_ge(sem["seg_free"], NT)
                sp.dma_start(seg[:].rearrange("p a b c -> p (a b c)"),
                             rows(acs_row, [[0, P], [1, 2 * HS * P]])).then_inc(sem["seg_loaded"], 16)

            def decay_rows_of(c):
                sp.wait_ge(sem["seg_free"], now("seg_free", c - 1))
                sp.dma_start(seg[:, c % 2, :, :].rearrange("p b c -> p (b c)"),
                             rows(acs_row, [[0, P], [1, HS * P]], c * HS * P)).then_inc(sem[f"seg_loaded{c}"], 16)

            def combine_rows():
                sp.wait_ge(sem["cT_ready"], 1)
                sp.sem_inc(sem["f_out_SP"], 1)
                sp.dma_start(c_row, cT).then_inc(sem["c_stored"], 16)
                sp.wait_ge(sem["c_stored"], 16)

            def combine_block(r):
                sp.wait_ge(sem["cb_free"], now("cb_free", r - 1) if r >= 2 else NR - 1 + r)
                sp.dma_start(cb[:, r % 2, :], rows(c_row, [[T, 2], [0, EH], [1, T]], 2 * r * T)
                             ).then_inc(sem[f"cb_loaded{r % 2}"], 16)

            def store(i):
                sp.wait_ge(sem["result_ready"], 1)
                sp.dma_start(out[i].rearrange("(t p) d -> p t d", p=P), x1[:]).then_inc(sem["stored"], 16)

            def next_x(i, more):
                sp.wait_ge(sem["x_free"], 1)
                if more:
                    load_x(i + 1)

            def last_stored():
                sp.wait_ge(sem["stored"], 16)
                sp.sem_inc(sem["x1_free"], 1)

            def settle_a():
                settle(sp, "SP", "a")

            def settle_f():
                settle(sp, "SP", "f")

            def iteration(i, a, f, more=True):
                if f: last_stored(); combine_rows(); combine_block(0); combine_block(1); combine_block(2)
                if a: decay_rows(); decay_rows_of(2)
                if f: combine_block(3)
                if a: decay_rows_of(3)
                if f: combine_block(4); combine_block(5); combine_block(6); combine_block(7)
                if a: next_x(i, more); settle_a()
                if f: store(i - 1); settle_f()

            iteration(0, True, False)
            with sp.Fori(1, SEQS - 1) as i:
                iteration(i, True, True)
            iteration(SEQS - 1, True, True, more=False)
            iteration(SEQS, False, True)
            sp.wait_ge(sem["stored"], 16)

        @block.gpsimd
        def _(pool):
            nc.gpsimd.memset(mhalf[:], -0.5).then_inc(s_fill, 1)
            nc.gpsimd.memset(ones[:], 1.0).then_inc(s_fill, 1)
            nc.gpsimd.memset(one1[:], 1.0).then_inc(s_fill, 1)
            give(pool, "POOL")
            pool.wait_ge(s_fill, 3)

            own = Own(pool, "pool")

            def root(n, ts=slice(0, NT)):
                pool.wait_ge(sem["var_ready"], n)
                nc.gpsimd.tensor_tensor(rstd[:, ts], ve[:, ts], mhalf[:, ts], ALU.pow).then_inc(sem["rstd_ready"], 1)

            def root_of_mean(dst, sums, width, ts):
                own.do(nc.gpsimd.tensor_scalar(sums[:, ts], sums[:, ts], 1.0 / width, EPS, ALU.mult, ALU.add))
                nc.gpsimd.tensor_tensor(dst[:, ts], sums[:, ts], mhalf[:, ts], ALU.pow).then_inc(sem["rstd_ready"], 1)

            def root_q():
                pool.wait_ge(sem["ssq_ready"], 1)
                root_of_mean(rq, ssq, D, slice(0, NT))

            def root_y(s):
                pool.wait_ge(sem["ssy_ready"], s + 1)
                root_of_mean(ry, ssy, DI, slice(2 * s, 2 * s + 2))

            def mask(c):
                pool.wait_ge(sem["seg_ready"], c + 1)
                nc.gpsimd.affine_select(out=seg[:, c % 2, :, :], in_=seg[:, c % 2, :, :], compare_op=ALU.is_ge, fill=NEVER,
                                        base=0, pattern=[[0, HS], [1, P]], channel_multiplier=-1
                                        ).then_inc(sem["masked"], 1)

            def rope_sum(s):
                pool.wait_ge(sem["rope_ready"], s + 1)
                sl = slice(2 * s, 2 * s + 2)
                nc.gpsimd.tensor_tensor(qrot[:, sl, :], qrot[:, sl, :], tmp[:, sl, :], ALU.add
                                        ).then_inc(sem["qrot_ready"], 1)

            def decayed(c):
                pool.wait_ge(sem["xdt_ready"], c + 1)
                v = "p (h d) -> p h d"
                nc.gpsimd.tensor_tensor(
                    xdec[:, c % 2, :].rearrange(v, h=HS), xdt[:, c % 2, :].rearrange(v, h=HS),
                    ed[:, c, :].unsqueeze(2).broadcast_to([P, HS, PD]), ALU.mult
                ).then_inc(sem["xdec_ready"], 1)

            def gated(c):
                pool.wait_ge(sem["z_ready"], c + 1)
                pool.wait_ge(sem["y_ready"], c + 1)
                own.do(nc.gpsimd.tensor_tensor(xD[:, c % 2, :], xD[:, c % 2, :], xdt[:, c % 2, :], ALU.add))
                if c < 2:
                    pool.sem_inc(sem["xdt_free"], 1)
                nc.gpsimd.tensor_tensor(zs[:, c, :], zs[:, c, :], xD[:, c % 2, :], ALU.mult
                                        ).then_inc(sem["yg_ready"], 1)

            def combine(j):
                r = j - SB
                pool.wait_ge(sem["product_ready"], r + 1)
                pool.wait_ge(sem[f"cb_loaded{r % 2}"], 16 * (r // 2 + 1))
                nc.gpsimd.tensor_tensor(hid[:, j % 2, :], hid[:, j % 2, :], cb[:, r % 2, :], ALU.mult
                                        ).then_inc(sem["routed_ready"], 1)

            def rest(j):
                pool.wait_ge(sem["hidden_high"], j + 1)
                own.do(nc.gpsimd.tensor_tensor(hidL[:, j % 2, :], hid[:, j % 2, :], hidH[:, j % 2, :].bitcast(fp32),
                                               ALU.subtract))
                pool.sem_inc(sem["hidden_split"], 1)
                pool.sem_inc(sem["hid_free"], 1)

            def final():
                pool.wait_ge(sem["fvar_ready"], 1)
                own.do(nc.gpsimd.tensor_tensor(frstd[:], fve[:], mhalf[:], ALU.pow))
                nc.gpsimd.tensor_tensor(fnm[:], fnm[:], frstd[:], ALU.mult).then_inc(sem["frstd_ready"], 1)

            def final_sum():
                pool.wait_ge(sem["normalised"], 1)
                own.do(nc.gpsimd.tensor_tensor(x1[:].rearrange("p t d -> p (t d)"), x1[:].rearrange("p t d -> p (t d)"),
                                               xT[:].rearrange("p k t -> p (k t)"), ALU.add))
                pool.sem_inc(sem["result_ready"], 1)
                pool.sem_inc(sem["xT_free"], 1)

            h0, h1 = slice(0, 2), slice(2, 4)

            def settle_a():
                settle(pool, "POOL", "a")

            def settle_f():
                settle(pool, "POOL", "f")

            def iteration(a, f, w=False):
                if a: root(1)
                if f: rest(0); rest(1); rest(2)
                if a: rope_sum(0); rope_sum(1); root_q()
                if f: rest(3); combine(4); combine(5); rest(4); rest(5); combine(6)
                if a: mask(0); decayed(0); mask(1); decayed(1)
                if f: rest(6)
                if a: gated(0); mask(2)
                if f: combine(7)
                if a: gated(1); decayed(2)
                if f: rest(7)
                if a: mask(3)
                if f: combine(8); rest(8)
                if a: root_y(0); gated(2); gated(3); root(2, h0)
                if f: combine(9)
                if a: root_y(1); root(3, h1)
                if f: rest(9); combine(10)
                if a: root(4, h0)
                if f: rest(10)
                if a: root(5, h1); settle_a()
                if f: combine(11); rest(11); final(); final_sum(); settle_f()
                own.settle()

            iteration(True, False)
            with pool.Fori(1, SEQS):
                iteration(True, True)
            iteration(False, True)

        @block.scalar
        def _(act):
            own = Own(act, "act")
            act.wait_ge(s_fill, 3)
            give(act, "ACT")
            act.sem_inc(sem["xT_free"], 1)

            def exp_a():
                act.wait_ge(s_const, 16 * len(FIRST))
                nc.scalar.activation(aneg[:], aneg[:], ACT.Exp).then_inc(s_aexp, 1)

            def split_high(n):
                loads, pieces, norm = SPLIT[n]
                act.wait_ge(w_loaded[n], 16 * len(loads))
                for src, hi, _ in pieces:
                    if norm is None:
                        ins = nc.scalar.copy(hi, src)
                    else:
                        ins = nc.scalar.activation(hi, src, ACT.Identity, scale=norm)
                ins.then_inc(s_high, 1)

            def evac_xT(k):
                if k == 0:
                    act.wait_ge(sem["xT_free"], 1)
                filled(act, "ACT", f"xT{k}")
                nc.scalar.copy(xT[:, k, :], bank(f"xT{k}")[:]).then_inc(sem["a_out_ACT"], 1)

            def square_q(s):
                act.wait_ge(sem["qrot_ready"], s + 1)
                for t, done in ((2 * s, "a_out_ACT" if s else None), (2 * s + 1, "ssq_ready" if s else "a_out_ACT")):
                    ins = nc.scalar.activation(zs[:, t, 0:D], qrot[:, t, :], ACT.Square, accum_out=ssq[:, t:t + 1])
                    if done:
                        ins.then_inc(sem[done], 1)

            def high(dst, name):
                filled(act, "ACT", name)
                nc.scalar.copy(dst, bank(name)[:]).then_inc(sem["hi_ready"], 1)

            def softplus():
                act.wait_ge(sem["na_ready"], 1)
                own.do(nc.scalar.activation(e1[:], na[:], ACT.Exp))
                nc.scalar.activation(l1[:], e1[:], ACT.Ln, bias=one1[:, 0:1]).then_inc(sem["ln_ready"], 1)

            def conv_first(b):
                filled(act, "ACT", f"xc{b}")
                nc.scalar.activation(xc[:, b, :], bank(f"xc{b}")[:], ACT.Identity, bias=cbv[:, b:b + 1],
                                     scale=cw[:, b, TAPS - 1:TAPS]).then_inc(sem["conv_first"], 1)

            def conv_silu(b, n):
                act.wait_ge(sem["conv_ready"], n)
                nc.scalar.activation(xc[:, b, :], xc[:, b, :], ACT.Silu).then_inc(sem["a_out_ACT"], 1)

            def decays():
                act.wait_ge(sem["acs_ready"], 1)
                nc.scalar.activation(ea[:].rearrange("p t h -> p (t h)"), acs[:, 0, :], ACT.Exp)
                nc.scalar.activation(el[:].rearrange("p t h -> p (t h)"), acs[:, 1, :], ACT.Exp)
                nc.scalar.activation(ed[:], ed[:], ACT.Exp).then_inc(sem["decay_ready"], 1)

            def exp_seg(c):
                act.wait_ge(sem["masked"], c + 1)
                nc.scalar.activation(seg[:, c % 2, :, :], seg[:, c % 2, :, :], ACT.Exp).then_inc(sem["exp_ready"], 1)

            def silu_z(j):
                filled(act, "ACT", f"z{j}")
                own.do(nc.scalar.activation(zs[:, j, :], bank(f"z{j}")[:], ACT.Silu))
                act.sem_inc(sem["a_out_ACT"], 1)
                act.sem_inc(sem["z_ready"], 1)

            def evac_B():
                filled(act, "ACT", "Bt")
                nc.scalar.copy(Btok[:].rearrange("p t n -> p (t n)"), bank("Bt")[:]).then_inc(sem["a_out_ACT"], 1)

            def evac_CB():
                filled(act, "ACT", "CB")
                nc.scalar.copy(CBs[:].rearrange("p t n -> p (t n)"), bank("CB")[:]).then_inc(sem["a_out_ACT"], 1)

            def evac_y(c):
                filled(act, "ACT", f"yT{c}")
                nc.scalar.copy(yT[:, c % 2, :, :].rearrange("p j n -> p (j n)"), bank(f"yT{c}")[:]
                               ).then_inc(sem["a_out_ACT"], 1)
                if c >= 2:
                    own.wait()
                ins = nc.scalar.activation(junk[c % 2], zs[:, c, :], ACT.Square, accum_out=ssy[:, c:c + 1])
                if c % 2:
                    ins.then_inc(sem["ssy_ready"], 1)
                else:
                    own.mark(ins)

            def exp_table():
                nc.scalar.preload_act_table_set("natural_log_exp_and_others")

            def silu_table():
                nc.scalar.preload_act_table_set("silu_and_others")

            def save_x1():
                act.wait_ge(sem["x1_ready"], 1)
                act.wait_ge(sem["x1_free"], 1)
                nc.scalar.copy(x1[:], tmp[:]).then_inc(sem["tmp_free"], 1)

            def score_tanh():
                act.wait_ge(sem["logits_ready"], 1)
                nc.scalar.activation(th[:], msk[:], ACT.Tanh, scale=0.5).then_inc(sem["tanh_ready"], 1)

            def evac_cT():
                filled(act, "ACT", "cT")
                nc.scalar.copy(cT, bank("cT")[0:E, :]).then_inc(sem["cT_ready"], 1)

            def gate(j):
                act.wait_ge(sem["hid_free"], now("hid_free", j - 1) if j >= 2 else HB - 1 + j)
                filled(act, "ACT", f"G{j}")
                nc.scalar.activation(hid[:, j % 2, :], bank(f"G{j}")[:], ACT.Silu).then_inc(sem["silu_ready"], 1)

            def final_norm():
                act.wait_ge(sem["frstd_ready"], 1)
                parts = xT[:].rearrange("p k (a d) -> p (k a) d", a=2)
                for t in range(NT):
                    ins = nc.scalar.activation(parts[:, t, :], acc[t // 2][:, (t % 2) * D:(t % 2 + 1) * D], ACT.Identity,
                                               bias=fnm[:, t:t + 1], scale=frstd[:, t:t + 1])
                own.do(ins)
                act.sem_inc(sem["acc_free"], 1)
                act.sem_inc(sem["normalised"], 1)

            def round_hidden(j):
                act.wait_ge(sem["down_done"], now("down_done", j - 1) if j >= 2 else HB - 1 + j)
                if j < SB:
                    act.wait_ge(sem["shared_ready"], j + 1)
                else:
                    act.wait_ge(sem["routed_ready"], j - SB + 1)
                nc.scalar.copy(hidH[:, j % 2, :], hid[:, j % 2, :]).then_inc(sem["hidden_high"], 1)

            def settle_a():
                settle(act, "ACT", "a")

            def settle_f():
                settle(act, "ACT", "f")

            def iteration(i, a, f, w=False):
                if w: exp_a(); split_high(0)
                if f: gate(0); gate(1); round_hidden(0)
                if a: evac_xT(0); evac_xT(1)
                if w: split_high(1)
                if f: gate(2); save_x1(); round_hidden(1); gate(3); round_hidden(2); evac_cT()
                if a: square_q(0)
                if w: split_high(2)
                if a: square_q(1); high(hTh[:, 0, :], "hT0"); high(hTh[:, 1, :], "hT1")
                if f: gate(4); round_hidden(3); gate(5)
                if w: split_high(3); split_high(4)
                if a: silu_table()
                if f: round_hidden(4)
                if w: split_high(5)
                if a: exp_table(); conv_first(4); softplus(); silu_table(); conv_first(5)
                if f: round_hidden(5)
                if a: conv_silu(4, 1)
                if f: gate(6)
                if a:
                    conv_silu(5, 2); conv_first(0); conv_first(1); conv_silu(0, 3); conv_first(2); exp_table()
                    conv_first(3); decays(); conv_silu(1, 4)
                if f: gate(7)
                if a: conv_silu(2, 5); conv_silu(3, 6); silu_z(0); evac_B(); evac_CB(); exp_seg(0)
                if f: round_hidden(6)
                if w: split_high(6)
                if a: exp_seg(1); silu_z(1)
                if w: split_high(7)
                if a: exp_seg(2)
                if w: split_high(8); split_high(9)
                if f: round_hidden(7)
                if a: evac_y(0)
                if f: gate(8)
                if a: silu_z(2); exp_seg(3); evac_y(1)
                if f: gate(9); round_hidden(8)
                if a: silu_z(3); evac_y(2)
                if f: round_hidden(9); gate(10)
                if a: evac_y(3)
                if f: gate(11); round_hidden(10); round_hidden(11)
                if a: high(fTh[:, 0, :], "fT0"); high(fTh[:, 1, :], "fT1"); score_tanh(); settle_a()
                if f: final_norm(); settle_f()
                own.settle()

            own.settle()
            iteration(0, True, False, True)
            with act.Fori(1, SEQS) as i:
                iteration(i, True, True)
            iteration(SEQS, False, True)

        @block.vector
        def _(dve):
            own = Own(dve, "dve")
            V = nc.vector
            dve.wait_ge(s_const, 16 * len(FIRST))
            give(dve, "DVE")

            def negate_a():
                dve.wait_ge(s_aexp, 1)
                own.do(V.tensor_scalar(aneg[:], aneg[:], -1.0, None, ALU.mult))

            def split_low(n):
                dve.wait_ge(s_high, n + 1)
                _, pieces, norm = SPLIT[n]
                for src, hi, lo in pieces:
                    if norm is None:
                        ins = V.tensor_tensor(lo, src, hi.bitcast(fp32), ALU.subtract)
                    else:
                        ins = V.scalar_tensor_tensor(lo, src, norm, hi.bitcast(fp32), ALU.mult, ALU.subtract)
                ins.then_inc(s_low, 1)

            def scale_out():
                dve.wait_ge(s_late, 16 * len(LATE))
                for k in range(NB):
                    ins = V.tensor_scalar(WO[:, k, :], WO[:, k, :], ngwc[:, k:k + 1], None, ALU.mult)
                ins.then_inc(s_scaled, 1)

            def moments(src, st, m, ts=range(NT)):
                for t in ts:
                    ins = V.bn_stats(st[:, t, :], src(t))
                own.do(ins)
                for t in ts:
                    ins = V.bn_aggr(m[:, t, :], st[:, t, :])
                own.do(ins)

            def send_variance(ts):
                sl = slice(ts[0], ts[-1] + 1)
                V.tensor_scalar(ve[:, sl], mv[:, sl, 1], EPS, None, ALU.add).then_inc(sem["var_ready"], 1)

            def normalise(dst, src, nth, ts=range(NT), done=None):
                dve.wait_ge(sem["rstd_ready"], nth)
                for t in ts:
                    ins = V.tensor_scalar(dst[:, t, :], src[:, t, :], mv[:, t, 0:1], rstd[:, t:t + 1],
                                          ALU.subtract, ALU.mult)
                if done:
                    ins.then_inc(sem[done], 1)
                else:
                    own.do(ins)

            def moments_x():
                dve.wait_ge(sem["x_loaded"], 16)
                moments(lambda t: xs[:, t, :], st6, mv)
                send_variance(range(NT))

            def norm_x():
                normalise(xn, xs, 1, done="xn_ready")

            def rope(s):
                filled(dve, "DVE", f"q{s}")
                if s == 0:
                    dve.wait_ge(sem["tmp_free"], 1)
                sl = slice(2 * s, 2 * s + 2)
                q = bank(f"q{s}")[:].rearrange("p (t h a f) -> p t h a f", t=2, a=2, f=HALF)
                o = tmp[:, sl, :].rearrange("p t (h a f) -> p t h a f", a=2, f=HALF)
                for a in range(2):
                    V.tensor_tensor(o[:, :, :, a, :], q[:, :, :, 1 - a, :],
                                    sin_t[:, sl, a, :].unsqueeze(2).broadcast_to([P, 2, HEADS, HALF]), ALU.mult)
                V.tensor_tensor(qrot[:, sl, :].rearrange("p t (g f) -> p t g f", f=HALF),
                                bank(f"q{s}")[:].rearrange("p (t g f) -> p t g f", t=2, f=HALF),
                                cos_t[:, sl, :].unsqueeze(2).broadcast_to([P, 2, 2 * HEADS, HALF]), ALU.mult
                                ).then_inc(sem["rope_ready"], 1)

            def norm_q():
                dve.wait_ge(sem["rstd_ready"], 2)
                for t in range(NT):
                    ins = V.tensor_scalar(xn[:, t, :], qrot[:, t, :], rq[:, t:t + 1], None, ALU.mult)
                ins.then_inc(sem["xn_ready"], 1)

            def low(lo, hi, name, n):
                dve.wait_ge(sem["hi_ready"], n)
                V.tensor_tensor(lo, bank(name)[:], hi.bitcast(fp32), ALU.subtract).then_inc(sem["a_out_DVE"], 1)

            def dt_bias_add():
                filled(dve, "DVE", "dt")
                parts = bank("dt")[:, 0:2 * NT * HS].rearrange("p (t a h) -> p t a h", t=NT, a=2)
                own.do(V.tensor_tensor(dr[:], parts[:, :, 0, :], dtb[:].unsqueeze(1).broadcast_to([P, NT, HS]), ALU.add))
                own.do(V.tensor_tensor(dr[:], dr[:], parts[:, :, 1, :], ALU.add))
                dve.sem_inc(sem["a_out_DVE"], 1)
                V.scalar_tensor_tensor(na[:], dr[:], -1.0, dr[:], ALU.mult, ALU.min).then_inc(sem["na_ready"], 1)

            def dt_finish():
                dve.wait_ge(sem["ln_ready"], 1)
                own.do(V.scalar_tensor_tensor(dt[:], dr[:], 0.0, l1[:], ALU.max, ALU.add))
                V.tensor_tensor(ad[:], dt[:], aneg[:].unsqueeze(1).broadcast_to([P, NT, HS]), ALU.mult
                                ).then_inc(sem["ad_ready"], 1)

            def conv(b, n):
                dve.wait_ge(sem["conv_first"], n)
                src = bank(f"xc{b}")
                for s in range(1, TAPS):
                    ins = V.scalar_tensor_tensor(xc[:, b, s:], src[:, 0:T - s], cw[:, b, TAPS - 1 - s:TAPS - s],
                                                 xc[:, b, s:], ALU.mult, ALU.add)
                    if s < TAPS - 1:
                        own.do(ins)
                ins.then_inc(sem["conv_ready"], 1)

            def evac_acs():
                filled(dve, "DVE", "acs")
                V.tensor_copy(acs[:].rearrange("p a n -> p (a n)"), bank("acs")[:, 0:2 * NT * HS])
                own.do(V.tensor_copy(acsT[:], bank("acs")[0:NT * HS, P:2 * P]))
                dve.sem_inc(sem["acsT_ready"], 1)
                dve.sem_inc(sem["a_out_DVE"], 1)
                V.tensor_tensor(ed[:].rearrange("p t h -> p (t h)"), acs[:, 1, :], acs[:, 0, :], ALU.subtract
                                ).then_inc(sem["acs_ready"], 1)

            def decay_exponents(c):
                if c != 1:
                    dve.wait_ge(sem[f"seg_loaded{c}" if c else "seg_loaded"], 16)
                V.tensor_tensor(seg[:, c % 2, :, :], seg[:, c % 2, :, :],
                                acs[:, 0, c * HS:(c + 1) * HS].unsqueeze(2).broadcast_to([P, HS, P]), ALU.subtract
                                ).then_inc(sem["seg_ready"], 1)

            def by_head(ap):
                return ap.rearrange("p (h d) -> p h d", h=HS)

            def along(small):
                return small.unsqueeze(2).broadcast_to([P, HS, PD])

            def times_dt(c):
                if c == 0:
                    dve.wait_ge(sem["decay_ready"], 1)
                if c >= 2:
                    dve.wait_ge(sem["xdt_free"], c - 1)
                filled(dve, "DVE", f"xt{c}")
                V.tensor_tensor(by_head(xD[:, c % 2, :]), by_head(bank(f"xt{c}")[:]), along(dbc[:]), ALU.mult)
                own.do(V.tensor_tensor(by_head(xdt[:, c % 2, :]), by_head(bank(f"xt{c}")[:]), along(dt[:, c, :]), ALU.mult))
                dve.sem_inc(sem["a_out_DVE"], 1)
                if c < NT - 1:
                    dve.sem_inc(sem["xdt_ready"], 1)

            def decay_CB(c):
                dve.wait_ge(sem["exp_ready"], c + 1)
                V.tensor_tensor(seg[:, c % 2, :, :], seg[:, c % 2, :, :],
                                CBs[:, c, :].unsqueeze(1).broadcast_to([P, HS, P]), ALU.mult
                                ).then_inc(sem["m_ready"], 1)

            def state_part(c):
                filled(dve, "DVE", f"yo{c}")
                own.do(V.tensor_tensor(by_head(xT[:, c % 2, :]), by_head(bank(f"yo{c}")[:]), along(ea[:, c, :]), ALU.mult))
                dve.sem_inc(sem["a_out_DVE"], 1)

            def new_state(c):
                if c:
                    own.do(V.tensor_tensor(by_head(S[:]), by_head(S[:]), along(el[:, c, :]), ALU.mult))
                filled(dve, "DVE", f"st{c}")
                if c:
                    ins = V.tensor_tensor(S[:], S[:], bank(f"st{c}")[:], ALU.add)
                else:
                    ins = V.tensor_copy(S[:], bank("st0")[:])
                own.do(ins)
                dve.sem_inc(sem["a_out_DVE"], 1)

            def chunk_y(c):
                filled(dve, "DVE", f"yd{c}")
                dve.sem_inc(sem["seg_free"], 1)
                if c:
                    ins = V.tensor_tensor(xdt[:, c % 2, :], xT[:, c % 2, :], bank(f"yd{c}")[:], ALU.add)
                else:
                    ins = V.tensor_copy(xdt[:, c % 2, :], bank(f"yd{c}")[:])
                own.do(ins)
                dve.sem_inc(sem["a_out_DVE"], 1)
                dve.sem_inc(sem["y_ready"], 1)

            def mixed_out(s, nth):
                ts = (2 * s, 2 * s + 1)
                filled(dve, "DVE", f"out{s}")
                dve.wait_ge(sem["rstd_ready"], nth)
                for t in ts:
                    ins = V.scalar_tensor_tensor(
                        tmp[:, t, :], bank(f"out{s}")[:, (t % 2) * D:(t % 2 + 1) * D], ry[:, t:t + 1],
                        qrot[:, t, :], ALU.mult, ALU.add)
                own.do(ins)
                dve.sem_inc(sem["a_out_DVE"], 1)
                moments(lambda t: tmp[:, t, :], st6, mv, ts)
                send_variance(ts)

            def form_x1(s, nth):
                ts = (2 * s, 2 * s + 1)
                normalise(tmp, tmp, nth, ts)
                sl = slice(2 * s, 2 * s + 2)
                own.do(V.tensor_tensor(tmp[:, sl, :], tmp[:, sl, :], xs[:, sl, :], ALU.add))
                if s:
                    dve.sem_inc(sem["x_free"], 1)
                    dve.sem_inc(sem["x1_ready"], 1)
                moments(lambda t: tmp[:, t, :], st6, mv, ts)
                send_variance(ts)

            def norm_x1(s, nth):
                normalise(xn, tmp, nth, (2 * s, 2 * s + 1), "xn_ready")

            def up(j):
                dve.wait_ge(sem["silu_ready"], j + 1)
                filled(dve, "DVE", f"U{j}")
                own.do(V.tensor_tensor(hid[:, j % 2, :], hid[:, j % 2, :], bank(f"U{j}")[:], ALU.mult))
                dve.sem_inc(sem["f_out_DVE"], 1)
                dve.sem_inc(sem["shared_ready" if j < SB else "product_ready"], 1)

            te = "p (t e) -> p t e"

            def route_logits():
                filled(dve, "DVE", "logits")
                parts = bank("logits")[:, 0:2 * NT * E].rearrange("p (t a e) -> p t a e", t=NT, a=2)
                own.do(V.tensor_copy(msk[:].rearrange(te, t=NT), parts[:, :, 0, :]))
                own.do(V.tensor_tensor(msk[:].rearrange(te, t=NT), msk[:].rearrange(te, t=NT), parts[:, :, 1, :], ALU.add))
                dve.sem_inc(sem["a_out_DVE"], 1)
                dve.sem_inc(sem["logits_ready"], 1)

            def route_scores():
                dve.wait_ge(sem["tanh_ready"], 1)
                own.do(V.tensor_scalar(sc[:], th[:], 0.5, 0.5, ALU.mult, ALU.add))
                own.do(V.tensor_tensor(sbs[:].rearrange(te, t=NT), sc[:].rearrange(te, t=NT),
                                       ebias[:].unsqueeze(1).broadcast_to([P, NT, E]), ALU.add))

            def route_groups():
                pairs = sbs[:].rearrange("p (g a b) -> p g a b", a=2, b=2)
                V.tensor_tensor(hi2[:], pairs[:, :, :, 0], pairs[:, :, :, 1], ALU.max)
                own.do(V.tensor_tensor(lo2[:], pairs[:, :, :, 0], pairs[:, :, :, 1], ALU.min))
                V.tensor_tensor(m1[:], hi2[:, :, 0], hi2[:, :, 1], ALU.max)
                V.tensor_tensor(mn[:], hi2[:, :, 0], hi2[:, :, 1], ALU.min)
                own.do(V.tensor_tensor(rk[:], lo2[:, :, 0], lo2[:, :, 1], ALU.max))
                own.do(V.tensor_tensor(mn[:], mn[:], rk[:], ALU.max))
                own.do(V.tensor_tensor(gs[:], m1[:], mn[:], ALU.add))
                g4 = gs[:].rearrange("p (t g) -> p t g", t=NT)
                theirs = g4.unsqueeze(2).broadcast_to([P, NT, GROUPS, GROUPS])
                ours = g4.unsqueeze(3).broadcast_to([P, NT, GROUPS, GROUPS])
                v4 = "p (t g j) -> p t g j"
                GT, EQ = (b[:].rearrange(v4, t=NT, g=GROUPS) for b in (gt, eq))
                V.tensor_tensor(GT, theirs, ours, ALU.is_gt)
                own.do(V.tensor_tensor(EQ, theirs, ours, ALU.is_equal))
                own.do(V.tensor_tensor(EQ, EQ, tri[:].unsqueeze(1).broadcast_to([P, NT, GROUPS, GROUPS]), ALU.mult))
                own.do(V.tensor_tensor(gt[:], gt[:], eq[:], ALU.add))
                own.do(V.reduce_sum(rk[:], gt[:].rearrange("p (g j) -> p g j", j=GROUPS), AX.X))
                own.do(V.tensor_scalar(rk[:], rk[:], float(TOPG), NEVER, ALU.is_ge, ALU.mult))
                own.do(V.tensor_tensor(msk[:].rearrange("p (g j) -> p g j", j=GROUPS),
                                       sbs[:].rearrange("p (g j) -> p g j", j=GROUPS),
                                       rk[:].unsqueeze(2).broadcast_to([P, NT * GROUPS, GROUPS]), ALU.add))

            def route_experts():
                for t in range(NT):
                    ins = V.max(v8[:, t, :], msk[:, t * E:(t + 1) * E])
                own.do(ins)
                m3 = msk[:].rearrange(te, t=NT)
                fourth = v8[:, :, TOPK - 1:TOPK].broadcast_to([P, NT, E])
                V.tensor_tensor(gt[:].rearrange(te, t=NT), m3, fourth, ALU.is_gt)
                own.do(V.tensor_tensor(eq[:].rearrange(te, t=NT), m3, fourth, ALU.is_equal))
                V.reduce_sum(ws[:], gt[:].rearrange(te, t=NT), AX.X)
                own.do(V.tensor_tensor_scan(pre[:], reset[:], eq[:], 0.0, ALU.mult, ALU.add))
                p3 = pre[:].rearrange(te, t=NT)
                own.do(V.tensor_tensor(p3, p3, ws[:].unsqueeze(2).broadcast_to([P, NT, E]), ALU.add))
                own.do(V.scalar_tensor_tensor(eq[:], pre[:], float(TOPK), eq[:], ALU.is_le, ALU.mult))
                own.do(V.tensor_tensor(gt[:], gt[:], eq[:], ALU.add))
                own.do(V.tensor_tensor(gt[:], gt[:], sc[:], ALU.mult))
                own.do(V.reduce_sum(ws[:], gt[:].rearrange(te, t=NT), AX.X))
                own.do(V.tensor_scalar(ws[:], ws[:], 1e-20, None, ALU.add))
                own.do(V.reciprocal(ws[:], ws[:]))
                V.tensor_tensor(gt[:].rearrange(te, t=NT), gt[:].rearrange(te, t=NT),
                                ws[:].unsqueeze(2).broadcast_to([P, NT, E]), ALU.mult).then_inc(sem["c_ready"], 1)

            def final():
                dve.wait_ge(sem["acc_ready"], 1)
                dve.sem_inc(sem["down_done"], 1)
                moments(lambda t: acc[t // 2][:, (t % 2) * D:(t % 2 + 1) * D], fst6, fmv)
                V.tensor_scalar(fnm[:], fmv[:, :, 0], -1.0, None, ALU.mult)
                V.tensor_scalar(fve[:], fmv[:, :, 1], EPS, None, ALU.add).then_inc(sem["fvar_ready"], 1)

            def settle_a():
                settle(dve, "DVE", "a")

            def settle_f():
                settle(dve, "DVE", "f")

            def iteration(a, f, w=False):
                if a: moments_x()
                if f: up(0)
                if w: split_low(0); negate_a()
                if a: norm_x()
                if f: route_groups(); up(1); route_experts(); up(2)
                if w: split_low(1)
                if a: rope(0); rope(1)
                if f: up(3)
                if w: split_low(2)
                if a: norm_q(); low(hTl[:, 0, :], hTh[:, 0, :], "hT0", 1)
                if w: split_low(3)
                if f: up(4)
                if a: low(hTl[:, 1, :], hTh[:, 1, :], "hT1", 2); dt_bias_add()
                if w: split_low(4); split_low(5)
                if f: up(5)
                if a: conv(4, 1); dt_finish(); conv(5, 2); evac_acs()
                if f: up(6)
                if a:
                    conv(0, 3); conv(1, 4); conv(2, 5); conv(3, 6); decay_exponents(0); decay_exponents(1)
                    times_dt(0); decay_CB(0); times_dt(1); new_state(0)
                if w: split_low(6)
                if a: decay_CB(1); chunk_y(0)
                if f: up(7)
                if a: decay_exponents(2)
                if w: split_low(7); split_low(8); split_low(9)
                if a: state_part(1); new_state(1)
                if w: scale_out()
                if a: chunk_y(1); times_dt(2); state_part(2); decay_CB(2)
                if f: up(8)
                if a:
                    decay_exponents(3); new_state(2); chunk_y(2); decay_CB(3); times_dt(3); state_part(3); chunk_y(3)
                if f: up(9)
                if a: mixed_out(0, 3)
                if f: up(10)
                if a: mixed_out(1, 5); form_x1(0, 4); form_x1(1, 6)
                if f: up(11)
                if a:
                    norm_x1(0, 7); norm_x1(1, 8); low(fTl[:, 0, :], fTh[:, 0, :], "fT0", 3)
                    low(fTl[:, 1, :], fTh[:, 1, :], "fT1", 4)
                if f: final()
                if a: route_logits(); route_scores(); settle_a()
                if f: settle_f()
                own.settle()

            iteration(True, False, True)
            with dve.Fori(1, SEQS):
                iteration(True, True)
            iteration(False, True)

        @block.tensor
        def _(pe):
            pe.wait_ge(s_const, 16 * len(FIRST))
            pe.wait_ge(s_fill, 3)
            give(pe, "PE")

            def out_of(name):
                part, n = WHERE[name]
                if SLOTS[part][n][2] == "with U":
                    n += 1
                who = SLOTS[part][n][2]
                return f"{part}_out_{who}", count(part, 2, who, n)

            def slot(name):
                part, n = WHERE[name]
                if n >= 3:
                    s, k = out_of(SLOTS[part][n - 3][0])
                    pe.wait_ge(sem[s], now(s, k))
                else:
                    s, k = out_of([slot[0] for slot in SLOTS[part][n::3]][-1])
                    pe.wait_ge(sem[s], k)
                return bank(name)

            def read_out(name):
                s, k = out_of(name)
                pe.wait_ge(sem[s], now(s, k))

            def fill(name, ins):
                part, n = WHERE[name]
                ins.then_inc(sem[f"{part}_for_{SLOTS[part][n][1]}"], 1)

            def split_mm(dst, parts, last=True):
                n, total = 0, 3 * len(parts)
                for ah, al, bh, bl in parts:
                    for l, r in ((ah, bh), (ah, bl), (al, bh)):
                        ins = nc.tensor.matmul(dst, l, r, start=n == 0, stop=n == total - 1)
                        n += 1
                return ins

            def transposes(name, src, n=NT):
                b = slot(name)
                for t in range(n):
                    ins = nc.tensor.transpose(b[:, t * P:(t + 1) * P], src(t), ident[:])
                return ins

            def x_transposes(names, nth):
                pe.wait_ge(sem["xn_ready"], nth)
                for k, name in enumerate(names):
                    fill(name, transposes(name, lambda t: xn[:, t, k * P:(k + 1) * P]))

            def project_q(s):
                b = slot(f"q{s}")
                read_out("xT1")
                for t in range(2):
                    for k in range(KD):
                        ins = nc.tensor.matmul(b[:, t * D:(t + 1) * D], xT[:, k, (2 * s + t) * P:(2 * s + t + 1) * P],
                                               WQ[:, k, :], start=k == 0, stop=k == KD - 1)
                fill(f"q{s}", ins)

            def narrow(b, hi, lo, w, n):
                for t in range(NT):
                    tk = slice(t * P, (t + 1) * P)
                    for k in range(KD):
                        nc.tensor.matmul(b[:, 2 * n * t:2 * n * (t + 1)], hi[:, k, tk], w[:, k, :],
                                         start=k == 0, stop=False, skip_group_check=True)
                        ins = nc.tensor.matmul(b[:, 2 * n * t:2 * n * t + n], lo[:, k, tk], w[:, k, 0:n],
                                               start=False, stop=k == KD - 1, skip_group_check=True)
                return ins

            def weights_split(n):
                pe.wait_ge(s_low, n)

            def out_weights():
                pe.wait_ge(s_scaled, 1)

            def project_dt():
                b = slot("dt")
                read_out("hT1")
                fill("dt", narrow(b, hTh, hTl, DT, HS))

            def project(name, col):
                b = slot(name)
                cs = slice(col, col + P)
                fill(name, split_mm(b[:], [(ZH[:, k, cs], ZL[:, k, cs], hTh[:, k, :], hTl[:, k, :]) for k in range(KD)]))

            def project_x(b):
                project(f"xc{b}", DI + b * P)

            def cumulate():
                b = slot("acs")
                pe.wait_ge(sem["ad_ready"], 1)
                rhs = ad[:].rearrange("p t h -> p (t h)")
                n = NT * HS
                nc.tensor.matmul(b[:, 0:n], upper[:], rhs, start=True, stop=True)
                nc.tensor.matmul(b[:, n:2 * n], ones[:], rhs, start=True, stop=True)
                fill("acs", nc.tensor.matmul(b[0:n, P:2 * P], rhs, upper[:], start=True, stop=True))

            def project_z(c):
                tk = slice(c * P, (c + 1) * P)
                fill(f"z{c}", split_mm(slot(f"z{c}")[:], [(hTh[:, k, tk], hTl[:, k, tk], ZH[:, k, 0:DI], ZL[:, k, 0:DI])
                                                          for k in range(KD)]))

            def B_by_token():
                read_out("xc4")
                fill("Bt", transposes("Bt", lambda t: xc[:, 4, t * P:(t + 1) * P]))

            def CB():
                b = slot("CB")
                read_out("xc5")
                for t in range(NT):
                    tk = slice(t * P, (t + 1) * P)
                    ins = nc.tensor.matmul(b[:, tk], xc[:, 4, tk], xc[:, 5, tk], start=True, stop=True)
                fill("CB", ins)

            def x_by_token(c):
                read_out("xc3")
                fill(f"xt{c}", transposes(f"xt{c}", lambda j: xc[:, j, c * P:(c + 1) * P], NB))

            def from_state(c):
                b = slot(f"yo{c}")
                read_out(f"st{c - 1}")
                fill(f"yo{c}", nc.tensor.matmul(b[:], xc[:, 5, c * P:(c + 1) * P], S[:], start=True, stop=True))

            def state(c):
                b = slot(f"st{c}")
                pe.wait_ge(sem["xdec_ready"], c + 1)
                fill(f"st{c}", nc.tensor.matmul(b[:], Btok[:, c, :], xdec[:, c % 2, :], start=True, stop=True))

            def diagonal(c):
                b = slot(f"yd{c}")
                pe.wait_ge(sem["m_ready"], c + 1)
                for h in range(HS):
                    hs = slice(h * PD, (h + 1) * PD)
                    ins = nc.tensor.matmul(b[:, hs], seg[:, c % 2, h, :], xdt[:, c % 2, hs], start=True, stop=True)
                fill(f"yd{c}", ins)

            def y_by_channel(c):
                b = slot(f"yT{c}")
                pe.wait_ge(sem["yg_ready"], c + 1)
                for j in range(NB):
                    ins = nc.tensor.transpose(b[:, j * P:(j + 1) * P], zs[:, c, j * P:(j + 1) * P], ident[:])
                fill(f"yT{c}", ins)

            def project_out(s):
                b = slot(f"out{s}")
                for t in range(2):
                    read_out(f"yT{2 * s + t}")
                    for j in range(NB):
                        ins = nc.tensor.matmul(b[:, t * D:(t + 1) * D], yT[:, t, j, :], WO[:, j, :],
                                               start=j == 0, stop=j == NB - 1)
                fill(f"out{s}", ins)

            def logits():
                b = slot("logits")
                read_out("fT1")
                fill("logits", narrow(b, fTh, fTl, R, E))

            def combine_by_expert():
                b = slot("cT")
                pe.wait_ge(sem["c_ready"], 1)
                for t in range(NT):
                    ins = nc.tensor.transpose(b[0:E, t * P:(t + 1) * P], gt[:, t * E:(t + 1) * E], ident[:])
                fill("cT", ins)

            def hidden(name, hi, lo, j):
                b = slot(name)
                cs = slice(j * P, (j + 1) * P)
                fill(name, split_mm(b[:], [(hi[:, k, cs], lo[:, k, cs], fTh[:, k, :], fTl[:, k, :]) for k in range(KD)]))

            def down(j):
                pe.wait_ge(sem["hidden_split"], j + 1)
                if j == 0:
                    pe.wait_ge(sem["acc_free"], 1)
                for t in range(NT):
                    dst, tk, w = acc[t // 2][:, (t % 2) * D:(t % 2 + 1) * D], slice(t * P, (t + 1) * P), j % 2
                    for n, (l, r) in enumerate(((hidH, WDH), (hidH, WDL), (hidL, WDH))):
                        ins = nc.tensor.matmul(dst, l[:, w, tk], r[:, j, :], start=j == 0 and t % 2 == 0 and n == 0,
                                               stop=j == HB - 1 and n == 2, skip_group_check=True)
                        if t == 0 and n == 0 and j >= SB:
                            ins.then_inc(sem["cb_free"], 1)
                ins.then_inc(sem["acc_ready" if j == HB - 1 else "down_done"], 1)

            def gate(j):
                hidden(f"G{j}", GH, GL, j)

            def up(j):
                hidden(f"U{j}", UH, UL, j)

            def settle_a():
                settle(pe, "PE", "a")

            def settle_f():
                settle(pe, "PE", "f")

            def iteration(a, f, w=False):
                if f: gate(0); up(0); gate(1); up(1); gate(2)
                if a: x_transposes(("xT0", "xT1"), 1)
                if f: down(0)
                if a: project_q(0)
                if f: up(2); gate(3)
                if a: project_q(1)
                if f: up(3); combine_by_expert(); down(1); gate(4); down(2)
                if a: x_transposes(("hT0", "hT1"), 2)
                if f: up(4); gate(5); up(5)
                if w: weights_split(KD)
                if a: project_dt(); project_x(4); project_x(5)
                if f: gate(6); down(3); up(6)
                if a: cumulate(); project_x(0); project_x(1)
                if f: down(4)
                if a: project_x(2); project_x(3)
                if f: gate(7); down(5)
                if a: project_z(0); B_by_token(); CB(); x_by_token(0); x_by_token(1)
                if f: up(7)
                if a: state(0); diagonal(0)
                if f: gate(8)
                if a: project_z(1); from_state(1); state(1); diagonal(1); y_by_channel(0)
                if f: up(8)
                if a: x_by_token(2); from_state(2); project_z(2)
                if f: down(6)
                if a: state(2); diagonal(2); y_by_channel(1)
                if f: gate(9)
                if a: x_by_token(3)
                if f: up(9)
                if a: from_state(3); project_z(3); diagonal(3)
                if w: out_weights()
                if a: project_out(0)
                if f: down(7)
                if a: y_by_channel(2)
                if f: gate(10); up(10)
                if a: y_by_channel(3); project_out(1)
                if f: down(8); gate(11); down(9); up(11); down(10)
                if a: x_transposes(("fT0", "fT1"), 4)
                if f: down(11)
                if w: weights_split(KD + 1)
                if a: logits(); settle_a()
                if f: settle_f()
                if w: weights_split(len(SPLIT))

            iteration(True, False, True)
            with pe.Fori(1, SEQS):
                iteration(True, True)
            iteration(False, True)


def kernel(**inputs):
    import numpy as np
    import concourse.bacc as bacc
    from concourse.bass_utils import run_bass_kernel_spmd as run

    g = {k: np.asarray(v) for k, v in inputs.items()}

    def t(a):
        return np.ascontiguousarray(a.T)

    def by_expert(w):
        return np.ascontiguousarray(w.transpose(1, 0, 2).reshape(D, E * EH))

    angle = np.arange(T, dtype=np.float32)[:, None] * (
        np.float32(1.0) / np.float32(10000.0) ** (np.arange(0, 2 * HALF, 2, dtype=np.float32) / np.float32(2 * HALF))
    )[None, :]
    angle = angle.astype(np.float32)
    sin = np.sin(angle).astype(np.float32)
    arrays = {
        "x": g["L0_attn_x"],
        "wq_t": t(g["L0_attn_W_in"][:D]),
        "wzx_t": t(g["L0_attn_W_zxbcdt"]),
        "conv_w": g["L0_attn_conv_w"], "conv_b": g["L0_attn_conv_b"], "dt_bias": g["L0_attn_dt_bias"],
        "a_log": g["L0_attn_A_log"], "d_param": g["L0_attn_D_param"],
        "npw": g["L0_attn_norm_pre_w"], "ngw": g["L0_attn_norm_gated_w"],
        "wo_t": t(g["L0_attn_W_out"]),
        "router_t": t(g["L0_ffn_router_w"]), "cbias": g["L0_ffn_correction_bias"],
        "wg_t": by_expert(g["L0_ffn_gate_w"]), "wu_t": by_expert(g["L0_ffn_up_w"]),
        "wd": g["L0_ffn_down_w"].reshape(E * EH, D),
        "swg_t": t(g["L0_ffn_shared_gate_w"]), "swu_t": t(g["L0_ffn_shared_up_w"]),
        "swd_t": t(g["L0_ffn_shared_down_w"]),
        "c_ident": np.eye(P, dtype=np.float32),
        "c_upper": np.triu(np.ones((P, P), np.float32)),
        "c_cos": np.cos(angle).astype(np.float32),
        "c_sin": np.concatenate([-sin, sin], axis=1),
        "c_reset": (np.arange(NT * E) % E != 0).astype(np.float32),
        "c_tri": np.tril(np.ones((GROUPS, GROUPS), np.float32), -1),
    }
    nc = bacc.Bacc("TRN2", target_bir_lowering=False, num_devices=1)
    in_map, args = {}, []
    for name, a in arrays.items():
        a = np.ascontiguousarray(a)
        in_map[f"in_{name}"] = a
        args.append(nc.dram_tensor(f"in_{name}", a.shape, mybir.dt.from_np(a.dtype), kind="ExternalInput").ap())
    args.append(nc.dram_tensor("out", (SEQS, T, D), mybir.dt.float32, kind="ExternalOutput").ap())
    build(nc, *args)
    return run(nc, [in_map], core_ids=[0]).results[0]["out"]
```
